# Optimizing a Trainium2 kernel written in Bass

```python
import numpy as np
import jax
import jax.numpy as jnp

def _softmax(x, axis=-1):
    return jax.nn.softmax(x, axis=axis)

def _gelu(x):
    return jax.nn.gelu(x, approximate=True)

def _silu(x):
    return jax.nn.silu(x)

def _sigmoid(x):
    return jax.nn.sigmoid(x)

def _layernorm(x, axis=-1, eps=1e-05):
    m = jnp.mean(x, axis=axis, keepdims=True)
    v = jnp.var(x, axis=axis, keepdims=True)
    return (x - m) / jnp.sqrt(v + eps)

def _scatter_add(tgt, idx, src, axis=0):
    return tgt.at[idx].add(src)

def _segment_sum(src, seg, n):
    return jax.ops.segment_sum(src, seg, n)
kernel_name = 'mk_flamingo_gated_d1_seqx_r4_8cd355'

def setup_inputs(seed: int=0):
    np.random.seed(seed)
    _w = jnp.asarray

    def _rec_inputs():
        import jax
        import jax.numpy as jnp
        _rk = jax.random.key(seed)
        x = 7.22e-05 + 1 * jax.random.normal(jax.random.fold_in(_rk, 1), (8, 112, 512), jnp.float32)
        _lenS = 112 - jax.random.randint(jax.random.fold_in(_rk, 7), (8,), 0, max(1, 112 // 4) + 1, jnp.int32)
        _lenS2 = 375 - jax.random.randint(jax.random.fold_in(_rk, 8), (8,), 0, max(1, 375 // 4) + 1, jnp.int32)
        _ctx_2048P = jax.random.normal(jax.random.fold_in(_rk, 11), (8, 16, 512), jnp.float32)
        _ctx_2048c = jax.random.dirichlet(jax.random.fold_in(_rk, 511), 0.3 * jnp.ones((16,), jnp.float32), (8, 375))
        _ctx_2048t = jnp.einsum('bsk,bkd->bsd', _ctx_2048c, _ctx_2048P)
        _ctx_2048t = _ctx_2048t * jax.lax.rsqrt(jnp.mean(jnp.square(_ctx_2048t)) + 1e-12) * 0.953939
        ctx_2048 = -0.000514642 + 1.00011 * (_ctx_2048t + 0.3 * jax.random.normal(jax.random.fold_in(_rk, 611), (8, 375, 512), jnp.float32))
        _g = jax.random.normal(jax.random.fold_in(_rk, 9001), (2, 1), jnp.float32)
        _g = jnp.sign(_g) * jnp.maximum(jnp.abs(_g), 1.0) + (_g == 0) * 1.0
        g_xattn = _g[0]
        g_ffn = _g[1]
        return (x, ctx_2048, g_xattn, g_ffn)
    x, ctx_2048, g_xattn, g_ffn = _rec_inputs()

    def _L0_xattn_setup():
        import jax, jax.numpy as jnp
        import numpy as np
        HIDDEN = 512
        NUM_HEADS = 16
        NUM_KV_HEADS = 4
        HEAD_DIM = 128
        ROPE_THETA = 10000.0
        EPS = 1e-06

        def rms_norm(x, w, eps=EPS):
            var = jnp.mean(jnp.square(x), axis=-1, keepdims=True)
            return x * jax.lax.rsqrt(var + eps) * w

        def rope_cache(L, head_dim, theta, dtype):
            inv_freq = 1.0 / theta ** (jnp.arange(0, head_dim, 2, dtype=jnp.float32) / head_dim)
            t = jnp.arange(L, dtype=jnp.float32)
            freqs = jnp.outer(t, inv_freq)
            emb = jnp.concatenate([freqs, freqs], -1)
            cos = jnp.cos(emb).astype(dtype)[None, :, None, :]
            sin = jnp.sin(emb).astype(dtype)[None, :, None, :]
            return (cos, sin)

        def rotate_half(x):
            x1, x2 = jnp.split(x, 2, axis=-1)
            return jnp.concatenate([-x2, x1], axis=-1)
        key = jax.random.key(seed)
        ks = jax.random.split(key, 10)
        B, L, T = (2, 512, 128)
        q_out = NUM_HEADS * HEAD_DIM
        kv_out = NUM_KV_HEADS * HEAD_DIM
        s = lambda fan_in: 1.0 / np.sqrt(fan_in)
        return {'x': jax.random.normal(ks[0], (B, L, HIDDEN), jnp.float32), 'h_ctx_kv': jax.random.normal(ks[1], (B, T, HIDDEN), jnp.float32), 'wq': jax.random.normal(ks[2], (HIDDEN, q_out), jnp.float32) * s(HIDDEN), 'wk': jax.random.normal(ks[3], (HIDDEN, kv_out), jnp.float32) * s(HIDDEN), 'wv': jax.random.normal(ks[4], (HIDDEN, kv_out), jnp.float32) * s(HIDDEN), 'wo': jax.random.normal(ks[5], (q_out, HIDDEN), jnp.float32) * s(q_out), 'wk_ctx': jax.random.normal(ks[6], (HIDDEN, kv_out), jnp.float32) * s(HIDDEN), 'wv_ctx': jax.random.normal(ks[7], (HIDDEN, kv_out), jnp.float32) * s(HIDDEN), 'q_norm_w': jnp.ones((HEAD_DIM,), jnp.float32), 'k_norm_w': jnp.ones((HEAD_DIM,), jnp.float32)}
    _L0_xattn_all = _L0_xattn_setup()
    _L0_xattn_in = {k: v for k, v in _L0_xattn_all.items() if k in ('wq', 'wk', 'wv', 'wo', 'wk_ctx', 'wv_ctx', 'q_norm_w', 'k_norm_w')}
    del _L0_xattn_all

    def _L0_ffn_setup():
        import jax, jax.numpy as jnp
        import numpy as np
        E = 8
        K = 2
        DIM = 512
        INTER = 352
        N_SHARED = 2
        STD = 0.02
        key = jax.random.key(seed)
        ks = jax.random.split(key, 9)
        B, S = (2, 512)
        return {'x': jax.random.normal(ks[0], (B, S, DIM), dtype=jnp.float32), 'gate_w': jax.random.normal(ks[1], (E, DIM), dtype=jnp.float32) * STD, 'router_bias': jnp.zeros((E,), dtype=jnp.float32), 'W1': jax.random.normal(ks[2], (E, DIM, INTER), dtype=jnp.float32) * STD, 'W3': jax.random.normal(ks[3], (E, DIM, INTER), dtype=jnp.float32) * STD, 'W2': jax.random.normal(ks[4], (E, INTER, DIM), dtype=jnp.float32) * STD, 'sw1': jax.random.normal(ks[5], (N_SHARED * INTER, DIM), dtype=jnp.float32) * STD, 'sw3': jax.random.normal(ks[6], (N_SHARED * INTER, DIM), dtype=jnp.float32) * STD, 'sw2': jax.random.normal(ks[7], (DIM, N_SHARED * INTER), dtype=jnp.float32) * STD}
    _L0_ffn_all = _L0_ffn_setup()
    _L0_ffn_in = {k: v for k, v in _L0_ffn_all.items() if k in ('gate_w', 'router_bias', 'W1', 'W3', 'W2', 'sw1', 'sw3', 'sw2')}
    del _L0_ffn_all
    return {'x': x, 'ctx_2048': ctx_2048, 'g_xattn': g_xattn, 'g_ffn': g_ffn, 'L0_xattn_wq': _L0_xattn_in['wq'], 'L0_xattn_wk': _L0_xattn_in['wk'], 'L0_xattn_wv': _L0_xattn_in['wv'], 'L0_xattn_wo': _L0_xattn_in['wo'], 'L0_xattn_wk_ctx': _L0_xattn_in['wk_ctx'], 'L0_xattn_wv_ctx': _L0_xattn_in['wv_ctx'], 'L0_xattn_q_norm_w': _L0_xattn_in['q_norm_w'], 'L0_xattn_k_norm_w': _L0_xattn_in['k_norm_w'], 'L0_ffn_gate_w': _L0_ffn_in['gate_w'], 'L0_ffn_router_bias': _L0_ffn_in['router_bias'], 'L0_ffn_W1': _L0_ffn_in['W1'], 'L0_ffn_W3': _L0_ffn_in['W3'], 'L0_ffn_W2': _L0_ffn_in['W2'], 'L0_ffn_sw1': _L0_ffn_in['sw1'], 'L0_ffn_sw3': _L0_ffn_in['sw3'], 'L0_ffn_sw2': _L0_ffn_in['sw2']}

def reference(x, ctx_2048, g_xattn, g_ffn, L0_xattn_wq, L0_xattn_wk, L0_xattn_wv, L0_xattn_wo, L0_xattn_wk_ctx, L0_xattn_wv_ctx, L0_xattn_q_norm_w, L0_xattn_k_norm_w, L0_ffn_gate_w, L0_ffn_router_bias, L0_ffn_W1, L0_ffn_W3, L0_ffn_W2, L0_ffn_sw1, L0_ffn_sw3, L0_ffn_sw2):
    import jax
    import jax.numpy as jnp

    def _L0_xattn_ref(x, h_ctx_kv, wq, wk, wv, wo, wk_ctx, wv_ctx, q_norm_w, k_norm_w):
        import jax, jax.numpy as jnp
        import numpy as np
        HIDDEN = 512
        NUM_HEADS = 16
        NUM_KV_HEADS = 4
        HEAD_DIM = 128
        ROPE_THETA = 10000.0
        EPS = 1e-06

        def rms_norm(x, w, eps=EPS):
            var = jnp.mean(jnp.square(x), axis=-1, keepdims=True)
            return x * jax.lax.rsqrt(var + eps) * w

        def rope_cache(L, head_dim, theta, dtype):
            inv_freq = 1.0 / theta ** (jnp.arange(0, head_dim, 2, dtype=jnp.float32) / head_dim)
            t = jnp.arange(L, dtype=jnp.float32)
            freqs = jnp.outer(t, inv_freq)
            emb = jnp.concatenate([freqs, freqs], -1)
            cos = jnp.cos(emb).astype(dtype)[None, :, None, :]
            sin = jnp.sin(emb).astype(dtype)[None, :, None, :]
            return (cos, sin)

        def rotate_half(x):
            x1, x2 = jnp.split(x, 2, axis=-1)
            return jnp.concatenate([-x2, x1], axis=-1)
        B, L, _ = x.shape
        T = h_ctx_kv.shape[1]
        rep = NUM_HEADS // NUM_KV_HEADS
        q = (x @ wq).reshape(B, L, NUM_HEADS, HEAD_DIM)
        k = (x @ wk).reshape(B, L, NUM_KV_HEADS, HEAD_DIM)
        v = (x @ wv).reshape(B, L, NUM_KV_HEADS, HEAD_DIM)
        q = rms_norm(q, q_norm_w)
        k = rms_norm(k, k_norm_w)
        k_ctx = (h_ctx_kv @ wk_ctx).reshape(B, T, NUM_KV_HEADS, HEAD_DIM)
        v_ctx = (h_ctx_kv @ wv_ctx).reshape(B, T, NUM_KV_HEADS, HEAD_DIM)
        k_ctx = rms_norm(k_ctx, k_norm_w)
        cos, sin = rope_cache(L, HEAD_DIM, ROPE_THETA, x.dtype)
        q = q * cos + rotate_half(q) * sin
        k = k * cos + rotate_half(k) * sin
        k_full = jnp.concatenate([k_ctx, k], axis=1)
        v_full = jnp.concatenate([v_ctx, v], axis=1)
        k_full = jnp.repeat(k_full, rep, axis=2)
        v_full = jnpp_repeat = jnp.repeat(v_full, rep, axis=2)
        i = jnp.arange(L)[:, None]
        j = jnp.arange(L)[None, :]
        causal = jnp.where(j > i, -jnp.inf, 0.0).astype(x.dtype)
        mask = jnp.concatenate([jnp.zeros((L, T), x.dtype), causal], axis=1)
        scale = 1.0 / np.sqrt(HEAD_DIM)
        scores = jnp.einsum('blhd,bmhd->bhlm', q, k_full) * scale + mask
        probs = jax.nn.softmax(scores, axis=-1)
        out = jnp.einsum('bhlm,bmhd->blhd', probs, v_full)
        out = out.reshape(B, L, NUM_HEADS * HEAD_DIM)
        return out @ wo

    def _L0_ffn_ref(x, gate_w, router_bias, W1, W3, W2, sw1, sw3, sw2):
        import jax, jax.numpy as jnp
        import numpy as np
        E = 8
        K = 2
        DIM = 512
        INTER = 352
        N_SHARED = 2
        STD = 0.02
        B, S, D = x.shape
        X = x.reshape(-1, D)
        T = X.shape[0]
        logits = jnp.einsum('td,ed->te', X, gate_w)
        scores = jax.nn.sigmoid(logits)
        sel = scores + router_bias[None, :]
        _, idx = jax.lax.top_k(sel, K)
        w = jnp.take_along_axis(scores, idx, axis=1)
        w = w / jnp.clip(jnp.sum(w, axis=-1, keepdims=True), 1e-12)
        gate_full = jnp.zeros((T, E), dtype=w.dtype).at[jnp.arange(T)[:, None], idx].set(w)
        h1 = jnp.einsum('td,edh->eth', X, W1)
        h3 = jnp.einsum('td,edh->eth', X, W3)
        y = jnp.einsum('eth,ehd->etd', jax.nn.silu(h1) * h3, W2)
        out = jnp.einsum('etd,te->td', y, gate_full)
        shared = jnp.einsum('th,dh->td', jax.nn.silu(jnp.einsum('td,hd->th', X, sw1)) * jnp.einsum('td,hd->th', X, sw3), sw2)
        out = out + shared
        return out.reshape(B, S, D)
    x = x + jnp.tanh(g_xattn[0]) * _L0_xattn_ref(_layernorm(x, axis=-1), ctx_2048, L0_xattn_wq, L0_xattn_wk, L0_xattn_wv, L0_xattn_wo, L0_xattn_wk_ctx, L0_xattn_wv_ctx, L0_xattn_q_norm_w, L0_xattn_k_norm_w)
    x = x + jnp.tanh(g_ffn[0]) * _L0_ffn_ref(_layernorm(x, axis=-1), L0_ffn_gate_w, L0_ffn_router_bias, L0_ffn_W1, L0_ffn_W3, L0_ffn_W2, L0_ffn_sw1, L0_ffn_sw3, L0_ffn_sw2)
    return x

_drawn_inputs = setup_inputs


def setup_inputs(seed=0):
    import zlib

    import numpy as np

    out = dict(_drawn_inputs(seed))
    spreads = {'L0_xattn_q_norm_w': (1.0, 0.599),
     'L0_xattn_k_norm_w': (1.0, 0.6),
     'L0_ffn_router_bias': (0.0, 2.0)}
    factors = {'L0_ffn_gate_w': 22.757}
    for name, (base, spread) in spreads.items():
        noise = np.random.default_rng([zlib.crc32(name.encode()), seed]).standard_normal(out[name].shape)
        drawn = base * np.exp(spread * noise) if base else spread * noise
        out[name] = jnp.asarray(drawn.astype(out[name].dtype))
    for name, factor in factors.items():
        out[name] = (out[name] * factor).astype(out[name].dtype)
    return out
```

```python
from contextlib import ExitStack

import numpy as np

import concourse.bass as bass
from concourse import mybir

F32 = mybir.dt.float32
F32R = mybir.dt.float32r
ALU = mybir.AluOpType
ACT = mybir.ActivationFunctionType
AX = mybir.AxisListType

B, L, DM = 8, 112, 512
T = 375
NH, NKV, HD = 16, 4, 128
REP = NH // NKV
KT = DM // 128
CR = 125
NCT = T // CR
NKT = NCT + 1
NKEY = T + L
NSC = NKEY + NKEY % 2
MO = T - T % 2
MW = NSC - MO
NPAD = NKT * CR
QW, KW = NH * HD, NKV * HD
GW = REP * L
NQ = QW // 512
E, INTER, TOPK = 8, 352, 2
GH = 2 * INTER
NG = E // 2 + 1
NFT = GH // 128
TAIL = GH - NFT * 128
NT = B * L
HALF = NT // 2
EPS_LN, EPS_RMS = 1e-5, 1e-6
THETA = 10000.0
MASKED = -1e30


def constants():
    inv = 1.0 / THETA ** (np.arange(0, HD, 2, dtype=np.float32) / np.float32(HD))
    freqs = np.outer(np.arange(L, dtype=np.float32), inv.astype(np.float32)).astype(np.float32)
    emb = np.concatenate([freqs, freqs], -1)
    cos, sin = np.cos(emb).astype(np.float32), np.sin(emb).astype(np.float32)
    sin[:, :HD // 2] *= -1.0
    mask = np.zeros((L, MW), np.float32)
    mask[:, T - MO:T - MO + L] = np.where(np.arange(L)[None, :] > np.arange(L)[:, None], MASKED, 0.0)
    sel = np.zeros((4, NFT + 1, 128), np.float32)
    for j in range(NFT + 1):
        for c in range(128):
            h = j * 128 + c if j < NFT else NFT * 128 + c - (128 - TAIL)
            if NFT * 128 <= h < GH or (j < NFT):
                sel[h // INTER, j, c] = sel[2 + h // INTER, j, c] = 1.0
    one = np.zeros((4, NT), np.float32)
    one[0:2] = 1.0
    return {
        "c_ident": np.eye(128, dtype=np.float32),
        "c_cos": np.ascontiguousarray(np.tile(cos, (1, 4))),
        "c_sin": np.ascontiguousarray(np.tile(sin, (1, 4))),
        "c_mask": mask,
        "c_sel": np.ascontiguousarray(sel.reshape(4, -1)),
        "c_one": one,
        "c_rev": np.ascontiguousarray(np.broadcast_to(np.arange(E, 0, -1, dtype=np.float32), (L, B, E))),
    }


def at(b, n):
    return bass.ds(b * n, n)


def over_batches(eng, body):
    body(0, 0, 0)
    with eng.Fori(0, (B - 2) // 2) as i:
        body(i * 2 + 1, 1, i)
        body(i * 2 + 2, 0, i + 1)
    body(B - 1, 1, (B - 2) // 2)


def f32(ap):
    return ap.bitcast(F32)


def build(nc, io, out):
    with ExitStack() as ctx:
        def dram(name, shape):
            return nc.dram_tensor(name, shape, F32).ap()

        def const_sb(name, shape, dt=F32):
            return ctx.enter_context(nc.sbuf_tensor(name, shape, dt))

        scratch = {
            "q": dram("q_roped", (B, L, QW)),
            "k": dram("k_roped", (B, L, KW)),
            "v": dram("v_self", (B, L, KW)),
            "o": dram("attn_t", (B, 128, NH * L)),
        }
        banks = [ctx.enter_context(nc.psum_tensor(f"bank{i}", [128, 512], F32)) for i in range(8)]
        c = {
            "ident": const_sb("ident", [128, 128]),
            "identr": const_sb("identr", [128, 128], F32R),
            "neghalf": const_sb("neghalf", [128, 16]),
            "gates": const_sb("gates", [128, 2]),
            "tanhg": const_sb("tanhg", [128, 2]),
            "rq": const_sb("rq", [L, B * NH]),
            "wkn": const_sb("wkn", [128, HD]),
        }
        with ExitStack() as attn:
            wch = attn.enter_context(nc.sbuf_tensor("wctx_hi", [128, KT, 2, KW], F32R))
            wcl = attn.enter_context(nc.sbuf_tensor("wctx_lo", [128, KT, 2, KW], F32R))
            self_projections(nc, io, scratch, banks, c, wch, wcl)
            attention(nc, io, scratch, banks, c, wch, wcl)
        x1 = const_sb("x1", [L, B, DM])
        x2h = const_sb("x2t_hi", [128, KT, NT], F32R)
        x2l = const_sb("x2t_lo", [128, KT, NT], F32R)
        out_projection(nc, io, scratch, banks, c, x1, x2h, x2l)
        experts(nc, io, out, banks, c, x1, x2h, x2l)


def mm3(nc, out, wh, wl, xh, xl, start, stop):
    nc.tensor.matmul(out, wh, xh, start=start, stop=False)
    nc.tensor.matmul(out, wh, xl, start=False, stop=False)
    return nc.tensor.matmul(out, wl, xh, start=False, stop=stop)


def self_projections(nc, io, scratch, banks, c, wch, wcl):
    NCH = NQ + 2
    with ExitStack() as ctx:
        def sb(name, shape, dt=F32):
            return ctx.enter_context(nc.sbuf_tensor(name, shape, dt))

        def sem(name):
            return ctx.enter_context(nc.semaphore(name))

        waited = sem("waited")

        wh = sb("w_hi", [128, KT, NCH * 512], F32R)
        wl = sb("w_lo", [128, KT, NCH * 512], F32R)
        wraw = [sb(f"wraw{i}", [128, KT, 512]) for i in range(2)]
        x = [sb(f"x_p1_{i}", [L, DM]) for i in range(2)]
        st, mv = sb("ln_stats", [L, 6]), sb("ln_mv", [L, 2])
        ve, rstd = sb("ln_ve", [L, 1]), sb("ln_rstd", [L, 1])
        xn = sb("xn", [L, DM])
        xh = [sb(f"xt_hi{i}", [128, KT, L], F32R) for i in range(2)]
        xl = [sb(f"xt_lo{i}", [128, KT, L], F32R) for i in range(2)]
        cos, sin = sb("cos", [L, 4, HD]), sb("sin", [L, 4, HD])
        wn = [sb(f"wn{i}", [L, 4, HD]) for i in range(2)]
        tc = [sb(f"cosw{i}", [L, 4, HD]) for i in range(2)]
        ts = [sb(f"sinw{i}", [L, 4, HD]) for i in range(2)]
        sq = [sb(f"sq{i}", [L, 4, HD]) for i in range(2)]
        ra = [sb(f"rope_a{i}", [L, 4, HD]) for i in range(2)]
        rb = [sb(f"rope_b{i}", [L, 4, HD]) for i in range(2)]
        qo = [sb(f"q_out{i}", [L, 4, HD]) for i in range(2)]
        ko, vo = sb("k_out", [L, 4, HD]), sb("v_out", [L, 4, HD])
        ssq = sb("ssq", [L, NH + NKV])
        ssk, rk = sb("ssk", [L, NKV]), sb("rk", [L, NKV])
        ssr = sb("ssr", [L, NH])

        consts_in, ident_in = sem("consts_in"), sem("ident_in")
        x_in = [sem(f"x_in{i}") for i in range(2)]
        w_in = [sem(f"w_in{i}") for i in range(2)]
        whi, wlo, neg_set, idr = sem("whi"), sem("wlo"), sem("neg_set"), sem("idr")
        tabs, tabs_chain = sem("tables"), sem("tables_chain")
        ln_st, ln_mv, ln_ve, ln_r, ln_x = sem("ln_st"), sem("ln_mvs"), sem("ln_ves"), sem("ln_rs"), sem("ln_x")
        t_done, th, tl = sem("xt_psum"), sem("xt_his"), sem("xt_los")
        proj, squared, summed, mul_a, mul_b = sem("proj"), sem("squared"), sem("summed"), sem("mul_a"), sem("mul_b")
        q_sum, q_out = sem("q_sum"), [sem(f"q_stored{i}") for i in range(2)]
        k_sum, k_ss, k_r, k_fin, k_out = sem("k_sum"), sem("k_ss"), sem("k_r"), sem("k_fin"), sem("k_stored")
        v_fin, v_out = sem("v_fin"), sem("v_stored")
        q_ss, q_r, tanh_s = sem("q_ss"), sem("q_r"), sem("tanh_s")
        tbank, cbank = banks[0], [banks[1 + i] for i in range(NCH)]
        srcs = [io["wqkv"][:, :, n * 512:(n + 1) * 512] for n in range(NCH)]
        srcs += [io["wctx"][:, :, n * KW:(n + 1) * KW] for n in range(2)]

        def wdst(n, hi):
            if n < NCH:
                return (wh if hi else wl)[:, :, n * 512:(n + 1) * 512]
            return (wch if hi else wcl)[:, :, n - NCH, :]

        with nc.Block() as block:
            @block.sync
            def _(sp):
                for i in range(2):
                    sp.dma_start(x[i][:], io["x"][i]).then_inc(x_in[i], 16)
                sp.dma_start(c["ident"][:], io["c_ident"]).then_inc(ident_in, 16)
                for n in range(len(srcs)):
                    if n >= 2:
                        sp.wait_ge(wlo, n - 1)
                    sp.dma_start(wraw[n % 2][:], srcs[n]).then_inc(w_in[n % 2], 16)
                    if n == 0:
                        sp.dma_start(cos[:], io["c_cos"].rearrange("l (a d) -> l a d", a=4)).then_inc(consts_in, 16)
                        sp.dma_start(sin[:], io["c_sin"].rearrange("l (a d) -> l a d", a=4)).then_inc(consts_in, 16)
                        for i, name in enumerate(("qn", "kn")):
                            for a in range(4):
                                sp.dma_start(wn[i][:, a, :], io[name].partition_broadcast(L)).then_inc(consts_in, 16)
                        sp.dma_start(c["wkn"][:], io["kn"].partition_broadcast(128)).then_inc(consts_in, 16)
                        for i, name in enumerate(("g_xattn", "g_ffn")):
                            sp.dma_start(c["gates"][:, i:i + 1], io[name].partition_broadcast(128)).then_inc(consts_in, 16)

                def batch(b, par, k):
                    if not (isinstance(b, int) and (b == 0 or b == B - 1)):
                        sp.wait_ge(ln_x, b)
                        sp.dma_start(x[1 - par][:], io["x"][at(b + 1, 1), :, :].rearrange("a l d -> (a l) d")).then_inc(x_in[1 - par], 16)
                    for n in range(NQ):
                        sp.wait_ge(q_sum, b * NQ + n + 1)
                        sp.dma_start(scratch["q"][at(b, 1), :, n * 512:(n + 1) * 512].rearrange("a l d -> (a l) d"),
                                     qo[n % 2][:].rearrange("l a d -> l (a d)")).then_inc(q_out[n % 2], 16)
                    sp.wait_ge(k_fin, b * NKV + NKV)
                    sp.dma_start(scratch["k"][at(b, 1), :, :].rearrange("a l d -> (a l) d"),
                                 ko[:].rearrange("l a d -> l (a d)")).then_inc(k_out, 16)
                    sp.wait_ge(v_fin, b + 1)
                    sp.dma_start(scratch["v"][at(b, 1), :, :].rearrange("a l d -> (a l) d"),
                                 vo[:].rearrange("l a d -> l (a d)")).then_inc(v_out, 16)

                over_batches(sp, batch)
                for i in range(2):
                    sp.wait_ge(q_out[i], 16 * B * NQ // 2)
                sp.wait_ge(k_out, 16 * B)
                sp.wait_ge(v_out, 16 * B)

            @block.gpsimd
            def _(pool):
                nc.gpsimd.memset(c["neghalf"][:], -0.5).then_inc(neg_set, 1)
                pool.wait_ge(neg_set, 1)

                def norm(b):
                    pool.wait_ge(ln_mv, b + 1)
                    pool.sem_inc(waited, 1)
                    nc.gpsimd.tensor_scalar(ve[:], mv[:, 1:2], 1.0, EPS_LN, ALU.mult, ALU.add).then_inc(ln_ve, 1)
                    pool.wait_ge(ln_ve, b + 1)
                    nc.gpsimd.tensor_tensor(rstd[:], ve[:], c["neghalf"][0:L, 0:1], ALU.pow).then_inc(ln_r, 1)

                norm(0)

                def batch(b, par, k):
                    if not (isinstance(b, int) and b == B - 1):
                        norm(b + 1)
                    for n in range(NQ):
                        pool.wait_ge(mul_b, b * (2 * NQ + 2) + 2 * n + 2)
                        if not (isinstance(b, int) and b == 0 and n < 2):
                            pool.wait_ge(q_out[n % 2], b * (8 * NQ) + 16 * (n // 2))
                        nc.gpsimd.tensor_tensor(qo[n % 2][:], ra[n % 2][:], rb[n % 2][:], ALU.add).then_inc(q_sum, 1)
                    pool.wait_ge(mul_b, (b + 1) * (2 * NQ + 2))
                    pool.wait_ge(summed, (b + 1) * (NQ + 1))
                    if not (isinstance(b, int) and b == 0):
                        pool.wait_ge(k_out, b * 16)
                    nc.gpsimd.tensor_tensor(ko[:], ra[NQ % 2][:], rb[NQ % 2][:], ALU.add).then_inc(k_sum, 1)
                    pool.sem_inc(waited, 1)
                    nc.gpsimd.tensor_scalar(ssk[:], ssq[:, NH:], 1.0 / HD, EPS_RMS, ALU.mult, ALU.add).then_inc(k_ss, 1)
                    pool.wait_ge(k_ss, b + 1)
                    nc.gpsimd.tensor_tensor(rk[:], ssk[:], c["neghalf"][0:L, 0:NKV], ALU.pow).then_inc(k_r, 1)
                    pool.wait_ge(k_r, b + 1)
                    pool.wait_ge(k_sum, b + 1)
                    for h in range(NKV):
                        pool.sem_inc(waited, 1)
                        nc.gpsimd.tensor_scalar(ko[:, h, :], ko[:, h, :], rk[:, h:h + 1], 1.0, ALU.mult, ALU.mult).then_inc(k_fin, 1)
                    pool.sem_inc(waited, 1)
                    nc.gpsimd.tensor_scalar(ssr[:], ssq[:, 0:NH], 1.0, HD * EPS_RMS, ALU.mult, ALU.add).then_inc(q_ss, 1)
                    pool.wait_ge(q_ss, b + 1)
                    nc.gpsimd.tensor_tensor(c["rq"][:, at(b, NH)], ssr[:], c["neghalf"][0:L, 0:NH], ALU.pow).then_inc(q_r, 1)

                over_batches(pool, batch)

            @block.scalar
            def _(act):
                def weight(n):
                    act.wait_ge(w_in[n % 2], 16 * (n // 2 + 1))
                    nc.scalar.activation(wdst(n, True), wraw[n % 2][:], ACT.Copy).then_inc(whi, 1)

                act.wait_ge(ident_in, 16)
                nc.scalar.activation(c["identr"][:], c["ident"][:], ACT.Copy).then_inc(idr, 1)

                def xt(b, par):
                    act.wait_ge(t_done, b + 1)
                    if not (isinstance(b, int) and b < 2):
                        act.wait_ge(proj, (b - 1) * NCH)
                    nc.scalar.activation(xh[par][:], tbank[:, 0:KT * L].rearrange("p (k l) -> p k l", k=KT), ACT.Copy).then_inc(th, 1)

                xt(0, 0)
                for n in range(2):
                    weight(n)

                def batch(b, par, k):
                    first = isinstance(b, int) and b == 0
                    if not (isinstance(b, int) and b == B - 1):
                        xt(b + 1, 1 - par)
                    for n in range(NCH):
                        if first and n + 2 < len(srcs):
                            weight(n + 2)
                        act.wait_ge(proj, b * NCH + n + 1)
                        src = cbank[n][0:L, :].rearrange("l (a d) -> l a d", a=4)
                        if n <= NQ:
                            if not (first and n < 2):
                                act.wait_ge(summed, b * (NQ + 1) + max(n - 1, 0))
                            nc.scalar.activation(sq[n % 2][:], src, ACT.Square).then_inc(squared, 1)
                        else:
                            if not first:
                                act.wait_ge(v_out, b * 16)
                            nc.scalar.activation(vo[:], src, ACT.Copy).then_inc(v_fin, 1)

                over_batches(act, batch)
                act.wait_ge(consts_in, 13 * 16)
                nc.scalar.activation(c["tanhg"][:], c["gates"][:], ACT.Tanh).then_inc(tanh_s, 1)

            @block.vector
            def _(dve):
                def norm(b, par, k):
                    dve.wait_ge(x_in[par], k * 16 + 16)
                    dve.sem_inc(waited, 1)
                    nc.vector.bn_stats(st[:], x[par][:]).then_inc(ln_st, 1)
                    dve.wait_ge(ln_st, b + 1)
                    dve.sem_inc(waited, 1)
                    nc.vector.bn_aggr(mv[:], st[:]).then_inc(ln_mv, 1)
                    dve.wait_ge(ln_r, b + 1)
                    dve.wait_ge(ln_mv, b + 1)
                    if not (isinstance(b, int) and b == 0):
                        dve.wait_ge(t_done, b)
                    nc.vector.tensor_scalar(xn[:], x[par][:],
                                            mv[:, 0:1], rstd[:], ALU.subtract, ALU.mult).then_inc(ln_x, 1)

                def xt(b, par):
                    dve.wait_ge(th, b + 1)
                    if not (isinstance(b, int) and b < 2):
                        dve.wait_ge(proj, (b - 1) * NCH)
                    nc.vector.tensor_tensor(xl[par][:], tbank[:, 0:KT * L].rearrange("p (k l) -> p k l", k=KT),
                                            f32(xh[par][:]), ALU.subtract).then_inc(tl, 1)

                def weight(n):
                    dve.wait_ge(whi, n + 1)
                    nc.vector.tensor_tensor(wdst(n, False), wraw[n % 2][:], f32(wdst(n, True)), ALU.subtract).then_inc(wlo, 1)

                norm(0, 0, 0)
                xt(0, 0)
                for n in range(2):
                    weight(n)
                dve.wait_ge(consts_in, 13 * 16)
                half = HD // 2
                for i in range(2):
                    nc.vector.tensor_tensor(tc[i][:], wn[i][:], cos[:], ALU.mult).then_inc(tabs, 1)
                    nc.vector.tensor_tensor(ts[i][:, :, 0:half], wn[i][:, :, half:], sin[:, :, 0:half], ALU.mult).then_inc(tabs, 1)
                    nc.vector.tensor_tensor(ts[i][:, :, half:], wn[i][:, :, 0:half], sin[:, :, half:], ALU.mult).then_inc(tabs, 1)
                dve.wait_ge(tabs, 6)

                def batch(b, par, k):
                    first = isinstance(b, int) and b == 0
                    if not (isinstance(b, int) and b == B - 1):
                        norm(b + 1, 1 - par, k + par)
                        xt(b + 1, 1 - par)
                    for n in range(NQ + 1):
                        if first and n + 2 < len(srcs):
                            weight(n + 2)
                        i = 0 if n < NQ else 1
                        src = cbank[n][0:L, :].rearrange("l (a d) -> l a d", a=4)
                        dve.wait_ge(squared, b * (NQ + 1) + n + 1)
                        if n >= 2:
                            dve.wait_ge(q_sum, b * NQ + n - 1)
                        elif not first:
                            dve.wait_ge(*((k_sum, b) if n == 0 else (q_sum, b * NQ)))
                        nc.vector.tensor_tensor(ra[n % 2][:], src, tc[i][:], ALU.mult).then_inc(mul_a, 1)
                        nc.vector.tensor_tensor(rb[n % 2][:, :, 0:half], src[:, :, half:], ts[i][:, :, 0:half], ALU.mult).then_inc(mul_b, 1)
                        nc.vector.tensor_tensor(rb[n % 2][:, :, half:], src[:, :, 0:half], ts[i][:, :, half:], ALU.mult).then_inc(mul_b, 1)
                        if n == 0 and not first:
                            dve.wait_ge(q_ss, b)
                        nc.vector.tensor_reduce(ssq[:, 4 * n:4 * n + 4], sq[n % 2][:], AX.X, ALU.add).then_inc(summed, 1)
                    if first:
                        weight(NCH + 1)

                over_batches(dve, batch)

            @block.tensor
            def _(pe):
                def xt(b):
                    pe.wait_ge(ln_x, b + 1)
                    if not (isinstance(b, int) and b == 0):
                        pe.wait_ge(tl, b)
                    for kt in range(KT):
                        mm = nc.tensor.transpose(tbank[:, kt * L:(kt + 1) * L], xn[:, kt * 128:(kt + 1) * 128], c["ident"][0:L, 0:L])
                    mm.then_inc(t_done, 1)

                pe.wait_ge(ident_in, 16)
                xt(0)

                def batch(b, par, k):
                    first = isinstance(b, int) and b == 0
                    if not (isinstance(b, int) and b == B - 1):
                        xt(b + 1)
                    pe.wait_ge(tl, b + 1)
                    for n in range(NCH):
                        if first:
                            pe.wait_ge(wlo, n + 1)
                        elif n <= NQ:
                            pe.wait_ge(summed, (b - 1) * (NQ + 1) + n + 1)
                        else:
                            pe.wait_ge(v_fin, b)
                        for kt in range(KT):
                            mm = mm3(nc, cbank[n][0:L, :], xh[par][:, kt, :], xl[par][:, kt, :],
                                     wh[:, kt, n * 512:(n + 1) * 512], wl[:, kt, n * 512:(n + 1) * 512],
                                     kt == 0, kt == KT - 1)
                        mm.then_inc(proj, 1)

                over_batches(pe, batch)


def attention(nc, io, scratch, banks, c, wch, wcl):
    with ExitStack() as ctx:
        def sb(name, shape, dt=F32):
            return ctx.enter_context(nc.sbuf_tensor(name, shape, dt))

        def sem(name):
            return ctx.enter_context(nc.semaphore(name))

        waited = sem("waited")

        def pair(name, shape, n=1):
            return [(sb(f"{name}_hi{i}", shape, F32R), sb(f"{name}_lo{i}", shape, F32R)) for i in range(n)]

        maskraw = sb("mask_raw", [L, MW])
        mask = sb("mask", [L, MW], F32R)
        craw = sb("ctx_raw", [128, KT, T])
        ct = pair("ctx_t", [128, KT, CR], 2)
        ktok = sb("k_tok", [CR, NKT, NKV, HD])
        vraw = sb("v_raw", [L, KW])
        sq = sb("csq", [CR, NKV, HD])
        css, csr, crk = sb("css", [CR, NCT, NKV]), sb("csr", [CR, NKV]), sb("crk", [CR, NCT, NKV])
        kT = pair("k_t", [128, NKV, NSC], 2)
        V = pair("v_tok", [CR, NKT, KW], 2)
        q = [sb(f"q_tok{i}", [L, QW]) for i in range(2)]
        qT = pair("q_t", [128, GW], 2)
        Pm = [sb(f"probs{i}", [L, NPAD]) for i in range(2 * REP)]
        pT = pair("p_t", [CR, NKT, GW])[0]
        oT = [sb(f"o_t{i}", [128, GW]) for i in range(2)]
        mx, nb = sb("row_max", [L, NH]), sb("neg_bias", [L, NH])
        rs, ri = sb("row_sum", [L, NH]), sb("row_inv", [L, NH])

        mask_in, mask_set, pads = sem("mask_in"), sem("mask_set"), sem("pads")
        ctx_in, kself_in, vself_in = sem("ctx_in"), sem("kself_in"), sem("vself_in")
        q_in = [sem(f"q_in{i}") for i in range(2)]
        cthi, ctlo = sem("ctx_his"), sem("ctx_los")
        kproj, vproj, csqd, csum, cadd, cpow, kscaled = (sem(n) for n in (
            "kproj", "vproj", "csquared", "csummed", "cadded", "cpowered", "kscaled"))
        vhi, vlo, vshi, vslo = sem("v_his"), sem("v_los"), sem("vself_his"), sem("vself_los")
        ktr, kthi, ktlo = sem("k_transposed"), sem("k_his"), sem("k_los")
        qtr, qthi, qtlo = sem("q_transposed"), sem("q_his"), sem("q_los")
        scored, maxed, biased, exped, inverted, normed = (sem(n) for n in (
            "scored", "maxed", "biased", "exped", "inverted", "normed"))
        ptr, pthi, ptlo, pv, oev = sem("p_transposed"), sem("p_his"), sem("p_los"), sem("pv_done"), sem("o_read")
        o_out = [sem(f"o_stored{i}") for i in range(2)]
        sbank, pbank, qbank, mbank, obank = banks[0:2], banks[2:4], banks[4], banks[5:7], banks[7]

        order = [("k", 0), ("k", 1), ("t", 0), ("v", 0), ("v", 1), ("t", 1), ("k", 2), ("v", 2), ("t", NCT), ("t", 2)]
        splits = {("k", 0): 1, ("v", 1): 2}
        NM = len(order)
        assert NM % 2 == 0
        SPLIT = -1
        slots = {s: [s - 1] for s in range(NM + 1)}

        T_ORDER = [t for kind, t in order if kind == "t"]

        def schedule(eng, prologue, step, filler, last):
            prologue()
            for use in range(SPLIT, NM):
                filler(0, 0, 0, use)

            def batch(b, par, k):
                final = isinstance(b, int) and b == B - 1
                for g in range(NKV):
                    for h in range(REP):
                        step(b, par, k, g, h)
                        if not final:
                            for use in slots.get(g * REP + h, []):
                                filler(b + 1, 1 - par, k + par, use)
                    last(b, par, k, g)

            over_batches(eng, batch)

        with nc.Block() as block:
            @block.sync
            def _(sp):
                sp.dma_start(maskraw[:], io["c_mask"]).then_inc(mask_in, 16)

                def load_ctx(b):
                    if not (isinstance(b, int) and b == 0):
                        sp.wait_ge(ctlo, b * NCT)
                    sp.dma_start(craw[:], io["ctxt"][at(b, 1), :, :, :].rearrange("a p k t -> (a p) k t")).then_inc(ctx_in, 16)

                def load(b, par, k):
                    if not (isinstance(b, int) and b < 2):
                        sp.wait_ge(qtr, (b - 1) * NKV)
                    sp.dma_start(q[par][:], scratch["q"][at(b, 1), :, :].rearrange("a l d -> (a l) d")).then_inc(q_in[par], 16)
                    if not (isinstance(b, int) and b == 0):
                        sp.wait_ge(ktr, b * NKT)
                    sp.dma_start(ktok[0:L, NCT, :, :], scratch["k"][at(b, 1), :, :].rearrange("a l (h d) -> (a l) h d", h=NKV)).then_inc(kself_in, 16)
                    if not (isinstance(b, int) and b == 0):
                        sp.wait_ge(vslo, b)
                    sp.dma_start(vraw[:], scratch["v"][at(b, 1), :, :].rearrange("a l d -> (a l) d")).then_inc(vself_in, 16)

                for b in range(2):
                    load_ctx(b)
                    load(b, b, 0)

                def batch(b, par, k):
                    def store(b, k, g):
                        sp.wait_ge(oev, b * NKV + g + 1)
                        sp.dma_start(scratch["o"][at(b, 1), :, g * GW:(g + 1) * GW].rearrange("a p n -> (a p) n"),
                                     oT[g % 2][:]).then_inc(o_out[g % 2], 16)
                    for g in range(NKV):
                        store(b, k, g)
                        if not (isinstance(b, int) and b >= B - 2):
                            if g == 0:
                                load_ctx(b + 2)
                            if g == 1:
                                load(b + 2, par, k + 1)

                batch(0, 0, 0)
                with sp.Fori(0, (B - 4) // 2) as i:
                    batch(i * 2 + 1, 1, i)
                    batch(i * 2 + 2, 0, i + 1)
                batch(B - 3, 1, (B - 4) // 2)
                batch(B - 2, 0, (B - 2) // 2)
                batch(B - 1, 1, (B - 2) // 2)
                for i in range(2):
                    sp.wait_ge(o_out[i], 16 * B * NKV // 2)

            @block.gpsimd
            def _(pool):
                def prologue():
                    for i in range(2 * REP):
                        nc.gpsimd.memset(Pm[i][:, NKEY:], 0.0).then_inc(pads, 1)
                    for i in range(2):
                        for m in kT[i]:
                            nc.gpsimd.memset(f32(m[:, :, NKEY:]), 0.0).then_inc(pads, 1)
                    pool.wait_ge(pads, 2 * REP + 8)

                def filler(b, par, k, use):
                    if use == SPLIT:
                        return
                    kind, t = order[use]
                    if kind == "k":
                        pool.wait_ge(csum, b * NCT + t + 1)
                        if not (isinstance(b, int) and b == 0 and t == 0):
                            pool.wait_ge(cpow, b * NCT + t)
                        pool.sem_inc(waited, 1)
                        nc.gpsimd.tensor_scalar(csr[:], css[:, t, :], 1.0 / HD, EPS_RMS, ALU.mult, ALU.add).then_inc(cadd, 1)
                        pool.wait_ge(cadd, b * NCT + t + 1)
                        nc.gpsimd.tensor_tensor(crk[:, t, :], csr[:], c["neghalf"][0:CR, 0:NKV], ALU.pow).then_inc(cpow, 1)
                    if kind == "v" and t == 0:
                        pool.wait_ge(vself_in, b * 16 + 16)
                        if not (isinstance(b, int) and b < 2):
                            pool.wait_ge(pv, (b - 1) * NKV)
                        pool.sem_inc(waited, 1)
                        nc.gpsimd.tensor_copy(V[par][0][0:L, NCT, :], vraw[:]).then_inc(vshi, 1)
                        pool.wait_ge(vshi, b + 1)
                        nc.gpsimd.tensor_tensor(V[par][1][0:L, NCT, :], vraw[:], f32(V[par][0][0:L, NCT, :]), ALU.subtract).then_inc(vslo, 1)

                def norm(b, g, h):
                    pool.wait_ge(inverted, b * NH + g * REP + h + 1)
                    p = Pm[(g % 2) * REP + h]
                    col = g * REP + h
                    pool.sem_inc(waited, 1)
                    nc.gpsimd.tensor_scalar(p[:, 0:NKEY], p[:, 0:NKEY], ri[:, col:col + 1], 1.0, ALU.mult, ALU.mult).then_inc(normed, 1)

                def step(b, par, k, g, h):
                    if h:
                        norm(b, g, h - 1)

                def last(b, par, k, g):
                    norm(b, g, REP - 1)

                schedule(pool, prologue, step, filler, last)

            @block.scalar
            def _(act):
                def prologue():
                    act.wait_ge(mask_in, 16)
                    nc.scalar.activation(mask[:], maskraw[:], ACT.Copy).then_inc(mask_set, 1)

                def filler(b, par, k, use):
                    if use == SPLIT:
                        ctx_hi(b, par, 0)
                        return
                    kind, t = order[use]
                    bank = mbank[use % 2]
                    if (kind, t) in splits:
                        ctx_hi(b, par, splits[kind, t])
                    if kind == "k":
                        act.wait_ge(kproj, b * NCT + t + 1)
                        if not (isinstance(b, int) and b == 0 and t == 0):
                            act.wait_ge(csum, b * NCT + t)
                        nc.scalar.activation(sq[:], bank[0:CR, :].rearrange("r (h d) -> r h d", h=NKV), ACT.Square).then_inc(csqd, 1)
                    elif kind == "v":
                        act.wait_ge(vproj, b * NCT + t + 1)
                        if not (isinstance(b, int) and b < 2):
                            act.wait_ge(pv, (b - 1) * NKV)
                        nc.scalar.activation(V[par][0][:, t, :], bank[0:CR, :], ACT.Copy).then_inc(vhi, 1)
                    else:
                        n = L if t == NCT else CR
                        act.wait_ge(ktr, b * NKT + T_ORDER.index(t) + 1)
                        if not (isinstance(b, int) and b < 2):
                            act.wait_ge(scored, (b - 1) * NH)
                        nc.scalar.activation(kT[par][0][:, :, t * CR:t * CR + n],
                                             bank[:, 0:NKV * CR].rearrange("p (h r) -> p h r", h=NKV)[:, :, 0:n], ACT.Copy).then_inc(kthi, 1)

                def ctx_hi(b, par, t):
                    act.wait_ge(ctx_in, b * 16 + 16)
                    if not (isinstance(b, int) and b == 0 and t < 2):
                        act.wait_ge(vproj, b * NCT + t - 1)
                    nc.scalar.activation(ct[(par * NCT + t) % 2][0][:], craw[:, :, t * CR:(t + 1) * CR], ACT.Copy).then_inc(cthi, 1)

                def q_hi(b, g):
                    act.wait_ge(qtr, b * NKV + g + 1)
                    if not (isinstance(b, int) and b == 0 and g < 2):
                        act.wait_ge(scored, (b * NKV + g - 1) * REP)
                    nc.scalar.activation(qT[g % 2][0][:], qbank[:, 0:GW], ACT.Copy).then_inc(qthi, 1)

                def p_hi(b, g, h):
                    n = b * NH + g * REP + h
                    act.wait_ge(ptr, n + 1)
                    if h == 0 and not (isinstance(b, int) and b == 0 and g == 0):
                        act.wait_ge(pv, b * NKV + g)
                    nc.scalar.activation(pT[0][:, :, h * L:(h + 1) * L],
                                         pbank[h % 2][0:CR, 0:NKT * L].rearrange("r (t l) -> r t l", t=NKT), ACT.Copy).then_inc(pthi, 1)

                def prev(b, g):
                    return (b, g - 1) if g else (b - 1, NKV - 1)

                def step(b, par, k, g, h):
                    if not (isinstance(b, int) and b == 0 and g == 0):
                        p_hi(*prev(b, g), h)
                    n = b * NH + g * REP + h
                    p = Pm[(g % 2) * REP + h]
                    col = g * REP + h
                    act.wait_ge(biased, n + 1)
                    if not (isinstance(b, int) and b == 0 and g < 2):
                        act.wait_ge(ptr, n + 1 - 2 * REP)
                    if not (isinstance(b, int) and b == 0):
                        act.wait_ge(inverted, n + 1 - NH)
                    nc.scalar.activation(p[:, 0:NKEY], sbank[h % 2][0:L, 0:NKEY], ACT.Exp, bias=nb[:, col:col + 1],
                                         scale=c["rq"][:, bass.ds(n, 1)],
                                         accum_out=rs[:, col:col + 1]).then_inc(exped, 1)

                def last(b, par, k, g):
                    if g < NKV - 1:
                        q_hi(b, g + 1)
                    elif not (isinstance(b, int) and b == B - 1):
                        q_hi(b + 1, 0)

                def start():
                    prologue()
                    q_hi(0, 0)

                schedule(act, start, step, filler, last)
                for h in range(REP):
                    p_hi(B - 1, NKV - 1, h)

            @block.vector
            def _(dve):
                def ctx_lo(b, par, t):
                    dve.wait_ge(cthi, b * NCT + t + 1)
                    hi, lo = ct[(par * NCT + t) % 2]
                    nc.vector.tensor_tensor(lo[:], craw[:, :, t * CR:(t + 1) * CR], f32(hi[:]), ALU.subtract).then_inc(ctlo, 1)

                def k_norm(b, t, bank):
                    dve.wait_ge(cpow, b * NCT + t + 1)
                    if not (isinstance(b, int) and b == 0):
                        dve.wait_ge(ktr, b * NKT)
                    for h in range(NKV):
                        nc.vector.scalar_tensor_tensor(out=ktok[:, t, h, :], in0=bank[0:CR, h * HD:(h + 1) * HD],
                                                       scalar=crk[:, t, h:h + 1], in1=c["wkn"][0:CR, :],
                                                       op0=ALU.mult, op1=ALU.mult).then_inc(kscaled, 1)

                def filler(b, par, k, use):
                    if use == SPLIT:
                        ctx_lo(b, par, 0)
                        return
                    if use and order[use - 1][0] == "k":
                        k_norm(b, order[use - 1][1], mbank[(use - 1) % 2])
                    kind, t = order[use]
                    bank = mbank[use % 2]
                    if (kind, t) in splits:
                        ctx_lo(b, par, splits[kind, t])
                    if kind == "k":
                        dve.wait_ge(csqd, b * NCT + t + 1)
                        if not (isinstance(b, int) and b == 0):
                            dve.wait_ge(cadd, (b - 1) * NCT + t + 1)
                        nc.vector.tensor_reduce(css[:, t, :], sq[:], AX.X, ALU.add).then_inc(csum, 1)
                    elif kind == "v":
                        dve.wait_ge(vhi, b * NCT + t + 1)
                        nc.vector.tensor_tensor(V[par][1][:, t, :], bank[0:CR, :], f32(V[par][0][:, t, :]), ALU.subtract).then_inc(vlo, 1)
                    else:
                        n = L if t == NCT else CR
                        dve.wait_ge(kthi, b * NKT + T_ORDER.index(t) + 1)
                        nc.vector.tensor_tensor(kT[par][1][:, :, t * CR:t * CR + n],
                                                bank[:, 0:NKV * CR].rearrange("p (h r) -> p h r", h=NKV)[:, :, 0:n],
                                                f32(kT[par][0][:, :, t * CR:t * CR + n]), ALU.subtract).then_inc(ktlo, 1)

                def q_lo(b, g):
                    dve.wait_ge(qthi, b * NKV + g + 1)
                    if not (isinstance(b, int) and b == 0 and g < 2):
                        dve.wait_ge(scored, (b * NKV + g - 1) * REP)
                    nc.vector.tensor_tensor(qT[g % 2][1][:], qbank[:, 0:GW], f32(qT[g % 2][0][:]), ALU.subtract).then_inc(qtlo, 1)

                def p_lo(b, g, h):
                    n = b * NH + g * REP + h
                    dve.wait_ge(pthi, n + 1)
                    if h == 0 and not (isinstance(b, int) and b == 0 and g == 0):
                        dve.wait_ge(pv, b * NKV + g)
                    nc.vector.tensor_tensor(pT[1][:, :, h * L:(h + 1) * L],
                                            pbank[h % 2][0:CR, 0:NKT * L].rearrange("r (t l) -> r t l", t=NKT),
                                            f32(pT[0][:, :, h * L:(h + 1) * L]), ALU.subtract).then_inc(ptlo, 1)

                def o_read(b, g):
                    n = b * NKV + g
                    dve.wait_ge(pv, n + 1)
                    if not (isinstance(b, int) and b == 0 and g < 2):
                        dve.wait_ge(o_out[g % 2], (b * (NKV // 2) + g // 2) * 16)
                    nc.vector.tensor_copy(oT[g % 2][:], obank[:, 0:GW]).then_inc(oev, 1)

                def prev(b, g):
                    return (b, g - 1) if g else (b - 1, NKV - 1)

                def invert(b, g, h):
                    n = b * NH + g * REP + h
                    col = g * REP + h
                    dve.wait_ge(exped, n + 1)
                    if not (isinstance(b, int) and b == 0):
                        dve.wait_ge(normed, n + 1 - NH)
                    nc.vector.reciprocal(ri[:, col:col + 1], rs[:, col:col + 1]).then_inc(inverted, 1)

                def step(b, par, k, g, h):
                    n = b * NH + g * REP + h
                    col = g * REP + h
                    dve.wait_ge(scored, n + 1)
                    nc.vector.tensor_reduce(mx[:, col:col + 1], sbank[h % 2][0:L, 0:NKEY], AX.X, ALU.max).then_inc(maxed, 1)
                    if not (isinstance(b, int) and b == 0 and g == 0):
                        if h == 1:
                            before = prev(b, g)
                            if not (isinstance(b, int) and b == 0 and g == 1):
                                o_read(*prev(*before))
                        p_lo(*prev(b, g), h)
                    dve.wait_ge(maxed, n + 1)
                    if not (isinstance(b, int) and b == 0):
                        dve.wait_ge(exped, n + 1 - NH)
                    nc.vector.tensor_scalar(nb[:, col:col + 1], mx[:, col:col + 1], c["rq"][:, bass.ds(n, 1)], -1.0, ALU.mult, ALU.mult).then_inc(biased, 1)
                    if h:
                        invert(b, g, h - 1)

                def last(b, par, k, g):
                    invert(b, g, REP - 1)
                    if g < NKV - 1:
                        q_lo(b, g + 1)
                    elif not (isinstance(b, int) and b == B - 1):
                        q_lo(b + 1, 0)

                def start():
                    for m in (*V[0], *V[1]):
                        nc.vector.memset(f32(m[96:CR, NCT, :]), 0.0).then_inc(pads, 1)
                    q_lo(0, 0)

                schedule(dve, start, step, filler, last)
                o_read(B - 1, NKV - 2)
                for h in range(REP):
                    p_lo(B - 1, NKV - 1, h)
                o_read(B - 1, NKV - 1)

            @block.tensor
            def _(pe):
                def q_t(b, par, k, g):
                    pe.wait_ge(q_in[par], k * 16 + 16)
                    if not (isinstance(b, int) and b == 0 and g == 0):
                        pe.wait_ge(qtlo, b * NKV + g)
                    for r in range(REP):
                        hh = g * REP + r
                        mm = nc.tensor.transpose(qbank[:, r * L:(r + 1) * L], q[par][:, hh * HD:(hh + 1) * HD], c["ident"][0:L, 0:L])
                    mm.then_inc(qtr, 1)

                def bank_read(b, use):
                    kind, t = order[use]
                    if kind == "k":
                        pe.wait_ge(kscaled, (b * NCT + t + 1) * NKV)
                    elif kind == "v":
                        pe.wait_ge(vlo, b * NCT + t + 1)
                    else:
                        pe.wait_ge(ktlo, b * NKT + T_ORDER.index(t) + 1)

                def filler(b, par, k, use):
                    if use == SPLIT:
                        return
                    kind, t = order[use]
                    bank = mbank[use % 2]
                    ctb = ct[(par * NCT + t) % 2]
                    if use >= 2:
                        bank_read(b, use - 2)
                    elif not (isinstance(b, int) and b == 0):
                        bank_read(b - 1, NM + use - 2)
                    if kind in "kv":
                        pe.wait_ge(ctlo, b * NCT + t + 1)
                        i = 0 if kind == "k" else 1
                        for kt in range(KT):
                            mm = mm3(nc, bank[0:CR, :], ctb[0][:, kt, :], ctb[1][:, kt, :],
                                     wch[:, kt, i, :], wcl[:, kt, i, :], kt == 0, kt == KT - 1)
                        mm.then_inc(kproj if kind == "k" else vproj, 1)
                    else:
                        n = L if t == NCT else CR
                        if t == NCT:
                            pe.wait_ge(kself_in, b * 16 + 16)
                        else:
                            pe.wait_ge(kscaled, (b * NCT + t + 1) * NKV)
                        for h in range(NKV):
                            mm = nc.tensor.transpose(bank[:, h * CR:h * CR + n], ktok[0:n, t, h, :], c["ident"][0:n, 0:n])
                        mm.then_inc(ktr, 1)

                def p_t(b, g, h):
                    n = b * NH + g * REP + h
                    p = Pm[(g % 2) * REP + h]
                    pe.wait_ge(normed, n + 1)
                    if not (isinstance(b, int) and b == 0 and g == 0 and h < 2):
                        pe.wait_ge(ptlo, n - 1)
                    for t in range(NKT):
                        mm = nc.tensor.transpose(pbank[h % 2][0:CR, t * L:(t + 1) * L], p[:, t * CR:(t + 1) * CR], c["ident"][0:L, 0:L])
                    mm.then_inc(ptr, 1)

                def pv_of(b, par, g):
                    n = b * NKV + g
                    pe.wait_ge(ptlo, (n + 1) * REP)
                    if not (isinstance(b, int) and b == 0 and g == 0):
                        pe.wait_ge(oev, n)
                    for t in range(NKT):
                        mm = mm3(nc, obank[:, 0:GW], V[par][0][:, t, g * HD:(g + 1) * HD], V[par][1][:, t, g * HD:(g + 1) * HD],
                                 pT[0][:, t, :], pT[1][:, t, :], t == 0, t == NKT - 1)
                    mm.then_inc(pv, 1)

                def prev(b, par, g):
                    return (b, par, g - 1) if g else (b - 1, 1 - par, NKV - 1)

                def step(b, par, k, g, h):
                    n = b * NH + g * REP + h
                    if h == 0:
                        pe.wait_ge(qtlo, b * NKV + g + 1)
                        if g == 0:
                            pe.wait_ge(ktlo, b * NKT + NKT)
                            pe.wait_ge(vlo, b * NCT + NCT)
                            pe.wait_ge(vslo, b + 1)
                    if not (isinstance(b, int) and b == 0 and g == 0 and h < 2):
                        pe.wait_ge(exped, n - 1)
                    cols = slice(h * L, (h + 1) * L)
                    bank = sbank[h % 2]
                    mm3(nc, bank[0:L, 0:NSC], qT[g % 2][0][:, cols], qT[g % 2][1][:, cols],
                        kT[par][0][:, g, :], kT[par][1][:, g, :], True, False)
                    nc.tensor.matmul(bank[0:L, MO:NSC], c["identr"][0:L, 0:L], mask[:], start=False, stop=True).then_inc(scored, 1)
                    if not (isinstance(b, int) and b == 0 and g == 0):
                        pb, _, pg = prev(b, par, g)
                        p_t(pb, pg, h)

                def last(b, par, k, g):
                    if g < NKV - 1:
                        q_t(b, par, k, g + 1)
                    elif not (isinstance(b, int) and b == B - 1):
                        q_t(b + 1, 1 - par, k + par, 0)
                    if not (isinstance(b, int) and b == 0 and g == 0):
                        pv_of(*prev(b, par, g))

                def prologue():
                    pe.wait_ge(mask_set, 1)
                    pe.wait_ge(pads, 2 * REP + 8)
                    q_t(0, 0, 0, 0)

                schedule(pe, prologue, step, filler, last)
                for h in range(REP):
                    p_t(B - 1, NKV - 1, h)
                pv_of(B - 1, 1, NKV - 1)


def out_projection(nc, io, scratch, banks, c, x1, x2h, x2l):
    with ExitStack() as ctx:
        def sb(name, shape, dt=F32):
            return ctx.enter_context(nc.sbuf_tensor(name, shape, dt))

        def sem(name):
            return ctx.enter_context(nc.semaphore(name))

        waited = sem("waited")

        NW = 4
        HW = NH // NW
        woh, wol = sb("wo_hi", [128, NH, DM], F32R), sb("wo_lo", [128, NH, DM], F32R)
        wraw = [sb(f"wo_raw{i}", [128, HW, DM]) for i in range(2)]
        oraw = sb("o_raw", [128, NH * L])
        oh = [sb(f"o_hi{i}", [128, NH * L], F32R) for i in range(2)]
        ol = [sb(f"o_lo{i}", [128, NH * L], F32R) for i in range(2)]
        x = [sb(f"x_in{i}", [L, DM]) for i in range(2)]
        st, mv, ve, rstd = sb("st2", [L, 6]), sb("mv2", [L, 2]), sb("ve2", [L, 1]), sb("rstd2", [L, 1])
        xn = sb("xn2", [L, DM])

        w_in, o_in, x_in = [sem(f"wo_in{i}") for i in range(2)], sem("o_in"), [sem(f"x_ins{i}") for i in range(2)]
        whi, wlo, ohi, olo = sem("wo_his"), sem("wo_los"), sem("o_his"), sem("o_los")
        proj, x1_set, ln_st, ln_mv, ln_ve, ln_r, ln_x = (sem(n) for n in (
            "o_proj", "x1_set", "ln2_st", "ln2_mv", "ln2_ve", "ln2_r", "ln2_x"))
        t_done, th, tl = sem("x2_psum"), sem("x2_his"), sem("x2_los")
        ybank, tbank = banks[0:2], banks[2]

        with nc.Block() as block:
            @block.sync
            def _(sp):
                def load(b, par, k):
                    if not (isinstance(b, int) and b == 0):
                        sp.wait_ge(olo, b)
                    sp.dma_start(oraw[:], scratch["o"][at(b, 1), :, :].rearrange("a p n -> (a p) n")).then_inc(o_in, 16)
                    if not (isinstance(b, int) and b < 2):
                        sp.wait_ge(x1_set, b - 1)
                    sp.dma_start(x[par][:], io["x"][at(b, 1), :, :].rearrange("a l d -> (a l) d")).then_inc(x_in[par], 16)

                for n in range(NW):
                    if n >= 2:
                        sp.wait_ge(wlo, n - 1)
                    sp.dma_start(wraw[n % 2][:], io["wo"][:, n * HW:(n + 1) * HW, :]).then_inc(w_in[n % 2], 16)
                    if n == 1:
                        load(0, 0, 0)
                with sp.Fori(0, (B - 2) // 2) as i:
                    load(i * 2 + 1, 1, i)
                    load(i * 2 + 2, 0, i + 1)
                load(B - 1, 1, (B - 2) // 2)

            @block.gpsimd
            def _(pool):
                def batch(b, par, k):
                    pool.wait_ge(ln_mv, b + 1)
                    pool.sem_inc(waited, 1)
                    nc.gpsimd.tensor_scalar(ve[:], mv[:, 1:2], 1.0, EPS_LN, ALU.mult, ALU.add).then_inc(ln_ve, 1)
                    pool.wait_ge(ln_ve, b + 1)
                    nc.gpsimd.tensor_tensor(rstd[:], ve[:], c["neghalf"][0:L, 0:1], ALU.pow).then_inc(ln_r, 1)

                over_batches(pool, batch)

            @block.scalar
            def _(act):
                def o_hi(b, par):
                    act.wait_ge(o_in, b * 16 + 16)
                    if not (isinstance(b, int) and b < 2):
                        act.wait_ge(proj, b - 1)
                    nc.scalar.activation(oh[par][:], oraw[:], ACT.Copy).then_inc(ohi, 1)

                for n in range(NW):
                    act.wait_ge(w_in[n % 2], 16 * (n // 2 + 1))
                    nc.scalar.activation(woh[:, n * HW:(n + 1) * HW, :], wraw[n % 2][:], ACT.Copy).then_inc(whi, 1)
                    if n == 0:
                        o_hi(0, 0)

                def batch(b, par, k):
                    if not (isinstance(b, int) and b == B - 1):
                        o_hi(b + 1, 1 - par)
                    act.wait_ge(t_done, b + 1)
                    nc.scalar.activation(x2h[:, :, at(b, L)], tbank[:, 0:KT * L].rearrange("p (k l) -> p k l", k=KT), ACT.Copy).then_inc(th, 1)

                over_batches(act, batch)

            @block.vector
            def _(dve):
                def o_lo(b, par):
                    dve.wait_ge(ohi, b + 1)
                    if not (isinstance(b, int) and b < 2):
                        dve.wait_ge(proj, b - 1)
                    nc.vector.tensor_tensor(ol[par][:], oraw[:], f32(oh[par][:]), ALU.subtract).then_inc(olo, 1)

                for n in range(NW):
                    dve.wait_ge(whi, n + 1)
                    nc.vector.tensor_tensor(wol[:, n * HW:(n + 1) * HW, :], wraw[n % 2][:], f32(woh[:, n * HW:(n + 1) * HW, :]), ALU.subtract).then_inc(wlo, 1)
                    if n == 0:
                        o_lo(0, 0)

                def batch(b, par, k):
                    if not (isinstance(b, int) and b == B - 1):
                        o_lo(b + 1, 1 - par)
                    x1b = x1[:, at(b, 1), :].rearrange("l a d -> l (a d)")
                    dve.wait_ge(proj, b + 1)
                    dve.wait_ge(x_in[par], k * 16 + 16)
                    nc.vector.scalar_tensor_tensor(out=x1b, in0=ybank[par][0:L, :], scalar=c["tanhg"][0:L, 0:1],
                                                   in1=x[par][:], op0=ALU.mult, op1=ALU.add).then_inc(x1_set, 1)
                    dve.wait_ge(x1_set, b + 1)
                    dve.sem_inc(waited, 1)
                    nc.vector.bn_stats(st[:], x1b).then_inc(ln_st, 1)
                    dve.wait_ge(ln_st, b + 1)
                    dve.sem_inc(waited, 1)
                    nc.vector.bn_aggr(mv[:], st[:]).then_inc(ln_mv, 1)
                    dve.wait_ge(ln_r, b + 1)
                    dve.wait_ge(ln_mv, b + 1)
                    if not (isinstance(b, int) and b == 0):
                        dve.wait_ge(t_done, b)
                    nc.vector.tensor_scalar(xn[:], x1b, mv[:, 0:1], rstd[:], ALU.subtract, ALU.mult).then_inc(ln_x, 1)
                    dve.wait_ge(th, b + 1)
                    nc.vector.tensor_tensor(x2l[:, :, at(b, L)], tbank[:, 0:KT * L].rearrange("p (k l) -> p k l", k=KT),
                                            f32(x2h[:, :, at(b, L)]), ALU.subtract).then_inc(tl, 1)

                over_batches(dve, batch)

            @block.tensor
            def _(pe):
                def x2t(b):
                    pe.wait_ge(ln_x, b + 1)
                    if not (isinstance(b, int) and b == 0):
                        pe.wait_ge(tl, b)
                    for kt in range(KT):
                        mm = nc.tensor.transpose(tbank[:, kt * L:(kt + 1) * L], xn[:, kt * 128:(kt + 1) * 128], c["ident"][0:L, 0:L])
                    mm.then_inc(t_done, 1)

                def batch(b, par, k):
                    pe.wait_ge(olo, b + 1)
                    if not (isinstance(b, int) and b < 2):
                        pe.wait_ge(x1_set, b - 1)
                    for h in range(NH):
                        if isinstance(b, int) and b == 0 and h % HW == 0:
                            pe.wait_ge(wlo, h // HW + 1)
                        cols = slice(h * L, (h + 1) * L)
                        mm = mm3(nc, ybank[par][0:L, :], oh[par][:, cols], ol[par][:, cols], woh[:, h, :], wol[:, h, :], h == 0, h == NH - 1)
                    mm.then_inc(proj, 1)
                    if not (isinstance(b, int) and b == 0):
                        x2t(b - 1)

                over_batches(pe, batch)
                x2t(B - 1)


def experts(nc, io, out, banks, c, x1, x2h, x2l):
    with ExitStack() as ctx:
        def sb(name, shape, dt=F32):
            return ctx.enter_context(nc.sbuf_tensor(name, shape, dt))

        def sem(name):
            return ctx.enter_context(nc.semaphore(name))

        waited = sem("waited")

        NJ = NFT + 1
        TB = KT * 256
        TW = KT * 2 * TAIL
        RING = 3
        assert NJ % RING == 0
        praw = [sb(f"up_raw{i}", [128, KT * 256]) for i in range(RING)]
        uph = [sb(f"up_hi{i}", [128, KT, 256], F32R) for i in range(2)]
        upl = [sb(f"up_lo{i}", [128, KT, 256], F32R) for i in range(2)]
        draw = sb("down_raw", [128, NJ, DM])
        dh, dl = sb("down_hi", [128, NJ, DM], F32R), sb("down_lo", [128, NJ, DM], F32R)
        uh, ul = sb("u_hi", [128, NJ, NT], F32R), sb("u_lo", [128, NJ, NT], F32R)
        sil = [sb(f"silu{i}", [128, HALF]) for i in range(2)]
        tt = [sb(f"h1h3_{i}", [128, HALF]) for i in range(2)]
        uf = [sb(f"u_f32_{i}", [128, HALF]) for i in range(2)]
        y = sb("y_t", [128, KT, NT])
        ob = [draw[0:L, i, :] for i in range(2)]
        gwraw = sb("gate_raw", [128, KT, E])
        gwh, gwl = sb("gate_hi", [128, KT, 128], F32R), sb("gate_lo", [128, KT, 128], F32R)
        bias = sb("router_bias", [L, B, E])
        lt = y[0:E, 0, :]
        sc, se, eq, pk = (sb(n, [L, B, E]) for n in ("scores", "select", "equal", "picked"))
        one1, rev, got = sb("first_pick", [L, B, E]), sb("reverse_index", [L, B, E]), sb("chosen", [L, B, E])
        rd, ws = sb("reduced", [L, B]), sb("weight_sum", [L, B])
        gf = sb("gates_f32", [L, B, E])
        ghr = sb("gates_hi", [L, B, E], F32R)
        gg = sb("gates_grouped", [L, B, E // 2, 4])
        selraw, sel = sb("sel_raw", [4, NJ * 128]), sb("sel", [4, NJ * 128], F32R)
        oneraw = y[0:4, 1, :]
        gT = sb("gates_t", [4, NG, NT], F32R)

        up_in = [sem(f"up_in{i}") for i in range(RING)]
        down_in, sm_in = sem("down_in"), sem("small_in")
        uphi, uplo, dhi, dlo = sem("up_his"), sem("up_los"), sem("down_his"), sem("down_los")
        zeroed, gwhi, gwlo, sels = sem("zeroed"), sem("gate_w_hi"), sem("gate_w_lo"), sem("sel_set")
        lgt, ltc, ltr, chain = sem("logits"), sem("logits_copied"), sem("logits_back"), sem("router_step")
        sigm, ggt, gtr, gtc = sem("sigmoid"), sem("gates_set"), sem("gates_turned"), sem("gates_t_set")
        h_done, sil_s, h_free, g_done, g_free = (sem(n) for n in ("h_done", "silu_s", "h_read", "gate_rows", "u_set"))
        uhi, ulo, d_done, y_set = sem("u_his"), sem("u_los"), sem("down_done"), sem("y_set")
        otr, oset, oout = sem("out_turned"), sem("out_set"), [sem(f"out_stored{i}") for i in range(2)]
        h1b, h3b, gb, yb = banks[0:2], banks[2:4], banks[4], banks[5:7]
        xb = banks[7]
        NCHAIN = 14

        def raw(j):
            return praw[j % RING][:, 0:TB if j < NFT else TW].rearrange("p (k n) -> p k n", k=KT)

        def rows(j):
            return 128 if j < NFT else TAIL

        with nc.Block() as block:
            @block.sync
            def _(sp):
                sp.dma_start(gwraw[:], io["gate_wt"]).then_inc(sm_in, 16)
                sp.dma_start(selraw[:], io["c_sel"]).then_inc(sm_in, 16)
                sp.dma_start(oneraw, io["c_one"]).then_inc(sm_in, 16)
                sp.dma_start(rev[:], io["c_rev"]).then_inc(sm_in, 16)
                for b in range(B):
                    sp.dma_start(bias[:, b, :], io["router_bias"].partition_broadcast(L)).then_inc(sm_in, 16)

                def group(g):
                    for j in range(NJ):
                        if not (isinstance(g, int) and g == 0 and j < RING):
                            sp.wait_ge(uplo, g * NJ + j + 1 - RING)
                        w = TB if j < NFT else TW
                        sp.dma_start(praw[j % RING][:, 0:w],
                                     io["w13"][at(g, 1), :, j * TB:j * TB + w].rearrange("a p n -> (a p) n")).then_inc(up_in[j % RING], 16)
                        if j == 1:
                            if not (isinstance(g, int) and g == 0):
                                sp.wait_ge(dlo, g)
                            sp.dma_start(draw[:, 0:NFT, :], io["w2"][at(g, 1), :, :, :].rearrange("a p j d -> (a p) j d")).then_inc(down_in, 16)
                            sp.dma_start(draw[0:TAIL, NFT, :], io["w2t"][at(g, 1), :, :].rearrange("a p d -> (a p) d")).then_inc(down_in, 16)

                group(0)
                with sp.Fori(1, NG) as g:
                    group(g)
                for b in range(B):
                    sp.wait_ge(oset, b + 1)
                    sp.dma_start(out[b], ob[b % 2]).then_inc(oout[b % 2], 16)
                for i in range(2):
                    sp.wait_ge(oout[i], 16 * B // 2)

            @block.gpsimd
            def _(pool):
                nc.gpsimd.memset(f32(gwh[:]), 0.0).then_inc(zeroed, 1)
                nc.gpsimd.memset(f32(gwl[:]), 0.0).then_inc(zeroed, 1)
                pool.wait_ge(zeroed, 2)
                pool.wait_ge(sm_in, (4 + B) * 16)
                pool.sem_inc(waited, 1)
                nc.gpsimd.tensor_copy(gwh[:, :, 0:E], gwraw[:]).then_inc(gwhi, 1)
                pool.wait_ge(gwhi, 1)
                nc.gpsimd.tensor_tensor(gwl[:, :, 0:E], gwraw[:], f32(gwh[:, :, 0:E]), ALU.subtract).then_inc(gwlo, 1)
                pool.sem_inc(waited, 1)
                nc.gpsimd.tensor_copy(sel[:], selraw[:]).then_inc(sels, 1)
                pool.sem_inc(waited, 1)
                nc.gpsimd.tensor_copy(gT[:, 0, :], oneraw).then_inc(sels, 1)

                def group(g):
                    pool.wait_ge(down_in, g * 32 + 32)
                    if not (isinstance(g, int) and g == 0):
                        pool.wait_ge(d_done, g * 2 * KT)
                    for part in (slice(0, NFT), slice(NFT, NJ)):
                        r = 128 if part.start == 0 else TAIL
                        pool.sem_inc(waited, 1)
                        nc.gpsimd.tensor_copy(dh[0:r, part, :], draw[0:r, part, :]).then_inc(dhi, 1)
                    pool.wait_ge(dhi, g * 2 + 2)
                    for part in (slice(0, NFT), slice(NFT, NJ)):
                        r = 128 if part.start == 0 else TAIL
                        op = nc.gpsimd.tensor_tensor(dl[0:r, part, :], draw[0:r, part, :], f32(dh[0:r, part, :]), ALU.subtract)
                    op.then_inc(dlo, 1)
                    for j in range(NJ):
                        for s in range(2):
                            n = (g * NJ + j) * 2 + s
                            pool.wait_ge(g_free, n + 1)
                            r = rows(j)
                            cols = slice(s * HALF, (s + 1) * HALF)
                            pool.sem_inc(waited, 1)
                            nc.gpsimd.tensor_copy(uh[0:r, j, cols], uf[s][0:r, :]).then_inc(uhi, 1)
                            pool.wait_ge(uhi, n + 1)
                            nc.gpsimd.tensor_tensor(ul[0:r, j, cols], uf[s][0:r, :], f32(uh[0:r, j, cols]), ALU.subtract).then_inc(ulo, 1)

                group(0)
                with pool.Fori(1, NG) as g:
                    group(g)

            @block.scalar
            def _(act):
                act.wait_ge(lgt, 2)
                for s in range(2):
                    nc.scalar.activation(lt[:, s * HALF:(s + 1) * HALF], h1b[s][0:E, 0:HALF], ACT.Copy).then_inc(ltc, 1)
                act.wait_ge(ltr, 1)
                nc.scalar.activation(sc[:], xb[0:L, 0:B * E].rearrange("l (b e) -> l b e", b=B), ACT.Sigmoid).then_inc(sigm, 1)

                def split(g, j):
                    w = 256 if j < NFT else 2 * TAIL
                    n = g * NJ + j
                    act.wait_ge(up_in[j % RING], (g * (NJ // RING) + j // RING + 1) * 16)
                    if not (isinstance(g, int) and g == 0 and j < 2):
                        act.wait_ge(h_done, (n - 1) * 2)
                    nc.scalar.activation(uph[j % 2][:, :, 0:w], raw(j), ACT.Copy).then_inc(uphi, 1)

                split(0, 0)

                def group(g):
                    for j in range(NJ):
                        if j + 1 < NJ:
                            split(g, j + 1)
                        elif not (isinstance(g, int) and g == NG - 1):
                            split(g + 1, 0)
                        for s in range(2):
                            n = (g * NJ + j) * 2 + s
                            act.wait_ge(h_done, n + 1)
                            if not (isinstance(g, int) and g == 0 and j == 0):
                                act.wait_ge(h_free, n - 1)
                            if j < NFT:
                                nc.scalar.activation(sil[s][:], h1b[s][:, 0:HALF], ACT.Silu).then_inc(sil_s, 1)
                            else:
                                nc.scalar.activation(sil[s][128 - TAIL:, :], h1b[s][0:TAIL, 0:HALF], ACT.Silu).then_inc(sil_s, 1)

                group(0)
                with act.Fori(1, NG - 1) as g:
                    group(g)
                group(NG - 1)

            @block.vector
            def _(dve):
                def split(g, j):
                    w = 256 if j < NFT else 2 * TAIL
                    n = g * NJ + j
                    dve.wait_ge(uphi, n + 1)
                    nc.vector.tensor_tensor(upl[j % 2][:, :, 0:w], raw(j), f32(uph[j % 2][:, :, 0:w]), ALU.subtract).then_inc(uplo, 1)

                count = [0]

                def router():
                    def then(op):
                        op.then_inc(chain, 1)
                        count[0] += 1
                        dve.wait_ge(chain, count[0])

                    def over_e(r):
                        return r[:].unsqueeze(2).broadcast_to([L, B, E])

                    V = nc.vector
                    dve.wait_ge(sigm, 1)
                    dve.wait_ge(sm_in, (4 + B) * 16)
                    then(V.tensor_tensor(se[:], sc[:], bias[:], ALU.add))
                    for first in (True, False):
                        then(V.tensor_reduce(rd[:], se[:], AX.X, ALU.max))
                        then(V.tensor_tensor(eq[:], se[:], over_e(rd), ALU.is_equal))
                        then(V.tensor_tensor(pk[:], eq[:], rev[:], ALU.mult))
                        then(V.tensor_reduce(rd[:], pk[:], AX.X, ALU.max))
                        then(V.tensor_tensor(one1[:] if first else got[:], pk[:], over_e(rd), ALU.is_equal))
                        if first:
                            then(V.scalar_tensor_tensor(out=se[:], in0=one1[:], scalar=-1e30, in1=se[:], op0=ALU.mult, op1=ALU.add))
                    then(V.tensor_tensor(got[:], got[:], one1[:], ALU.add))
                    then(V.tensor_tensor(gf[:], got[:], sc[:], ALU.mult))
                    then(V.tensor_reduce(ws[:], gf[:], AX.X, ALU.add))
                    then(V.tensor_scalar(ws[:], ws[:], 1e-12, None, ALU.max))
                    then(V.reciprocal(ws[:], ws[:]))
                    then(V.tensor_tensor(gf[:], gf[:], over_e(ws), ALU.mult))
                    then(V.tensor_copy(ghr[:], gf[:]))
                    then(V.tensor_copy(gg[:, :, :, 0:2], f32(ghr[:]).rearrange("l b (g e) -> l b g e", e=2)))
                    V.tensor_tensor(gg[:, :, :, 2:4], gf[:].rearrange("l b (g e) -> l b g e", e=2),
                                    gg[:, :, :, 0:2], ALU.subtract).then_inc(ggt, 1)
                    for g in range(1, NG):
                        for s in range(2):
                            n = (g - 1) * 2 + s
                            dve.wait_ge(gtr, n + 1)
                            V.tensor_copy(gT[:, g, s * HALF:(s + 1) * HALF], xb[0:4, 0:HALF]).then_inc(gtc, 1)

                def group(g):
                    first = isinstance(g, int) and g == 0
                    for j in range(NJ):
                        if j + 1 < NJ:
                            split(g, j + 1)
                        elif not (isinstance(g, int) and g == NG - 1):
                            split(g + 1, 0)
                        for s in range(2):
                            n = (g * NJ + j) * 2 + s
                            a = 0 if j < NFT else 128 - TAIL
                            r = rows(j)
                            src = (h3b[s] if j < NFT else h1b[s])[a:, 0:HALF]
                            dve.wait_ge(sil_s, n + 1)
                            nc.vector.tensor_tensor(tt[s][a:, :], src, sil[s][a:, :], ALU.mult).then_inc(h_free, 1)
                            dve.wait_ge(h_free, n + 1)
                            dve.wait_ge(g_done, n + 1)
                            if not (first and j == 0):
                                dve.wait_ge(ulo, n - 1)
                            nc.vector.tensor_tensor(uf[s][0:r, :], tt[s][a:, :], gb[a:, 0:HALF], ALU.mult).then_inc(g_free, 1)
                    for s in range(2):
                        for d in range(KT):
                            n = g * 2 * KT + s * KT + d
                            dve.wait_ge(d_done, n + 1)
                            dst = y[:, d, s * HALF:(s + 1) * HALF]
                            src = yb[d % 2][:, 0:HALF]
                            if first:
                                nc.vector.tensor_copy(dst, src).then_inc(y_set, 1)
                            else:
                                dve.wait_ge(y_set, n + 1 - 2 * KT)
                                nc.vector.tensor_tensor(dst, dst, src, ALU.add).then_inc(y_set, 1)

                router()
                split(0, 0)
                group(0)
                with dve.Fori(1, NG - 1) as g:
                    group(g)
                group(NG - 1)
                for b in range(B):
                    dve.wait_ge(otr, b + 1)
                    if b >= 2:
                        dve.wait_ge(oout[b % 2], 16 * (b // 2))
                    nc.vector.scalar_tensor_tensor(out=ob[b % 2], in0=yb[b % 2][0:L, :], scalar=c["tanhg"][0:L, 1:2],
                                                   in1=x1[:, b, :], op0=ALU.mult, op1=ALU.add).then_inc(oset, 1)

            @block.tensor
            def _(pe):
                pe.wait_ge(gwlo, 1)
                for s in range(2):
                    cols = slice(s * HALF, (s + 1) * HALF)
                    for kt in range(KT):
                        mm = mm3(nc, h1b[s][:, 0:HALF], gwh[:, kt, :], gwl[:, kt, :], x2h[:, kt, cols], x2l[:, kt, cols],
                                 kt == 0, kt == KT - 1)
                    mm.then_inc(lgt, 1)
                pe.wait_ge(ltc, 2)
                for b in range(B):
                    mm = nc.tensor.transpose(xb[0:L, b * E:(b + 1) * E], lt[:, b * L:(b + 1) * L], c["ident"][0:E, 0:E])
                mm.then_inc(ltr, 1)
                pe.wait_ge(ggt, 1)
                for g in range(1, NG):
                    for s in range(2):
                        n = (g - 1) * 2 + s
                        if n:
                            pe.wait_ge(gtc, n)
                        for i in range(B // 2):
                            b = s * (B // 2) + i
                            mm = nc.tensor.transpose(xb[0:4, i * L:(i + 1) * L], gg[:, b, g - 1, :], c["ident"][0:L, 0:L])
                        mm.then_inc(gtr, 1)
                pe.wait_ge(gtc, (NG - 1) * 2)
                pe.wait_ge(sels, 2)

                def group(g):
                    first = isinstance(g, int) and g == 0
                    for j in range(NJ):
                        pe.wait_ge(uplo, g * NJ + j + 1)
                        wh, wl = uph[j % 2], upl[j % 2]
                        for s in range(2):
                            n = (g * NJ + j) * 2 + s
                            cols = slice(s * HALF, (s + 1) * HALF)
                            if not (first and j == 0):
                                pe.wait_ge(h_free, n - 1)
                            for i, bank in enumerate((h1b[s], h3b[s]) if j < NFT else (h1b[s],)):
                                ws = slice(i * 128, (i + 1) * 128)
                                for kt in range(KT):
                                    mm = mm3(nc, bank[:, 0:HALF], wh[:, kt, ws], wl[:, kt, ws],
                                             x2h[:, kt, cols], x2l[:, kt, cols], kt == 0, kt == KT - 1)
                            mm.then_inc(h_done, 1)
                            if not (first and j == 0 and s == 0):
                                pe.wait_ge(g_free, n)
                                pe.sem_inc(waited, 1)
                            nc.tensor.matmul(gb[:, 0:HALF], sel[:, j * 128:(j + 1) * 128],
                                             gT[:, at(g, 1), cols].rearrange("e a n -> e (a n)"), start=True, stop=True).then_inc(g_done, 1)
                    pe.wait_ge(ulo, (g + 1) * 2 * NJ)
                    pe.wait_ge(dlo, g + 1)
                    for s in range(2):
                        cols = slice(s * HALF, (s + 1) * HALF)
                        for d in range(KT):
                            n = g * 2 * KT + s * KT + d
                            if not (first and s == 0 and d < 2):
                                pe.wait_ge(y_set, n - 1)
                            for j in range(NJ):
                                r = rows(j)
                                dc = slice(d * 128, (d + 1) * 128)
                                mm = mm3(nc, yb[d % 2][:, 0:HALF], dh[0:r, j, dc], dl[0:r, j, dc],
                                         uh[0:r, j, cols], ul[0:r, j, cols], j == 0, j == NJ - 1)
                            mm.then_inc(d_done, 1)

                group(0)
                with pe.Fori(1, NG) as g:
                    group(g)
                for b in range(B):
                    if b < 2:
                        pe.wait_ge(y_set, NG * 2 * KT)
                    else:
                        pe.wait_ge(oset, b - 1)
                    for d in range(KT):
                        mm = nc.tensor.transpose(yb[b % 2][0:L, d * 128:(d + 1) * 128], y[:, d, b * L:(b + 1) * L], c["ident"][:])
                    mm.then_inc(otr, 1)


def kernel(**inputs):
    import numpy as _np
    import concourse.bacc as _bacc
    from concourse import mybir as _mybir
    from concourse.bass_utils import run_bass_kernel_spmd as _run

    a = {n: _np.asarray(v) for n, v in inputs.items()}
    p = "L0_xattn_"
    f = "L0_ffn_"

    def rows_first(w):
        return w.reshape(w.shape[0] // 128, 128, w.shape[1]).transpose(1, 0, 2)

    def groups(w, shared):
        return _np.concatenate([shared[None], w.reshape(E // 2, 2, DM, INTER).transpose(0, 2, 1, 3).reshape(E // 2, DM, GH)])

    w1 = groups(a[f + "W1"], a[f + "sw1"].T).reshape(NG, KT, 128, GH).transpose(0, 2, 1, 3)
    w3 = groups(a[f + "W3"], a[f + "sw3"].T).reshape(NG, KT, 128, GH).transpose(0, 2, 1, 3)
    tiles = []
    for j in range(NFT + 1):
        cols = slice(j * 128, min((j + 1) * 128, GH))
        tiles.append(_np.concatenate([w1[..., cols], w3[..., cols]], -1).reshape(NG, 128, -1))
    w2 = _np.concatenate([a[f + "sw2"].T[None], a[f + "W2"].reshape(E // 2, GH, DM)])
    arrays = {
        "x": a["x"],
        "ctxt": a["ctx_2048"].transpose(0, 2, 1).reshape(B, KT, 128, T).transpose(0, 2, 1, 3),
        "g_xattn": a["g_xattn"], "g_ffn": a["g_ffn"],
        "wqkv": rows_first(_np.concatenate([a[p + "wq"], a[p + "wk"], a[p + "wv"]], 1)),
        "wctx": rows_first(_np.concatenate([a[p + "wk_ctx"], a[p + "wv_ctx"]], 1)),
        "wo": rows_first(a[p + "wo"]),
        "qn": a[p + "q_norm_w"], "kn": a[p + "k_norm_w"],
        "gate_wt": rows_first(a[f + "gate_w"].T),
        "router_bias": a[f + "router_bias"],
        "w13": _np.concatenate(tiles, -1),
        "w2": w2[:, :NFT * 128].reshape(NG, NFT, 128, DM).transpose(0, 2, 1, 3),
        "w2t": w2[:, NFT * 128:],
        **constants(),
    }
    nc = _bacc.Bacc("TRN2", target_bir_lowering=False, num_devices=1)
    launch, io = {}, {}
    for name, v in arrays.items():
        launch[f"in_{name}"] = _np.ascontiguousarray(v)
        io[name] = nc.dram_tensor(f"in_{name}", v.shape, _mybir.dt.float32, kind="ExternalInput").ap()
    out = nc.dram_tensor("out", (B, L, DM), _mybir.dt.float32, kind="ExternalOutput").ap()
    build(nc, io, out)
    r = _run(nc, [launch], core_ids=[0])
    return r.results[0]["out"]
```

```python
from contextlib import ExitStack

import numpy as np

import concourse.bass as bass
from concourse import mybir

F32 = mybir.dt.float32
F32R = mybir.dt.float32r
ALU = mybir.AluOpType
ACT = mybir.ActivationFunctionType
AX = mybir.AxisListType

B, L, DM = 8, 112, 512
T = 375
NH, NKV, HD = 16, 4, 128
REP = NH // NKV
KT = DM // 128
CR = 125
NCT = T // CR
NKT = NCT + 1
NKEY = T + L
NSC = NKEY + NKEY % 2
MO = T - T % 2
MW = NSC - MO
NPAD = NKT * CR
QW, KW = NH * HD, NKV * HD
GW = REP * L
NQ = QW // 512
E, INTER, TOPK = 8, 352, 2
GH = 2 * INTER
NG = E // 2 + 1
NFT = GH // 128
TAIL = GH - NFT * 128
NT = B * L
HALF = NT // 2
NWO = 4
NJ = NFT + 1
TB = KT * 256
TW = KT * 2 * TAIL
RING = 3
EPS_LN, EPS_RMS = 1e-5, 1e-6
THETA = 10000.0
MASKED = -1e30


def constants():
    inv = 1.0 / THETA ** (np.arange(0, HD, 2, dtype=np.float32) / np.float32(HD))
    freqs = np.outer(np.arange(L, dtype=np.float32), inv.astype(np.float32)).astype(np.float32)
    emb = np.concatenate([freqs, freqs], -1)
    cos, sin = np.cos(emb).astype(np.float32), np.sin(emb).astype(np.float32)
    sin[:, :HD // 2] *= -1.0
    mask = np.zeros((L, MW), np.float32)
    mask[:, T - MO:T - MO + L] = np.where(np.arange(L)[None, :] > np.arange(L)[:, None], MASKED, 0.0)
    sel = np.zeros((4, NFT + 1, 128), np.float32)
    for j in range(NFT + 1):
        for c in range(128):
            h = j * 128 + c if j < NFT else NFT * 128 + c - (128 - TAIL)
            if NFT * 128 <= h < GH or (j < NFT):
                sel[h // INTER, j, c] = sel[2 + h // INTER, j, c] = 1.0
    return {
        "c_ident": np.eye(128, dtype=np.float32),
        "c_cos": np.ascontiguousarray(np.tile(cos, (1, 4))),
        "c_sin": np.ascontiguousarray(np.tile(sin, (1, 4))),
        "c_mask": mask,
        "c_sel": np.ascontiguousarray(sel.reshape(4, -1)),
        "c_rev": np.ascontiguousarray(np.broadcast_to(np.arange(E, 0, -1, dtype=np.float32), (L, B, E))),
    }


def at(b, n):
    return bass.ds(b * n, n)


def over_batches(eng, body):
    body(0, 0, 0)
    with eng.Fori(0, (B - 2) // 2) as i:
        body(i * 2 + 1, 1, i)
        body(i * 2 + 2, 0, i + 1)
    body(B - 1, 1, (B - 2) // 2)


def is_first(b, n=1):
    return isinstance(b, int) and b < n


def is_last(b):
    return isinstance(b, int) and b == B - 1


def f32(ap):
    return ap.bitcast(F32)


def build(nc, io, out):
    with ExitStack() as ctx:
        def dram(name, shape):
            return nc.dram_tensor(name, shape, F32).ap()

        def const_sb(name, shape, dt=F32):
            return ctx.enter_context(nc.sbuf_tensor(name, shape, dt))

        scratch = {
            "q": dram("q_roped", (NQ, B, L, 512)),
            "k": dram("k_roped", (B, L, KW)),
            "v": dram("v_self", (B, L, KW)),
            "o": dram("attn_t", (B, 128, NH * L)),
        }
        banks = [ctx.enter_context(nc.psum_tensor(f"bank{i}", [128, 512], F32)) for i in range(8)]
        c = {
            "ident": const_sb("ident", [128, 128]),
            "identr": const_sb("identr", [128, 128], F32R),
            "neghalf": const_sb("neghalf", [128, 4 * B]),
            "gates": const_sb("gates", [128, 2]),
            "tanhg": const_sb("tanhg", [128, 2]),
            "rq": const_sb("rq", [L, B * NH]),
            "wkn": const_sb("wkn", [HD, 1]),
        }
        wo = {"raw": const_sb("wo_raw0", [128, NH // NWO, DM]), "in": ctx.enter_context(nc.semaphore("wo_in0"))}
        with ExitStack() as attn:
            wch = attn.enter_context(nc.sbuf_tensor("wctx_hi", [128, KT, 2, KW], F32R))
            wcl = attn.enter_context(nc.sbuf_tensor("wctx_lo", [128, KT, 2, KW], F32R))
            tiles = {"raw": attn.enter_context(nc.sbuf_tensor("ctx_raw", [128, KT, T], F32))}
            tiles["parts"] = [[attn.enter_context(nc.sbuf_tensor(f"ctx_t_{m}{i}", [128, KT, CR], F32R)) for m in ("hi", "lo")]
                              for i in range(NCT)]
            for name in ("ctx_in", "ctx_his", "ctx_los"):
                tiles[name] = attn.enter_context(nc.semaphore(name))
            self_projections(nc, io, scratch, banks, c, wch, wcl, tiles)
            attention(nc, io, scratch, banks, c, wch, wcl, tiles, wo)
        x1 = const_sb("x1", [L, B, DM])
        x2h = const_sb("x2t_hi", [128, KT, NT], F32R)
        x2l = const_sb("x2t_lo", [128, KT, NT], F32R)
        up = {"raw": [const_sb(f"up_raw{i}", [128, TB]) for i in range(RING)],
              "in": [ctx.enter_context(nc.semaphore(f"up_in{i}")) for i in range(RING)]}
        down = {"raw": const_sb("down_raw", [128, NJ, DM]), "in": ctx.enter_context(nc.semaphore("down_in"))}
        out_projection(nc, io, scratch, banks, c, x1, x2h, x2l, wo, up, down)
        experts(nc, io, out, banks, c, x1, x2h, x2l, wo["raw"], up, down)


def mm3(nc, out, wh, wl, xh, xl, start, stop):
    nc.tensor.matmul(out, wh, xh, start=start, stop=False)
    nc.tensor.matmul(out, wh, xl, start=False, stop=False)
    return nc.tensor.matmul(out, wl, xh, start=False, stop=stop)


def load_ctx(sp, io, tiles, b):
    sp.dma_start(tiles["raw"][:], io["ctxt"][at(b, 1), :, :, :].rearrange("a p k t -> (a p) k t")).then_inc(tiles["ctx_in"], 16)


def self_projections(nc, io, scratch, banks, c, wch, wcl, tiles):
    NCH = NQ + 2
    NPB = 4
    with ExitStack() as ctx:
        def sb(name, shape, dt=F32):
            return ctx.enter_context(nc.sbuf_tensor(name, shape, dt))

        def sem(name):
            return ctx.enter_context(nc.semaphore(name))

        waited = sem("waited")

        x = sb("x_all", [L, B, DM])
        wraw = [sb(f"wraw{i}", [128, KT, 512]) for i in range(2)]
        wh = [sb(f"w_hi{i}", [128, KT, 512], F32R) for i in range(2)]
        wl = [sb(f"w_lo{i}", [128, KT, 512], F32R) for i in range(2)]
        st, mv = sb("ln_stats", [L, B, 6]), sb("ln_mv", [L, B, 2])
        ve, rstd = sb("ln_ve", [L, B]), sb("ln_rstd", [L, B])
        xn = [sb(f"xn{i}", [L, DM]) for i in range(2)]
        xh, xl = sb("xt_hi", [128, B, KT * L], F32R), sb("xt_lo", [128, B, KT * L], F32R)
        cos, sin = sb("cos", [L, 4, HD]), sb("sin", [L, 4, HD])
        wn = [sb(f"wn{i}", [L, 4, HD]) for i in range(2)]
        tc = [sb(f"cosw{i}", [L, 4, HD]) for i in range(2)]
        ts = [sb(f"sinw{i}", [L, 4, HD]) for i in range(2)]
        sq = [sb(f"sq{i}", [L, 4, HD]) for i in range(2)]
        ra = [sb(f"rope_a{i}", [L, 4, HD]) for i in range(2)]
        rb = [sb(f"rope_b{i}", [L, 4, HD]) for i in range(2)]
        qo = [sb(f"q_out{i}", [L, 4, HD]) for i in range(2)]
        ko = [sb(f"k_out{i}", [L, 4, HD]) for i in range(2)]
        ss = [sb(f"sum_sq{i}", [L, B, 4]) for i in range(2)]
        ssr, ssk, rk = sb("q_ms", [L, B, 4]), sb("k_ms", [L, B, 4]), sb("rk", [L, B, 4])

        consts_in, ident_in, x_in = sem("consts_in"), sem("ident_in"), [sem(f"x_in_{b}") for b in range(B)]
        w_in = [sem(f"w_in{i}") for i in range(2)]
        whi, wlo, neg_set, idr, tabs = sem("w_his"), sem("w_los"), sem("neg_set"), sem("idr"), sem("tables")
        ln_st, ln_mv, ln_ve, ln_r, ln_x = sem("ln_st"), sem("ln_mvs"), sem("ln_ves"), sem("ln_rs"), sem("ln_x")
        t_done, th, tl = sem("xt_psum"), sem("xt_his"), sem("xt_los")
        proj, squared, summed, mul_a, mul_b = sem("proj"), sem("squared"), sem("summed"), sem("mul_a"), sem("mul_b")
        roped, k_ss, k_r, k_fin, v_fin = sem("roped"), sem("k_ss"), sem("k_r"), sem("k_fin"), sem("v_fin")
        rows_out = [sem(f"rows_stored{i}") for i in range(2)]
        sums_read = sem("sums_read")
        q_ss, q_r, tanh_s = sem("q_ss"), sem("q_r"), sem("tanh_s")
        cbank, tbank = banks[0:NPB], banks[NPB:NPB + 2]

        def over_chunks(body):
            def run(eng):
                body(0, 0, 0, "k")
                with eng.Fori(0, NQ // 2) as i:
                    body(i * 2 + 1, 1, i, "q")
                    body(i * 2 + 2, 0, i + 1, "q")
                body(NQ + 1, 1, NQ // 2, "v")
            return run

        def heads(ap):
            return ap.rearrange("l (a d) -> l a d", a=4)

        with nc.Block() as block:
            @block.sync
            def _(sp):
                def load_x(batches):
                    for b in batches:
                        sp.dma_start(x[:, b, :], io["x"][b]).then_inc(x_in[b], 16)

                def load(m, par):
                    sp.dma_start(wraw[par][:], io["wqkv"][at(m, 1), :, :, :].rearrange("a p k n -> (a p) k n")).then_inc(w_in[par], 16)

                load_x(range(2))
                sp.dma_start(c["ident"][:], io["c_ident"]).then_inc(ident_in, 16)
                load_x(range(2, B // 2))
                load(0, 0)
                load_x(range(B // 2, B))
                sp.dma_start(cos[:], heads(io["c_cos"])).then_inc(consts_in, 16)
                sp.dma_start(sin[:], heads(io["c_sin"])).then_inc(consts_in, 16)
                for i, name in enumerate(("qn", "kn")):
                    for a in range(4):
                        sp.dma_start(wn[i][:, a, :], io[name].partition_broadcast(L)).then_inc(consts_in, 16)
                load(1, 1)
                sp.dma_start(c["wkn"][:], io["kn"].rearrange("(p a) -> p a", a=1)).then_inc(consts_in, 16)
                for i, name in enumerate(("g_xattn", "g_ffn")):
                    sp.dma_start(c["gates"][:, i:i + 1], io[name].partition_broadcast(128)).then_inc(consts_in, 16)

                def chunk(m, par, k, kind):
                    sp.wait_ge(wlo, m + 1)
                    load(m + 2, par)
                    if kind == "v":
                        load_ctx(sp, io, tiles, 0)
                    for b in range(B):
                        if kind == "q":
                            sp.wait_ge(roped, m * B + b + 1)
                            dst, src = scratch["q"][at(m - 1, 1), b, :, :], qo[b % 2]
                        elif kind == "k":
                            sp.wait_ge(k_fin, 4 * (b + 1))
                            dst, src = scratch["k"][b:b + 1], ko[b % 2]
                        else:
                            sp.wait_ge(v_fin, b + 1)
                            dst, src = scratch["v"][b:b + 1], ko[b % 2]
                        sp.dma_start(dst.rearrange("a l d -> (a l) d"), src[:].rearrange("l a d -> l (a d)")).then_inc(rows_out[b % 2], 16)

                over_chunks(chunk)(sp)
                for i in range(2):
                    sp.wait_ge(rows_out[i], 16 * NCH * B // 2)

            @block.gpsimd
            def _(pool):
                nc.gpsimd.memset(c["neghalf"][:], -0.5).then_inc(neg_set, 1)
                pool.wait_ge(neg_set, 1)
                for b in range(B):
                    pool.wait_ge(ln_mv, b + 1)
                    nc.gpsimd.tensor_scalar(ve[:, b:b + 1], mv[:, b, 1:2], 1.0, EPS_LN, ALU.mult, ALU.add).then_inc(ln_ve, 1)
                    pool.wait_ge(ln_ve, b + 1)
                    nc.gpsimd.tensor_tensor(rstd[:, b:b + 1], ve[:, b:b + 1], c["neghalf"][0:L, 0:1], ALU.pow).then_inc(ln_r, 1)

                def chunk(m, par, k, kind):
                    if kind == "v":
                        return
                    for b in range(B):
                        pool.wait_ge(mul_b, (m * B + b + 1) * 2)
                        if not (kind == "k" and b < 2):
                            if kind == "k":
                                pool.wait_ge(k_fin, 4 * (b - 1))
                            else:
                                pool.wait_ge(rows_out[b % 2], (m * (B // 2) + b // 2) * 16)
                        nc.gpsimd.tensor_tensor(qo[b % 2][:], ra[b % 2][:], rb[b % 2][:], ALU.add).then_inc(roped, 1)
                        if kind == "k":
                            pool.wait_ge(summed, b + 1)
                            nc.gpsimd.tensor_scalar(ssk[:, b, :], ss[0][:, b, :], 1.0 / HD, EPS_RMS, ALU.mult, ALU.add).then_inc(k_ss, 1)
                            pool.wait_ge(k_ss, b + 1)
                            nc.gpsimd.tensor_tensor(rk[:, b, :], ssk[:, b, :], c["neghalf"][0:L, 0:4], ALU.pow).then_inc(k_r, 1)
                    if kind == "k":
                        pool.wait_ge(k_ss, B)
                        pool.sem_inc(sums_read, 1)
                    if kind == "q":
                        pool.wait_ge(summed, (m + 1) * B)
                        pool.sem_inc(waited, 1)
                        nc.gpsimd.tensor_scalar(ssr[:], ss[par][:], 1.0, HD * EPS_RMS, ALU.mult, ALU.add).then_inc(q_ss, 1)
                        pool.wait_ge(q_ss, m)
                        pool.sem_inc(sums_read, 1)
                        nc.gpsimd.tensor_tensor(c["rq"][:, at(m - 1, B * 4)], ssr[:].rearrange("l b h -> l (b h)"),
                                                c["neghalf"][0:L, 0:B * 4], ALU.pow).then_inc(q_r, 1)

                over_chunks(chunk)(pool)

            def weight_dst(m, par, hi):
                if isinstance(m, int) and m >= NCH:
                    return (wch if hi else wcl)[:, :, m - NCH, :]
                return (wh if hi else wl)[par][:]

            @block.scalar
            def _(act):
                def weight(m, par, k):
                    act.wait_ge(w_in[par], k * 16 + 16)
                    if not (isinstance(m, int) and (m < 2 or m >= NCH)):
                        act.wait_ge(proj, (m - 1) * B)
                    nc.scalar.activation(weight_dst(m, par, True), wraw[par][:], ACT.Copy).then_inc(whi, 1)

                def xt(b):
                    act.wait_ge(t_done, b + 1)
                    nc.scalar.activation(xh[:, b, :], tbank[b % 2][:, 0:KT * L], ACT.Copy).then_inc(th, 1)

                act.wait_ge(ident_in, 16)
                nc.scalar.activation(c["identr"][:], c["ident"][:], ACT.Copy).then_inc(idr, 1)
                xt(0)
                weight(0, 0, 0)

                def k_scale(b):
                    act.wait_ge(roped, b + 1)
                    act.wait_ge(k_r, b + 1)
                    if b >= 2:
                        act.wait_ge(rows_out[b % 2], 16 * (b // 2))
                    for h in range(4):
                        nc.scalar.activation(ko[b % 2][:, h, :], qo[b % 2][:, h, :], ACT.Copy, scale=rk[:, b, h:h + 1]).then_inc(k_fin, 1)

                def chunk(m, par, k, kind):
                    for b in range(B):
                        if kind == "k" and b + 1 < B:
                            xt(b + 1)
                        if b == (2 if kind == "k" else 1):
                            weight(m + 1, 1 - par, k + par)
                        if kind == "v" and b == 3:
                            weight(m + 2, par, k + 1)
                        if kind == "v" and b >= B - NCT:
                            t = b - (B - NCT)
                            act.wait_ge(tiles["ctx_in"], 16)
                            nc.scalar.activation(tiles["parts"][t][0][:], tiles["raw"][:, :, t * CR:(t + 1) * CR], ACT.Copy).then_inc(tiles["ctx_his"], 1)
                        act.wait_ge(proj, m * B + b + 1)
                        src = heads(cbank[b % NPB][0:L, :])
                        if kind != "v":
                            if not (kind == "k" and b < 2):
                                act.wait_ge(summed, m * B + b - 1)
                            nc.scalar.activation(sq[b % 2][:], src, ACT.Square).then_inc(squared, 1)
                            if kind == "k" and b >= 2:
                                k_scale(b - 2)
                        else:
                            act.wait_ge(rows_out[b % 2], ((NQ + 1) * (B // 2) + b // 2) * 16)
                            nc.scalar.activation(ko[b % 2][:], src, ACT.Copy).then_inc(v_fin, 1)
                    if kind == "k":
                        k_scale(B - 2)
                        k_scale(B - 1)

                over_chunks(chunk)(act)
                act.wait_ge(consts_in, 13 * 16)
                nc.scalar.activation(c["tanhg"][:], c["gates"][:], ACT.Tanh).then_inc(tanh_s, 1)

            @block.vector
            def _(dve):
                def weight(m, par):
                    dve.wait_ge(whi, m + 1)
                    nc.vector.tensor_tensor(weight_dst(m, par, False), wraw[par][:], f32(weight_dst(m, par, True)), ALU.subtract).then_inc(wlo, 1)

                def stats(b):
                    dve.wait_ge(x_in[b], 16)
                    nc.vector.bn_stats(st[:, b, :], x[:, b, :]).then_inc(ln_st, 1)
                    dve.wait_ge(ln_st, b + 1)
                    nc.vector.bn_aggr(mv[:, b, :], st[:, b, :]).then_inc(ln_mv, 1)

                def xn_of(b):
                    dve.wait_ge(ln_mv, b + 1)
                    dve.wait_ge(ln_r, b + 1)
                    if b >= 2:
                        dve.wait_ge(t_done, b - 1)
                    nc.vector.tensor_scalar(xn[b % 2][:], x[:, b, :], mv[:, b, 0:1], rstd[:, b:b + 1],
                                            ALU.subtract, ALU.mult).then_inc(ln_x, 1)

                def xt(b):
                    dve.wait_ge(th, b + 1)
                    nc.vector.tensor_tensor(xl[:, b, :], tbank[b % 2][:, 0:KT * L], f32(xh[:, b, :]), ALU.subtract).then_inc(tl, 1)

                stats(0)
                stats(1)
                xn_of(0)
                stats(2)
                xn_of(1)
                stats(3)
                xt(0)
                weight(0, 0)
                for b in range(B // 2, B):
                    stats(b)
                dve.wait_ge(consts_in, 13 * 16)
                half = HD // 2
                for i in range(2):
                    nc.vector.tensor_tensor(tc[i][:], wn[i][:], cos[:], ALU.mult).then_inc(tabs, 1)
                    nc.vector.tensor_tensor(ts[i][:, :, 0:half], wn[i][:, :, half:], sin[:, :, 0:half], ALU.mult).then_inc(tabs, 1)
                    nc.vector.tensor_tensor(ts[i][:, :, half:], wn[i][:, :, 0:half], sin[:, :, half:], ALU.mult).then_inc(tabs, 1)
                dve.wait_ge(tabs, 6)

                def chunk(m, par, k, kind):
                    i = 0 if kind == "q" else 1
                    for b in range(B):
                        if kind == "k" and b + 1 < B:
                            xt(b + 1)
                            if b + 2 < B:
                                xn_of(b + 2)
                        if b == (2 if kind == "k" else 1):
                            weight(m + 1, 1 - par)
                        if kind == "v" and b == 3:
                            weight(m + 2, par)
                        if kind == "v" and b >= B - NCT:
                            t = b - (B - NCT)
                            dve.wait_ge(tiles["ctx_his"], t + 1)
                            nc.vector.tensor_tensor(tiles["parts"][t][1][:], tiles["raw"][:, :, t * CR:(t + 1) * CR],
                                                    f32(tiles["parts"][t][0][:]), ALU.subtract).then_inc(tiles["ctx_los"], 1)
                        if kind == "v":
                            continue
                        src = heads(cbank[b % NPB][0:L, :])
                        dve.wait_ge(squared, m * B + b + 1)
                        if not (kind == "k" and b < 2):
                            dve.wait_ge(roped, m * B + b - 1)
                        nc.vector.tensor_tensor(ra[b % 2][:], src, tc[i][:], ALU.mult).then_inc(mul_a, 1)
                        nc.vector.tensor_tensor(rb[b % 2][:, :, 0:half], src[:, :, half:], ts[i][:, :, 0:half], ALU.mult).then_inc(mul_b, 1)
                        nc.vector.tensor_tensor(rb[b % 2][:, :, half:], src[:, :, 0:half], ts[i][:, :, half:], ALU.mult).then_inc(mul_b, 1)
                        if b == 0 and not (isinstance(m, int) and m == 0):
                            dve.wait_ge(sums_read, m)
                        nc.vector.tensor_reduce(ss[par][:, b, :], sq[b % 2][:], AX.X, ALU.add).then_inc(summed, 1)

                over_chunks(chunk)(dve)

            @block.tensor
            def _(pe):
                pe.wait_ge(ident_in, 16)

                def xt(b):
                    pe.wait_ge(ln_x, b + 1)
                    if b >= 2:
                        pe.wait_ge(tl, b - 1)
                    for kt in range(KT):
                        mm = nc.tensor.transpose(tbank[b % 2][:, kt * L:(kt + 1) * L], xn[b % 2][:, kt * 128:(kt + 1) * 128], c["ident"][0:L, 0:L])
                    mm.then_inc(t_done, 1)

                xt(0)

                def chunk(m, par, k, kind):
                    for b in range(B):
                        if kind == "k" and b + 1 < B:
                            xt(b + 1)
                        if b == 0:
                            pe.wait_ge(wlo, m + 1)
                        if kind == "k":
                            pe.wait_ge(tl, b + 1)
                        if kind == "v" and b >= NPB:
                            pe.wait_ge(v_fin, b - NPB + 1)
                        elif not (kind == "k" and b < NPB):
                            pe.wait_ge(mul_b, (m * B + b - NPB + 1) * 2)
                        for kt in range(KT):
                            cols = slice(kt * L, (kt + 1) * L)
                            mm = mm3(nc, cbank[b % NPB][0:L, :], xh[:, b, cols], xl[:, b, cols],
                                     wh[par][:, kt, :], wl[par][:, kt, :], kt == 0, kt == KT - 1)
                        mm.then_inc(proj, 1)

                over_chunks(chunk)(pe)


def attention(nc, io, scratch, banks, c, wch, wcl, tiles, wo):
    with ExitStack() as ctx:
        def sb(name, shape, dt=F32):
            return ctx.enter_context(nc.sbuf_tensor(name, shape, dt))

        def sem(name):
            return ctx.enter_context(nc.semaphore(name))

        waited = sem("waited")

        def pair(name, shape, n=1):
            return [(sb(f"{name}_hi{i}", shape, F32R), sb(f"{name}_lo{i}", shape, F32R)) for i in range(n)]

        maskraw = sb("mask_raw", [L, MW])
        mask = sb("mask", [L, MW], F32R)
        craw, ct, ctx_in, cthi, ctlo = (tiles[n] for n in ("raw", "parts", "ctx_in", "ctx_his", "ctx_los"))
        ktok = sb("k_tok", [CR, NKT, NKV, HD])
        vraw = sb("v_raw", [L, KW])
        sq = sb("csq", [CR, NKV, HD])
        css, csr, crk = sb("css", [CR, NCT, NKV]), sb("csr", [CR, NKV]), sb("crk", [CR, NCT, NKV])
        kT = pair("k_t", [128, NKV, NSC], 2)
        V = pair("v_tok", [CR, NKT, KW], 2)
        q = [sb(f"q_tok{i}", [L, QW]) for i in range(2)]
        qT = pair("q_t", [128, GW], 2)
        Pm = [sb(f"probs{i}", [L, NPAD]) for i in range(2 * REP)]
        pT = pair("p_t", [CR, NKT, GW], 2)
        oT = [sb(f"o_t{i}", [128, GW]) for i in range(2)]
        mx, nb = sb("row_max", [L, NH]), sb("neg_bias", [L, NH])
        rs, ri = sb("row_sum", [L, NH]), sb("row_inv", [L, NH])

        mask_in, mask_set, pads = sem("mask_in"), sem("mask_set"), sem("pads")
        kself_in, vself_in = sem("kself_in"), sem("vself_in")
        q_in = [sem(f"q_in{i}") for i in range(2)]
        kproj, vproj, csqd, csum, cadd, cpow, kscaled = (sem(n) for n in (
            "kproj", "vproj", "csquared", "csummed", "cadded", "cpowered", "kscaled"))
        vhi, vlo, vshi, vslo = sem("v_his"), sem("v_los"), sem("vself_his"), sem("vself_los")
        ktr, kthi, ktlo = sem("k_transposed"), sem("k_his"), sem("k_los")
        qtr, qthi, qtlo = sem("q_transposed"), sem("q_his"), sem("q_los")
        scored, maxed, biased, exped, inverted, normed = (sem(n) for n in (
            "scored", "maxed", "biased", "exped", "inverted", "normed"))
        ptr, pthi, ptlo, pv, oev = sem("p_transposed"), sem("p_his"), sem("p_los"), sem("pv_done"), sem("o_read")
        o_out = [sem(f"o_stored{i}") for i in range(2)]
        sbank, pbank, qbank, mbank, obank = banks[0:2], banks[2:4], banks[4], banks[5:7], banks[7]

        pieces = {0: [("c", 0)], 1: [("c", 1)], 2: [("k", 0), ("c", 2)], 4: [("k", 1)], 5: [("t", 0)], 6: [("k", 2)],
                  7: [("t", 1)], 8: [("t", NCT)], 9: [("v", 0)], 11: [("v", 1)], 12: [("t", 2)], 13: [("v", 2)]}
        order = [p for at_head in pieces.values() for p in at_head]
        users = [p for p in order if p[0] != "c"]
        T_ORDER = [t for kind, t in order if kind == "t"]
        assert len(users) % 2 == 0

        def bank_of(piece):
            return mbank[users.index(piece) % 2]

        def schedule(eng, start, step, piece, tail):
            start()
            for p in order:
                piece(0, 0, *p)

            def batch(b, par, k):
                for g in range(NKV):
                    for h in range(REP):
                        step(b, par, k, g, h)
                        if not is_last(b):
                            for p in pieces.get(g * REP + h, []):
                                piece(b + 1, 1 - par, *p)

            over_batches(eng, batch)
            tail()

        def back(b, g, n):
            return b + (g - n) // NKV, (g - n) % NKV

        def exists(b, g):
            return not isinstance(b, int) or b >= 0

        with nc.Block() as block:
            @block.sync
            def _(sp):
                sp.dma_start(maskraw[:], io["c_mask"]).then_inc(mask_in, 16)

                def next_ctx(b):
                    sp.wait_ge(ctlo, b * NCT)
                    load_ctx(sp, io, tiles, b)

                def load_self(b, par):
                    if not is_first(b, 2):
                        sp.wait_ge(qtr, (b - 1) * NKV)
                    sp.dma_start(q[par][:].rearrange("l (m d) -> l m d", m=NQ), scratch["q"][:, at(b, 1), :, :].rearrange("m a l d -> (a l) m d")).then_inc(q_in[par], 16)
                    if not is_first(b):
                        sp.wait_ge(ktr, b * NKT)
                    sp.dma_start(ktok[0:L, NCT, :, :], scratch["k"][at(b, 1), :, :].rearrange("a l (h d) -> (a l) h d", h=NKV)).then_inc(kself_in, 16)
                    if not is_first(b):
                        sp.wait_ge(vslo, b)
                    sp.dma_start(vraw[:], scratch["v"][at(b, 1), :, :].rearrange("a l d -> (a l) d")).then_inc(vself_in, 16)

                def store(b, g):
                    sp.wait_ge(oev, b * NKV + g + 1)
                    sp.dma_start(scratch["o"][at(b, 1), :, g * GW:(g + 1) * GW].rearrange("a p n -> (a p) n"),
                                 oT[g % 2][:]).then_inc(o_out[g % 2], 16)

                load_self(0, 0)
                next_ctx(1)
                load_self(1, 1)

                def batch(b, par):
                    for g in range(NKV):
                        if exists(*back(b, g, 3)):
                            store(*back(b, g, 3))
                        if not (isinstance(b, int) and b >= B - 2):
                            if g == 0:
                                next_ctx(b + 2)
                            if g == 2:
                                load_self(b + 2, par)

                batch(0, 0)
                with sp.Fori(0, (B - 4) // 2) as i:
                    batch(i * 2 + 1, 1)
                    batch(i * 2 + 2, 0)
                for b in range(B - 3, B):
                    batch(b, b % 2)
                sp.dma_start(wo["raw"][:], io["wo"][:, 0:NH // NWO, :]).then_inc(wo["in"], 16)
                for n in (3, 2, 1):
                    store(*back(B, 0, n))
                for i in range(2):
                    sp.wait_ge(o_out[i], 16 * B * NKV // 2)

            @block.gpsimd
            def _(pool):
                def start():
                    for i in range(2 * REP):
                        nc.gpsimd.memset(Pm[i][:, NKEY:], 0.0).then_inc(pads, 1)
                    for i in range(2):
                        for m in kT[i]:
                            nc.gpsimd.memset(f32(m[:, :, NKEY:]), 0.0).then_inc(pads, 1)
                    pool.wait_ge(pads, 2 * REP + 8)

                def piece(b, par, kind, t):
                    if kind == "c" and is_first(b):
                        return
                    if kind == "c":
                        pool.wait_ge(ctx_in, b * 16 + 16)
                        if not is_first(b):
                            pool.wait_ge(vproj, (b - 1) * NCT + t + 1)
                        src = craw[:, :, t * CR:(t + 1) * CR]
                        pool.sem_inc(waited, 1)
                        nc.gpsimd.tensor_copy(ct[t][0][:], src).then_inc(cthi, 1)
                        pool.wait_ge(cthi, b * NCT + t + 1)
                        nc.gpsimd.tensor_tensor(ct[t][1][:], src, f32(ct[t][0][:]), ALU.subtract).then_inc(ctlo, 1)
                    if kind == "k":
                        pool.wait_ge(csum, b * NCT + t + 1)
                        if not (is_first(b) and t == 0):
                            pool.wait_ge(cpow, b * NCT + t)
                        pool.sem_inc(waited, 1)
                        nc.gpsimd.tensor_scalar(csr[:], css[:, t, :], 1.0 / HD, EPS_RMS, ALU.mult, ALU.add).then_inc(cadd, 1)
                        pool.wait_ge(cadd, b * NCT + t + 1)
                        nc.gpsimd.tensor_tensor(crk[:, t, :], csr[:], c["neghalf"][0:CR, 0:NKV], ALU.pow).then_inc(cpow, 1)
                    if kind == "v" and t == 0:
                        pool.wait_ge(vself_in, b * 16 + 16)
                        if not is_first(b, 2):
                            pool.wait_ge(pv, (b - 1) * NKV)
                        pool.sem_inc(waited, 1)
                        nc.gpsimd.tensor_copy(V[par][0][0:L, NCT, :], vraw[:]).then_inc(vshi, 1)
                        pool.wait_ge(vshi, b + 1)
                        nc.gpsimd.tensor_tensor(V[par][1][0:L, NCT, :], vraw[:], f32(V[par][0][0:L, NCT, :]), ALU.subtract).then_inc(vslo, 1)

                def norm(b, g, pair):
                    pool.wait_ge(inverted, b * (NH // 2) + g * (REP // 2) + pair + 1)
                    pool.sem_inc(waited, 1)
                    for h in (2 * pair, 2 * pair + 1):
                        p = Pm[(g % 2) * REP + h]
                        col = g * REP + h
                        nc.gpsimd.tensor_scalar(p[:, 0:NKEY], p[:, 0:NKEY], ri[:, col:col + 1], 1.0, ALU.mult, ALU.mult).then_inc(normed, 1)

                def step(b, par, k, g, h):
                    if h == 0 and exists(*back(b, g, 1)):
                        norm(*back(b, g, 1), 1)
                    if h == 2:
                        norm(b, g, 0)

                schedule(pool, start, step, piece, lambda: norm(B - 1, NKV - 1, 1))

            @block.scalar
            def _(act):
                def start():
                    act.wait_ge(mask_in, 16)
                    nc.scalar.activation(mask[:], maskraw[:], ACT.Copy).then_inc(mask_set, 1)
                    q_hi(0, 0)

                def piece(b, par, kind, t):
                    if kind == "k":
                        act.wait_ge(kproj, b * NCT + t + 1)
                        if not (is_first(b) and t == 0):
                            act.wait_ge(csum, b * NCT + t)
                        nc.scalar.activation(sq[:], bank_of((kind, t))[0:CR, :].rearrange("r (h d) -> r h d", h=NKV), ACT.Square).then_inc(csqd, 1)
                    elif kind == "v":
                        act.wait_ge(vproj, b * NCT + t + 1)
                        if not is_first(b, 2):
                            act.wait_ge(pv, (b - 1) * NKV)
                        nc.scalar.activation(V[par][0][:, t, :], bank_of((kind, t))[0:CR, :], ACT.Copy).then_inc(vhi, 1)
                    elif kind == "t":
                        n = L if t == NCT else CR
                        act.wait_ge(ktr, b * NKT + T_ORDER.index(t) + 1)
                        if not is_first(b, 2):
                            act.wait_ge(scored, (b - 1) * NH)
                        nc.scalar.activation(kT[par][0][:, :, t * CR:t * CR + n],
                                             bank_of((kind, t))[:, 0:NKV * CR].rearrange("p (h r) -> p h r", h=NKV)[:, :, 0:n],
                                             ACT.Copy, scale=1.0 if t == NCT else c["wkn"][:, 0:1]).then_inc(kthi, 1)

                def q_hi(b, g):
                    act.wait_ge(qtr, b * NKV + g + 1)
                    if not (is_first(b) and g < 2):
                        act.wait_ge(scored, (b * NKV + g - 1) * REP)
                    nc.scalar.activation(qT[g % 2][0][:], qbank[:, 0:GW], ACT.Copy).then_inc(qthi, 1)

                def p_hi(b, g, h):
                    act.wait_ge(ptr, b * NH + g * REP + h + 1)
                    if h == 0 and not (is_first(b) and g < 2):
                        act.wait_ge(pv, b * NKV + g - 1)
                    nc.scalar.activation(pT[g % 2][0][:, :, h * L:(h + 1) * L],
                                         pbank[h % 2][0:CR, 0:NKT * L].rearrange("r (t l) -> r t l", t=NKT), ACT.Copy).then_inc(pthi, 1)

                def o_read(b, g):
                    act.wait_ge(pv, b * NKV + g + 1)
                    if not (is_first(b) and g < 2):
                        act.wait_ge(o_out[g % 2], (b * (NKV // 2) + g // 2) * 16)
                    nc.scalar.activation(oT[g % 2][:], obank[:, 0:GW], ACT.Copy).then_inc(oev, 1)

                def step(b, par, k, g, h):
                    if h == REP - 1 and exists(*back(b, g, 2)):
                        o_read(*back(b, g, 2))
                    if exists(*back(b, g, 1)):
                        p_hi(*back(b, g, 1), h)
                    if h == 2 and not (is_last(b) and g == NKV - 1):
                        q_hi(*back(b, g, -1))
                    n = b * NH + g * REP + h
                    col = g * REP + h
                    act.wait_ge(biased, n + 1)
                    if not (is_first(b) and g < 2):
                        act.wait_ge(ptr, n + 1 - 2 * REP)
                    if not is_first(b):
                        act.wait_ge(normed, n + 1 - NH)
                    nc.scalar.activation(Pm[(g % 2) * REP + h][:, 0:NKEY], sbank[h % 2][0:L, 0:NKEY], ACT.Exp, bias=nb[:, col:col + 1],
                                         scale=c["rq"][:, bass.ds(g * B * REP + b * REP + h, 1)],
                                         accum_out=rs[:, col:col + 1]).then_inc(exped, 1)

                def tail():
                    for h in range(REP):
                        p_hi(B - 1, NKV - 1, h)
                    o_read(B - 1, NKV - 2)
                    o_read(B - 1, NKV - 1)

                schedule(act, start, step, piece, tail)

            @block.vector
            def _(dve):
                def k_norm(b, t):
                    dve.wait_ge(cpow, b * NCT + t + 1)
                    if not is_first(b):
                        dve.wait_ge(ktr, b * NKT)
                    nc.vector.tensor_tensor(ktok[:, t, :, :], bank_of(("k", t))[0:CR, :].rearrange("r (h d) -> r h d", h=NKV),
                                            crk[:, t, :].unsqueeze(2).broadcast_to([CR, NKV, HD]), ALU.mult).then_inc(kscaled, 1)

                def piece(b, par, kind, t):
                    if kind == "c":
                        return
                    before = users.index((kind, t)) - 1
                    if before >= 0 and users[before][0] == "k":
                        k_norm(b, users[before][1])
                    bank = bank_of((kind, t))
                    if kind == "k":
                        dve.wait_ge(csqd, b * NCT + t + 1)
                        if not is_first(b):
                            dve.wait_ge(cadd, (b - 1) * NCT + t + 1)
                        nc.vector.tensor_reduce(css[:, t, :], sq[:], AX.X, ALU.add).then_inc(csum, 1)
                    elif kind == "v":
                        dve.wait_ge(vhi, b * NCT + t + 1)
                        nc.vector.tensor_tensor(V[par][1][:, t, :], bank[0:CR, :], f32(V[par][0][:, t, :]), ALU.subtract).then_inc(vlo, 1)
                    else:
                        n = L if t == NCT else CR
                        hi, lo = (m[:, :, t * CR:t * CR + n] for m in kT[par])
                        dve.wait_ge(kthi, b * NKT + T_ORDER.index(t) + 1)
                        nc.vector.scalar_tensor_tensor(out=lo, in0=bank[:, 0:NKV * CR].rearrange("p (h r) -> p h r", h=NKV)[:, :, 0:n],
                                                       scalar=1.0 if t == NCT else c["wkn"][:, 0:1], in1=f32(hi),
                                                       op0=ALU.mult, op1=ALU.subtract).then_inc(ktlo, 1)

                def q_lo(b, g):
                    dve.wait_ge(qthi, b * NKV + g + 1)
                    nc.vector.tensor_tensor(qT[g % 2][1][:], qbank[:, 0:GW], f32(qT[g % 2][0][:]), ALU.subtract).then_inc(qtlo, 1)

                def p_lo(b, g, h):
                    dve.wait_ge(pthi, b * NH + g * REP + h + 1)
                    nc.vector.tensor_tensor(pT[g % 2][1][:, :, h * L:(h + 1) * L],
                                            pbank[h % 2][0:CR, 0:NKT * L].rearrange("r (t l) -> r t l", t=NKT),
                                            f32(pT[g % 2][0][:, :, h * L:(h + 1) * L]), ALU.subtract).then_inc(ptlo, 1)

                def invert(b, g, pair):
                    n = b * NH + g * REP + 2 * pair
                    col = g * REP + 2 * pair
                    dve.wait_ge(exped, n + 2)
                    if not is_first(b):
                        dve.wait_ge(normed, n + 2 - NH)
                    nc.vector.reciprocal(ri[:, col:col + 2], rs[:, col:col + 2]).then_inc(inverted, 1)

                def step(b, par, k, g, h):
                    n = b * NH + g * REP + h
                    col = g * REP + h
                    dve.wait_ge(scored, n + 1)
                    nc.vector.tensor_reduce(mx[:, col:col + 1], sbank[h % 2][0:L, 0:NKEY], AX.X, ALU.max).then_inc(maxed, 1)
                    if h == 0 and exists(*back(b, g, 1)):
                        invert(*back(b, g, 1), 1)
                    if h == 2:
                        invert(b, g, 0)
                    dve.wait_ge(maxed, n + 1)
                    if not is_first(b):
                        dve.wait_ge(exped, n + 1 - NH)
                    nc.vector.tensor_scalar(nb[:, col:col + 1], mx[:, col:col + 1], c["rq"][:, bass.ds(g * B * REP + b * REP + h, 1)], -1.0, ALU.mult, ALU.mult).then_inc(biased, 1)
                    if exists(*back(b, g, 1)):
                        p_lo(*back(b, g, 1), h)
                    if h == 2 and not (is_last(b) and g == NKV - 1):
                        q_lo(*back(b, g, -1))

                def start():
                    for m in (*V[0], *V[1]):
                        nc.vector.memset(f32(m[96:CR, NCT, :]), 0.0).then_inc(pads, 1)
                    q_lo(0, 0)

                def tail():
                    invert(B - 1, NKV - 1, 1)
                    for h in range(REP):
                        p_lo(B - 1, NKV - 1, h)

                schedule(dve, start, step, piece, tail)

            @block.tensor
            def _(pe):
                def q_t(b, par, k, g):
                    pe.wait_ge(q_in[par], k * 16 + 16)
                    if not (is_first(b) and g == 0):
                        pe.wait_ge(qtlo, b * NKV + g)
                    for r in range(REP):
                        hh = g * REP + r
                        mm = nc.tensor.transpose(qbank[:, r * L:(r + 1) * L], q[par][:, hh * HD:(hh + 1) * HD], c["ident"][0:L, 0:L])
                    mm.then_inc(qtr, 1)

                def bank_read(b, kind, t):
                    if kind == "k":
                        pe.wait_ge(kscaled, b * NCT + t + 1)
                    elif kind == "v":
                        pe.wait_ge(vlo, b * NCT + t + 1)
                    else:
                        pe.wait_ge(ktlo, b * NKT + T_ORDER.index(t) + 1)

                def piece(b, par, kind, t):
                    if kind == "c":
                        return
                    use = users.index((kind, t))
                    bank = bank_of((kind, t))
                    if use >= 2:
                        bank_read(b, *users[use - 2])
                    elif not is_first(b):
                        bank_read(b - 1, *users[use - 2])
                    if kind in "kv":
                        pe.wait_ge(ctlo, b * NCT + t + 1)
                        i = 0 if kind == "k" else 1
                        for kt in range(KT):
                            mm = mm3(nc, bank[0:CR, :], ct[t][0][:, kt, :], ct[t][1][:, kt, :],
                                     wch[:, kt, i, :], wcl[:, kt, i, :], kt == 0, kt == KT - 1)
                        mm.then_inc(kproj if kind == "k" else vproj, 1)
                    else:
                        n = L if t == NCT else CR
                        if t == NCT:
                            pe.wait_ge(kself_in, b * 16 + 16)
                        else:
                            pe.wait_ge(kscaled, b * NCT + t + 1)
                        for h in range(NKV):
                            mm = nc.tensor.transpose(bank[:, h * CR:h * CR + n], ktok[0:n, t, h, :], c["ident"][0:n, 0:n])
                        mm.then_inc(ktr, 1)

                def p_t(b, g, h):
                    n = b * NH + g * REP + h
                    p = Pm[(g % 2) * REP + h]
                    pe.wait_ge(normed, n + 1)
                    if not (is_first(b) and g == 0 and h < 2):
                        pe.wait_ge(ptlo, n - 1)
                    for t in range(NKT):
                        mm = nc.tensor.transpose(pbank[h % 2][0:CR, t * L:(t + 1) * L], p[:, t * CR:(t + 1) * CR], c["ident"][0:L, 0:L])
                    mm.then_inc(ptr, 1)

                def pv_part(b, par, g, t):
                    n = b * NKV + g
                    if t == 0:
                        pe.wait_ge(ptlo, (n + 1) * REP)
                        if not (is_first(b) and g == 0):
                            pe.wait_ge(oev, n)
                    mm = mm3(nc, obank[:, 0:GW], V[par][0][:, t, g * HD:(g + 1) * HD], V[par][1][:, t, g * HD:(g + 1) * HD],
                             pT[g % 2][0][:, t, :], pT[g % 2][1][:, t, :], t == 0, t == NKT - 1)
                    if t == NKT - 1:
                        mm.then_inc(pv, 1)

                def step(b, par, k, g, h):
                    n = b * NH + g * REP + h
                    if h == 0:
                        pe.wait_ge(qtlo, b * NKV + g + 1)
                        if g == 0:
                            pe.wait_ge(ktlo, b * NKT + NKT)
                            pe.wait_ge(vlo, b * NCT + NCT)
                            pe.wait_ge(vslo, b + 1)
                    if not (is_first(b) and g == 0 and h < 2):
                        pe.wait_ge(exped, n - 1)
                    cols = slice(h * L, (h + 1) * L)
                    bank = sbank[h % 2]
                    mm3(nc, bank[0:L, 0:NSC], qT[g % 2][0][:, cols], qT[g % 2][1][:, cols],
                        kT[par][0][:, g, :], kT[par][1][:, g, :], True, False)
                    nc.tensor.matmul(bank[0:L, MO:NSC], c["identr"][0:L, 0:L], mask[:], start=False, stop=True).then_inc(scored, 1)
                    if h == 0 and exists(*back(b, g, 1)):
                        p_t(*back(b, g, 1), h)
                    if exists(*back(b, g, 2)):
                        vb, vg = back(b, g, 2)
                        pv_part(vb, par if g >= 2 else 1 - par, vg, h)
                    if h and exists(*back(b, g, 1)):
                        p_t(*back(b, g, 1), h)
                    if h == 1 and g < NKV - 1:
                        q_t(b, par, k, g + 1)
                    elif h == 1 and not is_last(b):
                        q_t(b + 1, 1 - par, k + par, 0)

                def start():
                    pe.wait_ge(mask_set, 1)
                    pe.wait_ge(pads, 2 * REP + 8)
                    q_t(0, 0, 0, 0)

                def tail():
                    for h in range(REP):
                        pv_part(B - 1, 1, NKV - 2, h)
                        p_t(B - 1, NKV - 1, h)
                    for t in range(NKT):
                        pv_part(B - 1, 1, NKV - 1, t)

                schedule(pe, start, step, piece, tail)


def load_up(sp, io, up, g, j):
    w = TB if j < NFT else TW
    sp.dma_start(up["raw"][j % RING][:, 0:w],
                 io["w13"][at(g, 1), :, j * TB:j * TB + w].rearrange("a p n -> (a p) n")).then_inc(up["in"][j % RING], 16)


def load_down(sp, io, down, g):
    sp.dma_start(down["raw"][:, 0:NFT, :], io["w2"][at(g, 1), :, :, :].rearrange("a p j d -> (a p) j d")).then_inc(down["in"], 16)
    sp.dma_start(down["raw"][0:TAIL, NFT, :], io["w2t"][at(g, 1), :, :].rearrange("a p d -> (a p) d")).then_inc(down["in"], 16)


def out_projection(nc, io, scratch, banks, c, x1, x2h, x2l, wo, up, down):
    with ExitStack() as ctx:
        def sb(name, shape, dt=F32):
            return ctx.enter_context(nc.sbuf_tensor(name, shape, dt))

        def sem(name):
            return ctx.enter_context(nc.semaphore(name))

        waited = sem("waited")

        NW = NWO
        HW = NH // NW
        woh, wol = sb("wo_hi", [128, NH, DM], F32R), sb("wo_lo", [128, NH, DM], F32R)
        wraw = [wo["raw"], sb("wo_raw1", [128, HW, DM])]
        oraw = [sb(f"o_raw{i}", [128, NH * L]) for i in range(2)]
        oh = [sb(f"o_hi{i}", [128, NH * L], F32R) for i in range(2)]
        ol = [sb(f"o_lo{i}", [128, NH * L], F32R) for i in range(2)]
        x = [sb(f"x_in{i}", [L, DM]) for i in range(2)]
        st, mv, ve, rstd = sb("st2", [L, 6]), sb("mv2", [L, 2]), sb("ve2", [L, 1]), sb("rstd2", [L, 1])
        xn = sb("xn2", [L, DM])

        w_in = [wo["in"], sem("wo_in1")]
        first_in = [sem(f"first_o_in{n}") for n in range(NW)]
        fhi, flo = sem("first_o_his"), sem("first_o_los")
        o_in, x_in = ([sem(f"{n}{i}") for i in range(2)] for n in ("o_in", "x_ins"))
        whi, wlo, ohi, olo = sem("wo_his"), sem("wo_los"), sem("o_his"), sem("o_los")
        proj, x1_set, ln_st, ln_mv, ln_ve, ln_r, ln_x = (sem(n) for n in (
            "o_proj", "x1_set", "ln2_st", "ln2_mv", "ln2_ve", "ln2_r", "ln2_x"))
        t_done, th, tl = sem("x2_psum"), sem("x2_his"), sem("x2_los")
        ybank, tbank = banks[0:2], banks[2]

        def over_steps(eng, step):
            with eng.Fori(1, B // 2 - 1) as i:
                step(i * 2, 0, i)
                step(i * 2 + 1, 1, i)
            for n in range(B - 2, B + 2):
                step(n, n % 2, n // 2)

        def has(n, back):
            return not isinstance(n, int) or 0 <= n - back < B

        with nc.Block() as block:
            @block.sync
            def _(sp):
                def load_x(b, par):
                    if not is_first(b, 2):
                        sp.wait_ge(x1_set, b - 1)
                    sp.dma_start(x[par][:], io["x"][at(b, 1), :, :].rearrange("a l d -> (a l) d")).then_inc(x_in[par], 16)

                def load(b, par):
                    if is_first(b, 4):
                        sp.wait_ge(flo, 2 * NW)
                    else:
                        sp.wait_ge(olo, b - 3)
                    sp.dma_start(oraw[par][:], scratch["o"][at(b, 1), :, :].rearrange("a p n -> (a p) n")).then_inc(o_in[par], 16)
                    load_x(b, par)

                for n in range(NW):
                    if n >= 2:
                        sp.wait_ge(wlo, n - 1)
                    if n:
                        sp.dma_start(wraw[n % 2][:], io["wo"][:, n * HW:(n + 1) * HW, :]).then_inc(w_in[n % 2], 16)
                    cols = slice(n * HW * L, (n + 1) * HW * L)
                    for b in range(2):
                        sp.dma_start(oraw[b][:, cols], scratch["o"][b][:, cols]).then_inc(first_in[n], 16)
                for b in range(2):
                    load_x(b, b)
                for b in range(2, 4):
                    load(b, b % 2)
                with sp.Fori(2, B // 2) as i:
                    load(i * 2, 0)
                    load(i * 2 + 1, 1)
                for j in range(RING):
                    load_up(sp, io, up, 0, j)
                load_down(sp, io, down, 0)

            @block.gpsimd
            def _(pool):
                def batch(b):
                    pool.wait_ge(ln_mv, b + 1)
                    pool.sem_inc(waited, 1)
                    nc.gpsimd.tensor_scalar(ve[:], mv[:, 1:2], 1.0, EPS_LN, ALU.mult, ALU.add).then_inc(ln_ve, 1)
                    pool.wait_ge(ln_ve, b + 1)
                    nc.gpsimd.tensor_tensor(rstd[:], ve[:], c["neghalf"][0:L, 0:1], ALU.pow).then_inc(ln_r, 1)

                with pool.Fori(0, B) as b:
                    batch(b)

            @block.scalar
            def _(act):
                def o_hi(b, par, k):
                    act.wait_ge(o_in[par], k * 16)
                    act.wait_ge(proj, b - 1)
                    nc.scalar.activation(oh[par][:], oraw[par][:], ACT.Copy).then_inc(ohi, 1)

                for n in range(NW):
                    act.wait_ge(w_in[n % 2], 16 * (n // 2 + 1))
                    nc.scalar.activation(woh[:, n * HW:(n + 1) * HW, :], wraw[n % 2][:], ACT.Copy).then_inc(whi, 1)
                    cols = slice(n * HW * L, (n + 1) * HW * L)
                    act.wait_ge(first_in[n], 32)
                    for b in range(2):
                        nc.scalar.activation(oh[b][:, cols], oraw[b][:, cols], ACT.Copy).then_inc(fhi, 1)
                o_hi(2, 0, 1)

                def step(n, par, k):
                    if has(n, -1):
                        o_hi(n + 1, 1 - par, k + par)
                    act.wait_ge(t_done, n - 1)
                    nc.scalar.activation(x2h[:, :, at(n - 2, L)], tbank[:, 0:KT * L].rearrange("p (k l) -> p k l", k=KT), ACT.Copy).then_inc(th, 1)

                over_steps(act, step)

            @block.vector
            def _(dve):
                def o_lo(b, par):
                    dve.wait_ge(ohi, b - 1)
                    dve.wait_ge(proj, b - 1)
                    nc.vector.tensor_tensor(ol[par][:], oraw[par][:], f32(oh[par][:]), ALU.subtract).then_inc(olo, 1)

                for n in range(NW):
                    dve.wait_ge(whi, n + 1)
                    nc.vector.tensor_tensor(wol[:, n * HW:(n + 1) * HW, :], wraw[n % 2][:], f32(woh[:, n * HW:(n + 1) * HW, :]), ALU.subtract).then_inc(wlo, 1)
                    cols = slice(n * HW * L, (n + 1) * HW * L)
                    for b in range(2):
                        dve.wait_ge(fhi, n * 2 + b + 1)
                        nc.vector.tensor_tensor(ol[b][:, cols], oraw[b][:, cols], f32(oh[b][:, cols]), ALU.subtract).then_inc(flo, 1)

                def normalise(b, par, k):
                    x1b = x1[:, at(b, 1), :].rearrange("l a d -> l (a d)")
                    dve.wait_ge(proj, b + 1)
                    dve.wait_ge(x_in[par], k * 16 + 16)
                    nc.vector.scalar_tensor_tensor(out=x1b, in0=ybank[par][0:L, :], scalar=c["tanhg"][0:L, 0:1],
                                                   in1=x[par][:], op0=ALU.mult, op1=ALU.add).then_inc(x1_set, 1)
                    dve.wait_ge(x1_set, b + 1)
                    dve.sem_inc(waited, 1)
                    nc.vector.bn_stats(st[:], x1b).then_inc(ln_st, 1)
                    dve.wait_ge(ln_st, b + 1)
                    dve.sem_inc(waited, 1)
                    nc.vector.bn_aggr(mv[:], st[:]).then_inc(ln_mv, 1)
                    dve.wait_ge(ln_r, b + 1)
                    dve.wait_ge(ln_mv, b + 1)
                    if not is_first(b):
                        dve.wait_ge(t_done, b)
                    nc.vector.tensor_scalar(xn[:], x1b, mv[:, 0:1], rstd[:], ALU.subtract, ALU.mult).then_inc(ln_x, 1)

                def step(n, par, k):
                    if has(n, -1):
                        o_lo(n + 1, 1 - par)
                    if has(n, 1):
                        normalise(n - 1, 1 - par, k - 1 + par)
                    dve.wait_ge(th, n - 1)
                    nc.vector.tensor_tensor(x2l[:, :, at(n - 2, L)], tbank[:, 0:KT * L].rearrange("p (k l) -> p k l", k=KT),
                                            f32(x2h[:, :, at(n - 2, L)]), ALU.subtract).then_inc(tl, 1)

                normalise(0, 0, 0)
                o_lo(2, 0)
                over_steps(dve, step)

            @block.tensor
            def _(pe):
                def heads(b, par, first, last):
                    for h in range(first, last):
                        cols = slice(h * L, (h + 1) * L)
                        mm = mm3(nc, ybank[par][0:L, :], oh[par][:, cols], ol[par][:, cols], woh[:, h, :], wol[:, h, :], h == 0, h == NH - 1)
                    if last == NH:
                        mm.then_inc(proj, 1)

                def x2t(b):
                    pe.wait_ge(ln_x, b + 1)
                    if not is_first(b):
                        pe.wait_ge(tl, b)
                    for kt in range(KT):
                        mm = nc.tensor.transpose(tbank[:, kt * L:(kt + 1) * L], xn[:, kt * 128:(kt + 1) * 128], c["ident"][0:L, 0:L])
                    mm.then_inc(t_done, 1)

                for n in range(NW):
                    pe.wait_ge(wlo, n + 1)
                    for b in range(2):
                        pe.wait_ge(flo, n * 2 + b + 1)
                        heads(b, b, n * HW, (n + 1) * HW)

                def step(n, par, k):
                    if has(n, 0):
                        pe.wait_ge(olo, n - 1)
                        pe.wait_ge(x1_set, n - 1)
                        heads(n, par, 0, NH)
                    x2t(n - 2)

                over_steps(pe, step)


def experts(nc, io, out, banks, c, x1, x2h, x2l, spare, up, down):
    with ExitStack() as ctx:
        def sb(name, shape, dt=F32):
            return ctx.enter_context(nc.sbuf_tensor(name, shape, dt))

        def sem(name):
            return ctx.enter_context(nc.semaphore(name))

        waited = sem("waited")

        assert NJ % RING == 0
        praw, up_in, draw, down_in = up["raw"], up["in"], down["raw"], down["in"]
        uph = [sb(f"up_hi{i}", [128, KT, 256], F32R) for i in range(2)]
        upl = [sb(f"up_lo{i}", [128, KT, 256], F32R) for i in range(2)]
        dh, dl = sb("down_hi", [128, NJ, DM], F32R), sb("down_lo", [128, NJ, DM], F32R)
        uh, ul = sb("u_hi", [128, NJ, NT], F32R), sb("u_lo", [128, NJ, NT], F32R)
        sil = [spare[:, i, 0:HALF] for i in range(2)]
        tt = [spare[:, 2 + i, 0:HALF] for i in range(2)]
        uf = [sb(f"u_f32_{i}", [128, HALF]) for i in range(2)]
        y = sb("y_t", [128, KT, NT])
        ob = [draw[0:L, i, :] for i in range(2)]
        gwraw = sb("gate_raw", [128, KT, E])
        gwh, gwl = sb("gate_hi", [128, KT, 128], F32R), sb("gate_lo", [128, KT, 128], F32R)
        bias = sb("router_bias", [L, B, E])
        lt = y[0:E, 0, :]
        sc, se, eq, pk = (sb(n, [L, B, E]) for n in ("scores", "select", "equal", "picked"))
        one1, rev, got = sb("first_pick", [L, B, E]), sb("reverse_index", [L, B, E]), sb("chosen", [L, B, E])
        rd, ws = sb("reduced", [L, B]), sb("weight_sum", [L, B])
        gf = sb("gates_f32", [L, B, E])
        ghr = sb("gates_hi", [L, B, E], F32R)
        gg = sb("gates_grouped", [L, B, E // 2, 4])
        selraw, sel = sb("sel_raw", [4, NJ * 128]), sb("sel", [4, NJ * 128], F32R)
        gT = sb("gates_t", [4, NG - 1, NT], F32R)

        sm_in = sem("small_in")
        uphi, uplo, dhi, dlo = sem("up_his"), sem("up_los"), sem("down_his"), sem("down_los")
        zeroed, gwhi, gwlo, sels = sem("zeroed"), sem("gate_w_hi"), sem("gate_w_lo"), sem("sel_set")
        lgt, ltc, ltr, chain = sem("logits"), sem("logits_copied"), sem("logits_back"), sem("router_step")
        sigm, ggt, gtr, gtc = sem("sigmoid"), sem("gates_set"), sem("gates_turned"), sem("gates_t_set")
        h_done, sil_s, h_free, g_done, g_free = (sem(n) for n in ("h_done", "silu_s", "h_read", "gate_rows", "u_set"))
        uhi, ulo, d_done, y_set = sem("u_his"), sem("u_los"), sem("down_done"), sem("y_set")
        otr, oset, oout = sem("out_turned"), sem("out_set"), [sem(f"out_stored{i}") for i in range(2)]
        h1b, h3b, gb, yb = banks[0:2], banks[2:4], banks[4], banks[5:7]
        xb = banks[7]
        NGT = (NG - 1) * 2
        tb = (xb, gb)

        def raw(j):
            return praw[j % RING][:, 0:TB if j < NFT else TW].rearrange("p (k n) -> p k n", k=KT)

        def rows(j):
            return 128 if j < NFT else TAIL

        with nc.Block() as block:
            @block.sync
            def _(sp):
                sp.dma_start(gwraw[:], io["gate_wt"]).then_inc(sm_in, 16)
                sp.dma_start(selraw[:], io["c_sel"]).then_inc(sm_in, 16)
                sp.dma_start(rev[:], io["c_rev"]).then_inc(sm_in, 16)
                for b in range(B):
                    sp.dma_start(bias[:, b, :], io["router_bias"].partition_broadcast(L)).then_inc(sm_in, 16)

                def group(g):
                    for j in range(RING if is_first(g) else 0, NJ):
                        sp.wait_ge(uplo, g * NJ + j + 1 - RING)
                        load_up(sp, io, up, g, j)
                        if j == 1:
                            sp.wait_ge(dlo, g)
                            load_down(sp, io, down, g)

                group(0)
                with sp.Fori(1, NG) as g:
                    group(g)
                for b in range(B):
                    sp.wait_ge(oset, b + 1)
                    sp.dma_start(out[b], ob[b % 2]).then_inc(oout[b % 2], 16)
                for i in range(2):
                    sp.wait_ge(oout[i], 16 * B // 2)

            @block.gpsimd
            def _(pool):
                nc.gpsimd.memset(f32(gwh[:]), 0.0).then_inc(zeroed, 1)
                nc.gpsimd.memset(f32(gwl[:]), 0.0).then_inc(zeroed, 1)
                pool.wait_ge(zeroed, 2)
                pool.wait_ge(sm_in, (3 + B) * 16)
                pool.sem_inc(waited, 1)
                nc.gpsimd.tensor_scalar(gwh[:, :, 0:E], gwraw[:], 1.0, 1.0, ALU.mult, ALU.mult).then_inc(gwhi, 1)
                pool.wait_ge(gwhi, 1)
                nc.gpsimd.tensor_tensor(gwl[:, :, 0:E], gwraw[:], f32(gwh[:, :, 0:E]), ALU.subtract).then_inc(gwlo, 1)
                nc.gpsimd.tensor_scalar(sel[:], selraw[:], 1.0, 1.0, ALU.mult, ALU.mult).then_inc(sels, 1)

                def group(g):
                    pool.wait_ge(down_in, g * 32 + 32)
                    if not (isinstance(g, int) and g == 0):
                        pool.wait_ge(d_done, g * 2 * KT)
                    for part in (slice(0, NFT), slice(NFT, NJ)):
                        r = 128 if part.start == 0 else TAIL
                        pool.sem_inc(waited, 1)
                        nc.gpsimd.tensor_scalar(dh[0:r, part, :], draw[0:r, part, :], 1.0, 1.0, ALU.mult, ALU.mult).then_inc(dhi, 1)
                    pool.wait_ge(dhi, g * 2 + 2)
                    for part in (slice(0, NFT), slice(NFT, NJ)):
                        r = 128 if part.start == 0 else TAIL
                        op = nc.gpsimd.tensor_tensor(dl[0:r, part, :], draw[0:r, part, :], f32(dh[0:r, part, :]), ALU.subtract)
                    op.then_inc(dlo, 1)
                    for j in range(NJ):
                        for s in range(2):
                            n = (g * NJ + j) * 2 + s
                            pool.wait_ge(g_free, n + 1)
                            r = rows(j)
                            cols = slice(s * HALF, (s + 1) * HALF)
                            pool.sem_inc(waited, 1)
                            nc.gpsimd.tensor_scalar(uh[0:r, j, cols], uf[s][0:r, :], 1.0, 1.0, ALU.mult, ALU.mult).then_inc(uhi, 1)
                            pool.wait_ge(uhi, n + 1)
                            nc.gpsimd.tensor_tensor(ul[0:r, j, cols], uf[s][0:r, :], f32(uh[0:r, j, cols]), ALU.subtract).then_inc(ulo, 1)

                group(0)
                with pool.Fori(1, NG) as g:
                    group(g)

            @block.scalar
            def _(act):
                def split(g, j):
                    w = 256 if j < NFT else 2 * TAIL
                    n = g * NJ + j
                    act.wait_ge(up_in[j % RING], (g * (NJ // RING) + j // RING + 1) * 16)
                    if not (isinstance(g, int) and g == 0 and j < 2):
                        act.wait_ge(h_done, (n - 1) * 2)
                    nc.scalar.activation(uph[j % 2][:, :, 0:w], raw(j), ACT.Copy).then_inc(uphi, 1)

                split(0, 0)

                def group(g):
                    for j in range(NJ):
                        if j + 1 < NJ:
                            split(g, j + 1)
                        elif not (isinstance(g, int) and g == NG - 1):
                            split(g + 1, 0)
                        if is_first(g) and j == 1:
                            act.wait_ge(lgt, 2)
                            for s in range(2):
                                nc.scalar.activation(lt[:, s * HALF:(s + 1) * HALF], tb[s][0:E, 0:HALF], ACT.Copy).then_inc(ltc, 1)
                        if is_first(g) and j == 2:
                            act.wait_ge(ltr, 1)
                            nc.scalar.activation(sc[:], xb[0:L, 0:B * E].rearrange("l (b e) -> l b e", b=B), ACT.Sigmoid).then_inc(sigm, 1)
                        for s in range(2):
                            n = (g * NJ + j) * 2 + s
                            act.wait_ge(h_done, n + 1)
                            if not (isinstance(g, int) and g == 0 and j == 0):
                                act.wait_ge(h_free, n - 1)
                            if j < NFT:
                                nc.scalar.activation(sil[s], h1b[s][:, 0:HALF], ACT.Silu).then_inc(sil_s, 1)
                            else:
                                nc.scalar.activation(sil[s][128 - TAIL:, :], h1b[s][0:TAIL, 0:HALF], ACT.Silu).then_inc(sil_s, 1)

                group(0)
                with act.Fori(1, NG - 1) as g:
                    group(g)
                group(NG - 1)

            @block.vector
            def _(dve):
                def split(g, j):
                    w = 256 if j < NFT else 2 * TAIL
                    n = g * NJ + j
                    dve.wait_ge(uphi, n + 1)
                    nc.vector.tensor_tensor(upl[j % 2][:, :, 0:w], raw(j), f32(uph[j % 2][:, :, 0:w]), ALU.subtract).then_inc(uplo, 1)

                count = [0]

                def router(part):
                    def then(op):
                        op.then_inc(chain, 1)
                        count[0] += 1
                        dve.wait_ge(chain, count[0])

                    def over_e(r):
                        return r[:].unsqueeze(2).broadcast_to([L, B, E])

                    V = nc.vector
                    if part == 0:
                        dve.wait_ge(sigm, 1)
                        dve.wait_ge(sm_in, (3 + B) * 16)
                        then(V.tensor_tensor(se[:], sc[:], bias[:], ALU.add))
                    if part < 2:
                        then(V.tensor_reduce(rd[:], se[:], AX.X, ALU.max))
                        then(V.tensor_tensor(eq[:], se[:], over_e(rd), ALU.is_equal))
                        then(V.tensor_tensor(pk[:], eq[:], rev[:], ALU.mult))
                        then(V.tensor_reduce(rd[:], pk[:], AX.X, ALU.max))
                        then(V.tensor_tensor(got[:] if part else one1[:], pk[:], over_e(rd), ALU.is_equal))
                    if part == 0:
                        then(V.scalar_tensor_tensor(out=se[:], in0=one1[:], scalar=-1e30, in1=se[:], op0=ALU.mult, op1=ALU.add))
                    if part == 1:
                        then(V.tensor_tensor(got[:], got[:], one1[:], ALU.add))
                    if part == 2:
                        then(V.tensor_tensor(gf[:], got[:], sc[:], ALU.mult))
                        then(V.tensor_reduce(ws[:], gf[:], AX.X, ALU.add))
                        then(V.tensor_scalar(ws[:], ws[:], 1e-12, None, ALU.max))
                        then(V.reciprocal(ws[:], ws[:]))
                    if part == 3:
                        then(V.tensor_tensor(gf[:], gf[:], over_e(ws), ALU.mult))
                        then(V.tensor_copy(ghr[:], gf[:]))
                        then(V.tensor_copy(gg[:, :, :, 0:2], f32(ghr[:]).rearrange("l b (g e) -> l b g e", e=2)))
                        V.tensor_tensor(gg[:, :, :, 2:4], gf[:].rearrange("l b (g e) -> l b g e", e=2),
                                        gg[:, :, :, 0:2], ALU.subtract).then_inc(ggt, 1)

                def group(g):
                    first = is_first(g)
                    for j in range(NJ):
                        if j + 1 < NJ:
                            split(g, j + 1)
                        elif not (isinstance(g, int) and g == NG - 1):
                            split(g + 1, 0)
                        if first and j >= 2:
                            router(j - 2)
                        for s in range(2):
                            n = (g * NJ + j) * 2 + s
                            a = 0 if j < NFT else 128 - TAIL
                            r = rows(j)
                            src = (h3b[s] if j < NFT else h1b[s])[a:, 0:HALF]
                            dve.wait_ge(sil_s, n + 1)
                            if first:
                                if j:
                                    dve.wait_ge(ulo, n - 1)
                                nc.vector.tensor_tensor(uf[s][0:r, :], src, sil[s][a:, :], ALU.mult).then_inc(h_free, 1)
                                dve.wait_ge(h_free, n + 1)
                                dve.sem_inc(g_free, 1)
                                continue
                            nc.vector.tensor_tensor(tt[s][a:, :], src, sil[s][a:, :], ALU.mult).then_inc(h_free, 1)
                            dve.wait_ge(h_free, n + 1)
                            dve.wait_ge(g_done, n + 1 - 2 * NJ)
                            dve.wait_ge(ulo, n - 1)
                            nc.vector.tensor_tensor(uf[s][0:r, :], tt[s][a:, :], gb[a:, 0:HALF], ALU.mult).then_inc(g_free, 1)
                    for s in range(2):
                        for d in range(KT):
                            n = g * 2 * KT + s * KT + d
                            dve.wait_ge(d_done, n + 1)
                            dst = y[:, d, s * HALF:(s + 1) * HALF]
                            src = yb[d % 2][:, 0:HALF]
                            if first:
                                nc.vector.tensor_copy(dst, src).then_inc(y_set, 1)
                                for i in range(n * 2, min(n * 2 + 2, NGT)):
                                    dve.wait_ge(gtr, i + 1)
                                    nc.vector.tensor_copy(gT[:, i // 2, (i % 2) * HALF:(i % 2 + 1) * HALF], tb[i % 2][0:4, 0:HALF]).then_inc(gtc, 1)
                            else:
                                dve.wait_ge(y_set, n + 1 - 2 * KT)
                                nc.vector.tensor_tensor(dst, dst, src, ALU.add).then_inc(y_set, 1)

                split(0, 0)
                group(0)
                with dve.Fori(1, NG - 1) as g:
                    group(g)
                group(NG - 1)
                for b in range(B):
                    dve.wait_ge(otr, b + 1)
                    if b >= 2:
                        dve.wait_ge(oout[b % 2], 16 * (b // 2))
                    nc.vector.scalar_tensor_tensor(out=ob[b % 2], in0=yb[b % 2][0:L, :], scalar=c["tanhg"][0:L, 1:2],
                                                   in1=x1[:, b, :], op0=ALU.mult, op1=ALU.add).then_inc(oset, 1)

            @block.tensor
            def _(pe):
                def logits():
                    pe.wait_ge(gwlo, 1)
                    for s in range(2):
                        cols = slice(s * HALF, (s + 1) * HALF)
                        for kt in range(KT):
                            mm = mm3(nc, tb[s][:, 0:HALF], gwh[:, kt, :], gwl[:, kt, :], x2h[:, kt, cols], x2l[:, kt, cols],
                                     kt == 0, kt == KT - 1)
                        mm.then_inc(lgt, 1)

                def turn_logits():
                    pe.wait_ge(ltc, 2)
                    for b in range(B):
                        mm = nc.tensor.transpose(xb[0:L, b * E:(b + 1) * E], lt[:, b * L:(b + 1) * L], c["ident"][0:E, 0:E])
                    mm.then_inc(ltr, 1)

                def turn_gates(n):
                    if n < 2:
                        pe.wait_ge(ggt, 1)
                    else:
                        pe.wait_ge(gtc, n - 1)
                    for i in range(B // 2):
                        b = (n % 2) * (B // 2) + i
                        mm = nc.tensor.transpose(tb[n % 2][0:4, i * L:(i + 1) * L], gg[:, b, n // 2, :], c["ident"][0:L, 0:L])
                    mm.then_inc(gtr, 1)

                def group(g):
                    first = is_first(g)
                    for j in range(NJ):
                        pe.wait_ge(uplo, g * NJ + j + 1)
                        wh, wl = uph[j % 2], upl[j % 2]
                        for s in range(2):
                            n = (g * NJ + j) * 2 + s
                            cols = slice(s * HALF, (s + 1) * HALF)
                            if not (first and j == 0):
                                pe.wait_ge(h_free, n - 1)
                            for i, bank in enumerate((h1b[s], h3b[s]) if j < NFT else (h1b[s],)):
                                ws = slice(i * 128, (i + 1) * 128)
                                for kt in range(KT):
                                    mm = mm3(nc, bank[:, 0:HALF], wh[:, kt, ws], wl[:, kt, ws],
                                             x2h[:, kt, cols], x2l[:, kt, cols], kt == 0, kt == KT - 1)
                            mm.then_inc(h_done, 1)
                            if first:
                                continue
                            pe.wait_ge(g_free, n)
                            pe.sem_inc(waited, 1)
                            nc.tensor.matmul(gb[:, 0:HALF], sel[:, j * 128:(j + 1) * 128],
                                             gT[:, at(g - 1, 1), cols].rearrange("e a n -> e (a n)"), start=True, stop=True).then_inc(g_done, 1)
                        if first and j == 0:
                            logits()
                        if first and j == 1:
                            turn_logits()
                    pe.wait_ge(dlo, g + 1)
                    for s in range(2):
                        cols = slice(s * HALF, (s + 1) * HALF)
                        pe.wait_ge(ulo, (g + 1) * 2 * NJ - 2 + s)
                        for d in range(KT):
                            n = g * 2 * KT + s * KT + d
                            if not (first and s == 0 and d < 2):
                                pe.wait_ge(y_set, n - 1)
                            for j in range(NJ):
                                if j == NJ - 1 and d == 0:
                                    pe.wait_ge(ulo, (g + 1) * 2 * NJ - 1 + s)
                                r = rows(j)
                                dc = slice(d * 128, (d + 1) * 128)
                                mm = mm3(nc, yb[d % 2][:, 0:HALF], dh[0:r, j, dc], dl[0:r, j, dc],
                                         uh[0:r, j, cols], ul[0:r, j, cols], j == 0, j == NJ - 1)
                            mm.then_inc(d_done, 1)
                            if first:
                                for i in range(n * 2, min(n * 2 + 2, NGT)):
                                    turn_gates(i)
                    if first:
                        pe.wait_ge(gtc, NGT)
                        pe.wait_ge(sels, 1)

                group(0)
                with pe.Fori(1, NG) as g:
                    group(g)
                for b in range(B):
                    if b < 2:
                        pe.wait_ge(y_set, NG * 2 * KT)
                    else:
                        pe.wait_ge(oset, b - 1)
                    for d in range(KT):
                        mm = nc.tensor.transpose(yb[b % 2][0:L, d * 128:(d + 1) * 128], y[:, d, b * L:(b + 1) * L], c["ident"][:])
                    mm.then_inc(otr, 1)


def kernel(**inputs):
    import numpy as _np
    import concourse.bacc as _bacc
    from concourse import mybir as _mybir
    from concourse.bass_utils import run_bass_kernel_spmd as _run

    a = {n: _np.asarray(v) for n, v in inputs.items()}
    p = "L0_xattn_"
    f = "L0_ffn_"

    def rows_first(w):
        return w.reshape(w.shape[0] // 128, 128, w.shape[1]).transpose(1, 0, 2)

    def groups(w, shared):
        return _np.concatenate([shared[None], w.reshape(E // 2, 2, DM, INTER).transpose(0, 2, 1, 3).reshape(E // 2, DM, GH)])

    w1 = groups(a[f + "W1"], a[f + "sw1"].T).reshape(NG, KT, 128, GH).transpose(0, 2, 1, 3)
    w3 = groups(a[f + "W3"], a[f + "sw3"].T).reshape(NG, KT, 128, GH).transpose(0, 2, 1, 3)
    tiles = []
    for j in range(NFT + 1):
        cols = slice(j * 128, min((j + 1) * 128, GH))
        tiles.append(_np.concatenate([w1[..., cols], w3[..., cols]], -1).reshape(NG, 128, -1))
    w2 = _np.concatenate([a[f + "sw2"].T[None], a[f + "W2"].reshape(E // 2, GH, DM)])
    arrays = {
        "x": a["x"],
        "ctxt": a["ctx_2048"].transpose(0, 2, 1).reshape(B, KT, 128, T).transpose(0, 2, 1, 3),
        "g_xattn": a["g_xattn"], "g_ffn": a["g_ffn"],
        "wqkv": rows_first(_np.concatenate([a[p + n] for n in ("wk", "wq", "wv", "wk_ctx", "wv_ctx")], 1))
                .reshape(128, KT, NQ + 4, 512).transpose(2, 0, 1, 3),
        "wo": rows_first(a[p + "wo"]),
        "qn": a[p + "q_norm_w"], "kn": a[p + "k_norm_w"],
        "gate_wt": rows_first(a[f + "gate_w"].T),
        "router_bias": a[f + "router_bias"],
        "w13": _np.concatenate(tiles, -1),
        "w2": w2[:, :NFT * 128].reshape(NG, NFT, 128, DM).transpose(0, 2, 1, 3),
        "w2t": w2[:, NFT * 128:],
        **constants(),
    }
    nc = _bacc.Bacc("TRN2", target_bir_lowering=False, num_devices=1)
    launch, io = {}, {}
    for name, v in arrays.items():
        launch[f"in_{name}"] = _np.ascontiguousarray(v)
        io[name] = nc.dram_tensor(f"in_{name}", v.shape, _mybir.dt.float32, kind="ExternalInput").ap()
    out = nc.dram_tensor("out", (B, L, DM), _mybir.dt.float32, kind="ExternalOutput").ap()
    build(nc, io, out)
    r = _run(nc, [launch], core_ids=[0])
    return r.results[0]["out"]
```

```python
from contextlib import ExitStack

import numpy as np

import concourse.bass as bass
from concourse import mybir

F32 = mybir.dt.float32
F32R = mybir.dt.float32r
I32 = mybir.dt.int32
ALU = mybir.AluOpType
ACT = mybir.ActivationFunctionType
AX = mybir.AxisListType

B, L, DM = 8, 112, 512
T = 375
NH, NKV, HD = 16, 4, 128
REP = NH // NKV
KT = DM // 128
CR = 125
NCT = T // CR
NKT = NCT + 1
NKEY = T + L
NSC = NKEY + NKEY % 2
MO = T - T % 2
MW = NSC - MO
NPAD = NKT * CR
QW, KW = NH * HD, NKV * HD
GW = REP * L
NQ = QW // 512
E, INTER, TOPK = 8, 352, 2
GH = 2 * INTER
NFT = GH // 128
TAIL = GH - NFT * 128
NT = B * L
HALF = NT // 2
NTT = NT // 128
NWO = 4
NJ = NFT + 1
TB = KT * 256
TW = KT * 2 * TAIL
RING = 3
SLOTS = 256
NBLK = (NT * TOPK + E * (SLOTS - 1)) // SLOTS
TILES = SLOTS // 128
NTILE = NBLK * TILES
EJ = -(-INTER // 128)
EW1 = 2 * INTER
EW = KT * EW1 + EJ * DM
EPS_LN, EPS_RMS = 1e-5, 1e-6
THETA = 10000.0
MASKED = -1e30


def constants():
    inv = 1.0 / THETA ** (np.arange(0, HD, 2, dtype=np.float32) / np.float32(HD))
    freqs = np.outer(np.arange(L, dtype=np.float32), inv.astype(np.float32)).astype(np.float32)
    emb = np.concatenate([freqs, freqs], -1)
    cos, sin = np.cos(emb).astype(np.float32), np.sin(emb).astype(np.float32)
    sin[:, :HD // 2] *= -1.0

    def token_tiles(rows):
        return np.ascontiguousarray(np.tile(rows, (B, 1)).reshape(NTT, 128, HD).transpose(1, 0, 2))

    mask = np.zeros((L, MW), np.float32)
    mask[:, T - MO:T - MO + L] = np.where(np.arange(L)[None, :] > np.arange(L)[:, None], MASKED, 0.0)
    return {
        "c_ident": np.eye(128, dtype=np.float32),
        "c_cos": token_tiles(cos),
        "c_sin": token_tiles(sin),
        "c_mask": mask,
        "c_token": np.ascontiguousarray(np.arange(NT, dtype=np.float32).reshape(B, L).T),
        "c_before": np.triu(np.ones((L, L), np.float32), 1),
        "c_block": np.ascontiguousarray(np.broadcast_to(np.arange(NBLK, dtype=np.float32), (128, NBLK))),
        "c_row": np.arange(128, dtype=np.float32).reshape(128, 1),
        "c_rev": np.ascontiguousarray(np.broadcast_to(np.arange(E, 0, -1, dtype=np.float32), (L, B, E))),
    }


def at(b, n):
    return bass.ds(b * n, n)


def over_batches(eng, body):
    body(0, 0, 0)
    with eng.Fori(0, (B - 2) // 2) as i:
        body(i * 2 + 1, 1, i)
        body(i * 2 + 2, 0, i + 1)
    body(B - 1, 1, (B - 2) // 2)


def is_first(b, n=1):
    return isinstance(b, int) and b < n


def is_last(b):
    return isinstance(b, int) and b == B - 1


def f32(ap):
    return ap.bitcast(F32)


def build(nc, io, out):
    with ExitStack() as ctx:
        def dram(name, shape):
            return nc.dram_tensor(name, shape, F32).ap()

        def const_sb(name, shape, dt=F32):
            return ctx.enter_context(nc.sbuf_tensor(name, shape, dt))

        scratch = {
            "q": dram("q_roped", (NQ, NT, 512)),
            "k": dram("k_roped", (NT, KW)),
            "v": dram("v_self", (NT, KW)),
            "rq": dram("q_factors", (NQ, NT, REP)),
            "o": dram("attn_t", (B, 128, NH * L)),
            "x2": dram("x2_rows", (NT, DM)),
            "slots": dram("slot_table", (NBLK * SLOTS, 2)),
            "y": dram("expert_rows", (NBLK * SLOTS, DM)),
        }
        banks = [ctx.enter_context(nc.psum_tensor(f"bank{i}", [128, 512], F32)) for i in range(8)]
        c = {
            "ident": const_sb("ident", [128, 128]),
            "identr": const_sb("identr", [128, 128], F32R),
            "neghalf": const_sb("neghalf", [128, 4 * B]),
            "gates": const_sb("gates", [128, 2]),
            "tanhg": const_sb("tanhg", [128, 2]),
            "rq": const_sb("rq", [L, B * NH]),
            "wkn": const_sb("wkn", [HD, 1]),
        }
        wo = {"raw": const_sb("wo_raw0", [128, NH // NWO, DM]), "in": ctx.enter_context(nc.semaphore("wo_in0")),
              "o_out": [ctx.enter_context(nc.semaphore(f"o_stored{i}")) for i in range(2)]}
        with ExitStack() as attn:
            wch = attn.enter_context(nc.sbuf_tensor("wctx_hi", [128, KT, 2, KW], F32R))
            wcl = attn.enter_context(nc.sbuf_tensor("wctx_lo", [128, KT, 2, KW], F32R))
            tiles = {"raw": attn.enter_context(nc.sbuf_tensor("ctx_raw", [128, KT, T], F32))}
            tiles["parts"] = [[attn.enter_context(nc.sbuf_tensor(f"ctx_t_{m}{i}", [128, KT, CR], F32R)) for m in ("hi", "lo")]
                              for i in range(NCT)]
            for name in ("ctx_in", "ctx_his", "ctx_los"):
                tiles[name] = attn.enter_context(nc.semaphore(name))
            used, stored = self_projections(nc, io, scratch, banks, c, wch, wcl, tiles)
            attention(nc, io, scratch, banks, c, wch, wcl, tiles, wo, used, stored)
        x1 = const_sb("x1", [L, B, DM])
        routed = {
            "w0": const_sb("expert_raw0", [128, EW]),
            "table": const_sb("slots", [128, NTILE, 2]),
            "wrow": const_sb("weight_rows", [128, NBLK]),
            "widx": [const_sb(f"weight_index{i}", [128, 1], I32) for i in range(2)],
            "xidx": [const_sb(f"token_index{i}", [128, 1], I32) for i in range(2)],
            "slot": const_sb("slot_of", [L, TOPK, B], I32),
            "xg": [const_sb(f"x_rows{i}", [128, DM]) for i in range(2)],
            "w_in": [ctx.enter_context(nc.semaphore(f"expert_in{i}")) for i in range(2)],
            "x_in": [ctx.enter_context(nc.semaphore(f"rows_in{i}")) for i in range(2)],
            "x2_out": [ctx.enter_context(nc.semaphore(f"x2_stored{i}")) for i in range(2)],
        }
        with ExitStack() as dense:
            def dense_sb(name, shape, dt=F32):
                return dense.enter_context(nc.sbuf_tensor(name, shape, dt))

            x2h = dense_sb("x2t_hi", [128, KT, NT], F32R)
            x2l = dense_sb("x2t_lo", [128, KT, NT], F32R)
            up = {"raw": [dense_sb(f"up_raw{i}", [128, TB]) for i in range(RING)],
                  "in": [dense.enter_context(nc.semaphore(f"up_in{i}")) for i in range(RING)]}
            down = {"raw": dense_sb("down_raw", [128, NJ, DM]), "in": dense.enter_context(nc.semaphore("down_in"))}
            out_projection(nc, io, scratch, banks, c, x1, x2h, x2l, wo, up, down, routed)
            shared_pair(nc, io, scratch, banks, c, x1, x2h, x2l, wo["raw"], up, down, routed)
        experts(nc, io, scratch, out, banks, c, x1, routed)


def mm3(nc, out, wh, wl, xh, xl, start, stop):
    nc.tensor.matmul(out, wh, xh, start=start, stop=False)
    nc.tensor.matmul(out, wh, xl, start=False, stop=False)
    return nc.tensor.matmul(out, wl, xh, start=False, stop=stop)


def load_ctx(sp, io, tiles, b):
    sp.dma_start(tiles["raw"][:], io["ctxt"][at(b, 1), :, :, :].rearrange("a p k t -> (a p) k t")).then_inc(tiles["ctx_in"], 16)


def keep_busy(nc, c, bank, n):
    for _ in range(n):
        nc.tensor.matmul(bank[:], c["identr"][:], c["identr"][:].unsqueeze(1).broadcast_to([128, 4, 128]), start=True, stop=True)


def self_projections(nc, io, scratch, banks, c, wch, wcl, tiles):
    NCH = NQ + 2
    NPB = 4
    with ExitStack() as ctx:
        def sb(name, shape, dt=F32):
            return ctx.enter_context(nc.sbuf_tensor(name, shape, dt))

        used = []

        def sem(name):
            used.append(ctx.enter_context(nc.semaphore(name)))
            return used[-1]

        waited = sem("waited")

        x = sb("x_all", [128, NTT, DM])
        wraw = [sb(f"wraw{i}", [128, KT, 512]) for i in range(2)]
        wh = [sb(f"w_hi{i}", [128, KT, 512], F32R) for i in range(2)]
        wl = [sb(f"w_lo{i}", [128, KT, 512], F32R) for i in range(2)]
        st, mv = sb("ln_stats", [128, NTT, 6]), sb("ln_mv", [128, NTT, 2])
        ve, rstd = sb("ln_ve", [128, NTT]), sb("ln_rstd", [128, NTT])
        xn = [sb(f"xn{i}", [128, DM]) for i in range(2)]
        xh, xl = sb("xt_hi", [128, NTT, KT * 128], F32R), sb("xt_lo", [128, NTT, KT * 128], F32R)
        cos, sin = sb("cos", [128, NTT, HD]), sb("sin", [128, NTT, HD])
        wn = [sb(f"wn{i}", [128, HD]) for i in range(2)]
        tc = [sb(f"cosw{i}", [128, NTT, HD]) for i in range(2)]
        ts = [sb(f"sinw{i}", [128, NTT, HD]) for i in range(2)]
        sq = [sb(f"sq{i}", [128, 4, HD]) for i in range(2)]
        ra = [sb(f"rope_a{i}", [128, 4, HD]) for i in range(2)]
        rb = [sb(f"rope_b{i}", [128, 4, HD]) for i in range(2)]
        qo = [sb(f"q_out{i}", [128, 4, HD]) for i in range(2)]
        ko = [sb(f"k_out{i}", [128, 4, HD]) for i in range(2)]
        ss = [sb(f"sum_sq{i}", [128, NTT, 4]) for i in range(2)]
        ssr, ssk, rk = sb("q_ms", [128, NTT, 4]), sb("k_ms", [128, NTT, 4]), sb("rk", [128, NTT, 4])
        rq = [sb(f"rq{i}", [128, NTT, 4]) for i in range(2)]
        rq_out = sem("rq_stored")

        consts_in, ident_in, x_in = sem("consts_in"), sem("ident_in"), [sem(f"x_in_{t}") for t in range(NTT)]
        w_in = [sem(f"w_in{i}") for i in range(2)]
        whi, wlo, neg_set, idr, tabs = sem("w_his"), sem("w_los"), sem("neg_set"), sem("idr"), sem("tables")
        ln_st, ln_mv, ln_ve, ln_r, ln_x = sem("ln_st"), sem("ln_mvs"), sem("ln_ves"), sem("ln_rs"), sem("ln_x")
        t_done, th, tl = sem("xt_psum"), sem("xt_his"), sem("xt_los")
        proj, squared, summed, mul_a, mul_b = sem("proj"), sem("squared"), sem("summed"), sem("mul_a"), sem("mul_b")
        roped, k_ss, k_r, k_fin, v_fin = sem("roped"), sem("k_ss"), sem("k_r"), sem("k_fin"), sem("v_fin")
        rows_out = [sem(f"rows_stored{i}") for i in range(2)]
        sums_read = sem("sums_read")
        q_ss, q_r, tanh_s = sem("q_ss"), sem("q_r"), sem("tanh_s")
        cbank, tbank = banks[0:NPB], banks[NPB:NPB + 2]

        def over_chunks(body):
            def run(eng):
                body(0, 0, 0, "k")
                with eng.Fori(0, NQ // 2) as i:
                    body(i * 2 + 1, 1, i, "q")
                    body(i * 2 + 2, 0, i + 1, "q")
                body(NQ + 1, 1, NQ // 2, "v")
            return run

        def before(k, par, t):
            return k * NTT + (par * NTT + t) // 2

        def heads(ap):
            return ap.rearrange("l (a d) -> l a d", a=4)

        with nc.Block() as block:
            @block.sync
            def _(sp):
                def load_x(tiles):
                    for t in tiles:
                        sp.dma_start(x[:, t, :], io["x"].rearrange("b l d -> (b l) d")[t * 128:(t + 1) * 128]).then_inc(x_in[t], 16)

                def load(m, par):
                    sp.dma_start(wraw[par][:], io["wqkv"][at(m, 1), :, :, :].rearrange("a p k n -> (a p) k n")).then_inc(w_in[par], 16)

                load_x(range(2))
                sp.dma_start(c["ident"][:], io["c_ident"]).then_inc(ident_in, 16)
                load_x(range(2, 4))
                load(0, 0)
                load_x(range(4, NTT))
                sp.dma_start(cos[:], io["c_cos"]).then_inc(consts_in, 16)
                sp.dma_start(sin[:], io["c_sin"]).then_inc(consts_in, 16)
                for i, name in enumerate(("qn", "kn")):
                    sp.dma_start(wn[i][:], io[name].partition_broadcast(128)).then_inc(consts_in, 16)
                load(1, 1)
                sp.dma_start(c["wkn"][:], io["kn"].rearrange("(p a) -> p a", a=1)).then_inc(consts_in, 16)
                for i, name in enumerate(("g_xattn", "g_ffn")):
                    sp.dma_start(c["gates"][:, i:i + 1], io[name].partition_broadcast(128)).then_inc(consts_in, 16)

                def chunk(m, par, k, kind):
                    sp.wait_ge(wlo, m + 1)
                    load(m + 2, par)
                    if kind == "v":
                        load_ctx(sp, io, tiles, 0)
                    for t in range(NTT):
                        buf = (par + t) % 2
                        if kind == "q":
                            sp.wait_ge(roped, m * NTT + t + 1)
                            dst, src = scratch["q"][at(m - 1, 1), t * 128:(t + 1) * 128, :], qo[buf]
                            dst = dst.rearrange("a l d -> (a l) d")
                        elif kind == "k":
                            sp.wait_ge(k_fin, 4 * (t + 1))
                            dst, src = scratch["k"][t * 128:(t + 1) * 128], ko[buf]
                        else:
                            sp.wait_ge(v_fin, t + 1)
                            dst, src = scratch["v"][t * 128:(t + 1) * 128], ko[buf]
                        sp.dma_start(dst, src[:].rearrange("l a d -> l (a d)")).then_inc(rows_out[buf], 16)
                over_chunks(chunk)(sp)

            @block.gpsimd
            def _(pool):
                nc.gpsimd.memset(c["neghalf"][:], -0.5).then_inc(neg_set, 1)
                pool.wait_ge(neg_set, 1)
                for t in range(NTT):
                    pool.wait_ge(ln_mv, t + 1)
                    nc.gpsimd.tensor_scalar(ve[:, t:t + 1], mv[:, t, 1:2], 1.0, EPS_LN, ALU.mult, ALU.add).then_inc(ln_ve, 1)
                    pool.wait_ge(ln_ve, t + 1)
                    nc.gpsimd.tensor_tensor(rstd[:, t:t + 1], ve[:, t:t + 1], c["neghalf"][:, 0:1], ALU.pow).then_inc(ln_r, 1)

                def chunk(m, par, k, kind):
                    if kind == "v":
                        return
                    for t in range(NTT):
                        buf = (par + t) % 2
                        pool.wait_ge(mul_b, (m * NTT + t + 1) * 2)
                        if not (kind == "k" and t < 2):
                            if kind == "k":
                                pool.wait_ge(k_fin, 4 * (t - 1))
                            else:
                                pool.wait_ge(rows_out[buf], before(k, par, t) * 16)
                        nc.gpsimd.tensor_tensor(qo[buf][:], ra[buf][:], rb[buf][:], ALU.add).then_inc(roped, 1)
                        if kind == "k":
                            pool.wait_ge(summed, t + 1)
                            nc.gpsimd.tensor_scalar(ssk[:, t, :], ss[0][:, t, :], 1.0 / HD, EPS_RMS, ALU.mult, ALU.add).then_inc(k_ss, 1)
                            pool.wait_ge(k_ss, t + 1)
                            nc.gpsimd.tensor_tensor(rk[:, t, :], ssk[:, t, :], c["neghalf"][:, 0:4], ALU.pow).then_inc(k_r, 1)
                    if kind == "k":
                        pool.wait_ge(k_ss, NTT)
                        pool.sem_inc(sums_read, 1)
                    if kind == "q":
                        pool.wait_ge(summed, (m + 1) * NTT)
                        pool.sem_inc(waited, 1)
                        nc.gpsimd.tensor_scalar(ssr[:], ss[par][:], 1.0, HD * EPS_RMS, ALU.mult, ALU.add).then_inc(q_ss, 1)
                        pool.wait_ge(q_ss, m)
                        pool.sem_inc(sums_read, 1)
                        if par == 0:
                            pool.wait_ge(rq_out, 16 * (m - 1))
                        pool.sem_inc(waited, 1)
                        nc.gpsimd.tensor_tensor(rq[par][:].rearrange("l t h -> l (t h)"), ssr[:].rearrange("l t h -> l (t h)"),
                                                c["neghalf"][:, 0:NTT * 4], ALU.pow).then_inc(q_r, 1)
                        pool.wait_ge(q_r, m)
                        pool.sem_inc(waited, 1)
                        pool.dma_start(scratch["rq"][at(m - 1, 1), :, :].rearrange("a (t p) h -> p (a t) h", p=128), rq[par][:]).then_inc(rq_out, 16)

                over_chunks(chunk)(pool)

            def weight_dst(m, par, hi):
                if isinstance(m, int) and m >= NCH:
                    return (wch if hi else wcl)[:, :, m - NCH, :]
                return (wh if hi else wl)[par][:]

            @block.scalar
            def _(act):
                def weight(m, par, k):
                    act.wait_ge(w_in[par], k * 16 + 16)
                    if not (isinstance(m, int) and (m < 2 or m >= NCH)):
                        act.wait_ge(proj, (m - 1) * NTT)
                    nc.scalar.activation(weight_dst(m, par, True), wraw[par][:], ACT.Copy).then_inc(whi, 1)

                def xt(t):
                    act.wait_ge(t_done, t + 1)
                    nc.scalar.activation(xh[:, t, :], tbank[t % 2][:], ACT.Copy).then_inc(th, 1)

                act.wait_ge(ident_in, 16)
                nc.scalar.activation(c["identr"][:], c["ident"][:], ACT.Copy).then_inc(idr, 1)
                xt(0)
                weight(0, 0, 0)

                def k_scale(t):
                    act.wait_ge(roped, t + 1)
                    act.wait_ge(k_r, t + 1)
                    if t >= 2:
                        act.wait_ge(rows_out[t % 2], 16 * (t // 2))
                    for h in range(4):
                        nc.scalar.activation(ko[t % 2][:, h, :], qo[t % 2][:, h, :], ACT.Copy, scale=rk[:, t, h:h + 1]).then_inc(k_fin, 1)

                def chunk(m, par, k, kind):
                    for t in range(NTT):
                        buf = (par + t) % 2
                        if kind == "k" and t + 1 < NTT:
                            xt(t + 1)
                        if t == (2 if kind == "k" else 1):
                            weight(m + 1, 1 - par, k + par)
                        if kind == "v" and t == 3:
                            weight(m + 2, par, k + 1)
                        if kind == "v" and t >= NTT - NCT:
                            ctile = t - (NTT - NCT)
                            act.wait_ge(tiles["ctx_in"], 16)
                            nc.scalar.activation(tiles["parts"][ctile][0][:], tiles["raw"][:, :, ctile * CR:(ctile + 1) * CR], ACT.Copy).then_inc(tiles["ctx_his"], 1)
                        act.wait_ge(proj, m * NTT + t + 1)
                        src = heads(cbank[t % NPB][:])
                        if kind != "v":
                            if not (kind == "k" and t < 2):
                                act.wait_ge(summed, m * NTT + t - 1)
                            nc.scalar.activation(sq[buf][:], src, ACT.Square).then_inc(squared, 1)
                            if kind == "k" and t >= 2:
                                k_scale(t - 2)
                        else:
                            act.wait_ge(rows_out[buf], before(k, par, t) * 16)
                            nc.scalar.activation(ko[buf][:], src, ACT.Copy).then_inc(v_fin, 1)
                    if kind == "k":
                        k_scale(NTT - 2)
                        k_scale(NTT - 1)

                over_chunks(chunk)(act)
                act.wait_ge(consts_in, 7 * 16)
                nc.scalar.activation(c["tanhg"][:], c["gates"][:], ACT.Tanh).then_inc(tanh_s, 1)

            @block.vector
            def _(dve):
                def weight(m, par):
                    dve.wait_ge(whi, m + 1)
                    nc.vector.tensor_tensor(weight_dst(m, par, False), wraw[par][:], f32(weight_dst(m, par, True)), ALU.subtract).then_inc(wlo, 1)

                def stats(t):
                    dve.wait_ge(x_in[t], 16)
                    nc.vector.bn_stats(st[:, t, :], x[:, t, :]).then_inc(ln_st, 1)
                    dve.wait_ge(ln_st, t + 1)
                    nc.vector.bn_aggr(mv[:, t, :], st[:, t, :]).then_inc(ln_mv, 1)

                def xn_of(t):
                    dve.wait_ge(ln_mv, t + 1)
                    dve.wait_ge(ln_r, t + 1)
                    if t >= 2:
                        dve.wait_ge(t_done, t - 1)
                    nc.vector.tensor_scalar(xn[t % 2][:], x[:, t, :], mv[:, t, 0:1], rstd[:, t:t + 1],
                                            ALU.subtract, ALU.mult).then_inc(ln_x, 1)

                def xt(t):
                    dve.wait_ge(th, t + 1)
                    nc.vector.tensor_tensor(xl[:, t, :], tbank[t % 2][:], f32(xh[:, t, :]), ALU.subtract).then_inc(tl, 1)

                stats(0)
                stats(1)
                xn_of(0)
                stats(2)
                xn_of(1)
                stats(3)
                xt(0)
                weight(0, 0)
                for t in range(4, NTT):
                    stats(t)
                dve.wait_ge(consts_in, 7 * 16)
                half = HD // 2
                for i in range(2):
                    w = wn[i][:].unsqueeze(1).broadcast_to([128, NTT, HD])
                    nc.vector.tensor_tensor(tc[i][:], w, cos[:], ALU.mult).then_inc(tabs, 1)
                    nc.vector.tensor_tensor(ts[i][:, :, 0:half], w[:, :, half:], sin[:, :, 0:half], ALU.mult).then_inc(tabs, 1)
                    nc.vector.tensor_tensor(ts[i][:, :, half:], w[:, :, 0:half], sin[:, :, half:], ALU.mult).then_inc(tabs, 1)
                dve.wait_ge(tabs, 6)

                def chunk(m, par, k, kind):
                    i = 0 if kind == "q" else 1
                    for t in range(NTT):
                        buf = (par + t) % 2
                        if kind == "k" and t + 1 < NTT:
                            xt(t + 1)
                            if t + 2 < NTT:
                                xn_of(t + 2)
                        if t == (2 if kind == "k" else 1):
                            weight(m + 1, 1 - par)
                        if kind == "v" and t == 3:
                            weight(m + 2, par)
                        if kind == "v" and t >= NTT - NCT:
                            ctile = t - (NTT - NCT)
                            dve.wait_ge(tiles["ctx_his"], ctile + 1)
                            nc.vector.tensor_tensor(tiles["parts"][ctile][1][:], tiles["raw"][:, :, ctile * CR:(ctile + 1) * CR],
                                                    f32(tiles["parts"][ctile][0][:]), ALU.subtract).then_inc(tiles["ctx_los"], 1)
                        if kind == "v":
                            continue
                        src = heads(cbank[t % NPB][:])
                        cosw, sinw = (a[:, t, :].unsqueeze(1).broadcast_to([128, 4, HD]) for a in (tc[i], ts[i]))
                        dve.wait_ge(squared, m * NTT + t + 1)
                        if not (kind == "k" and t < 2):
                            dve.wait_ge(roped, m * NTT + t - 1)
                        nc.vector.tensor_tensor(ra[buf][:], src, cosw, ALU.mult).then_inc(mul_a, 1)
                        nc.vector.tensor_tensor(rb[buf][:, :, 0:half], src[:, :, half:], sinw[:, :, 0:half], ALU.mult).then_inc(mul_b, 1)
                        nc.vector.tensor_tensor(rb[buf][:, :, half:], src[:, :, 0:half], sinw[:, :, half:], ALU.mult).then_inc(mul_b, 1)
                        if t == 0 and not (isinstance(m, int) and m == 0):
                            dve.wait_ge(sums_read, m)
                        nc.vector.tensor_reduce(ss[par][:, t, :], sq[buf][:], AX.X, ALU.add).then_inc(summed, 1)

                over_chunks(chunk)(dve)

            @block.tensor
            def _(pe):
                pe.wait_ge(ident_in, 16)

                def xt(t):
                    pe.wait_ge(ln_x, t + 1)
                    if t >= 2:
                        pe.wait_ge(tl, t - 1)
                    for kt in range(KT):
                        mm = nc.tensor.transpose(tbank[t % 2][:, kt * 128:(kt + 1) * 128], xn[t % 2][:, kt * 128:(kt + 1) * 128], c["ident"][:])
                    mm.then_inc(t_done, 1)

                xt(0)

                def chunk(m, par, k, kind):
                    for t in range(NTT):
                        if kind == "k" and t + 1 < NTT:
                            xt(t + 1)
                        if t == 0:
                            pe.wait_ge(wlo, m + 1)
                        if kind == "k":
                            pe.wait_ge(tl, t + 1)
                        if t < NPB and kind != "k":
                            last = t + NPB if t + NPB < NTT else t
                            pe.wait_ge(mul_b, ((m - 1) * NTT + last + 1) * 2)
                        elif kind == "v":
                            pe.wait_ge(v_fin, t - NPB + 1)
                        elif t >= NPB:
                            pe.wait_ge(mul_b, (m * NTT + t - NPB + 1) * 2)
                        for kt in range(KT):
                            cols = slice(kt * 128, (kt + 1) * 128)
                            mm = mm3(nc, cbank[t % NPB][:], xh[:, t, cols], xl[:, t, cols],
                                     wh[par][:, kt, :], wl[par][:, kt, :], kt == 0, kt == KT - 1)
                        mm.then_inc(proj, 1)

                over_chunks(chunk)(pe)
                pe.wait_ge(idr, 1)
                keep_busy(nc, c, banks[7], 12)
        return used, [(s, 16 * NCH * NTT // 2) for s in rows_out] + [(rq_out, 16 * NQ)]


def attention(nc, io, scratch, banks, c, wch, wcl, tiles, wo, used, stored):
    with ExitStack() as ctx:
        def sb(name, shape, dt=F32):
            return ctx.enter_context(nc.sbuf_tensor(name, shape, dt))

        def sem(name):
            return ctx.enter_context(nc.semaphore(name))

        waited = sem("waited")

        def pair(name, shape, n=1):
            return [(sb(f"{name}_hi{i}", shape, F32R), sb(f"{name}_lo{i}", shape, F32R)) for i in range(n)]

        maskraw = sb("mask_raw", [L, MW])
        mask = sb("mask", [L, MW], F32R)
        craw, ct, ctx_in, cthi, ctlo = (tiles[n] for n in ("raw", "parts", "ctx_in", "ctx_his", "ctx_los"))
        ktok = sb("k_tok", [CR, NKT, NKV, HD])
        vraw = sb("v_raw", [L, KW])
        sq = sb("csq", [CR, NKV, HD])
        css, csr, crk = sb("css", [CR, NCT, NKV]), sb("csr", [CR, NKV]), sb("crk", [CR, NCT, NKV])
        kT = pair("k_t", [128, NKV, NSC], 2)
        V = pair("v_tok", [CR, NKT, KW], 2)
        q = [sb(f"q_tok{i}", [L, QW]) for i in range(2)]
        qT = pair("q_t", [128, GW], 2)
        Pm = [sb(f"probs{i}", [L, NPAD]) for i in range(2 * REP)]
        pT = pair("p_t", [CR, NKT, GW], 2)
        oT = [sb(f"o_t{i}", [128, GW]) for i in range(2)]
        mx, nb = sb("row_max", [L, NH]), sb("neg_bias", [L, NH])
        rs, ri = sb("row_sum", [L, NH]), sb("row_inv", [L, NH])

        mask_in, mask_set, pads = sem("mask_in"), sem("mask_set"), sem("pads")
        kself_in, vself_in, rq_in = sem("kself_in"), sem("vself_in"), sem("rq_in")
        q_in = [sem(f"q_in{i}") for i in range(2)]
        kproj, vproj, csqd, csum, cadd, cpow, kscaled = (sem(n) for n in (
            "kproj", "vproj", "csquared", "csummed", "cadded", "cpowered", "kscaled"))
        vhi, vlo, vshi, vslo = sem("v_his"), sem("v_los"), sem("vself_his"), sem("vself_los")
        ktr, kthi, ktlo = sem("k_transposed"), sem("k_his"), sem("k_los")
        qtr, qthi, qtlo = sem("q_transposed"), sem("q_his"), sem("q_los")
        scored, maxed, biased, exped, inverted, normed = (sem(n) for n in (
            "scored", "maxed", "biased", "exped", "inverted", "normed"))
        ptr, pthi, ptlo, pv, oev = sem("p_transposed"), sem("p_his"), sem("p_los"), sem("pv_done"), sem("o_read")
        o_out = wo["o_out"]
        sbank, pbank, qbank, mbank, obank = banks[0:2], banks[2:4], banks[4], banks[5:7], banks[7]

        pieces = {0: [("c", 0)], 1: [("c", 1)], 2: [("k", 0), ("c", 2)], 4: [("k", 1)], 5: [("t", 0)], 6: [("k", 2)],
                  7: [("t", 1)], 8: [("t", NCT)], 9: [("v", 0)], 11: [("v", 1)], 12: [("t", 2)], 13: [("v", 2)]}
        order = [p for at_head in pieces.values() for p in at_head]
        users = [p for p in order if p[0] != "c"]
        users0 = [("k", 0), ("v", 0), ("t", 0), ("k", 1), ("v", 1), ("t", 1), ("k", 2), ("t", NCT), ("t", 2), ("v", 2)]
        assert users0[-2:] == users[-2:] and [p for p in users0 if p[0] == "t"] == [p for p in users if p[0] == "t"]
        T_ORDER = [t for kind, t in order if kind == "t"]
        assert len(users) % 2 == 0

        def users_of(b):
            return users0 if is_first(b) else users

        def bank_of(b, piece):
            return mbank[users_of(b).index(piece) % 2]

        def schedule(eng, start, first_q, step, piece, tail):
            start()
            for p in users0[:7]:
                piece(0, 0, *p)
            first_q()
            for p in users0[7:]:
                piece(0, 0, *p)

            def batch(b, par, k):
                for g in range(NKV):
                    for h in range(REP):
                        step(b, par, k, g, h)
                        if not is_last(b):
                            for p in pieces.get(g * REP + h, []):
                                piece(b + 1, 1 - par, *p)

            over_batches(eng, batch)
            tail()

        def back(b, g, n):
            return b + (g - n) // NKV, (g - n) % NKV

        def exists(b, g):
            return not isinstance(b, int) or b >= 0

        with nc.Block() as block:
            @block.sync
            def _(sp):
                sp.dma_start(maskraw[:], io["c_mask"]).then_inc(mask_in, 16)
                for sem, count in stored:
                    sp.wait_ge(sem, count)
                nums = sorted(sem.num for sem in used)
                assert nums == list(range(nums[0], nums[-1] + 1))
                sp.sem_clear(range(nums[0], nums[-1] + 1))

                def next_ctx(b):
                    sp.wait_ge(ctlo, b * NCT)
                    load_ctx(sp, io, tiles, b)

                def load_self(b, par):
                    if not is_first(b, 2):
                        sp.wait_ge(qtr, (b - 1) * NKV)
                    sp.dma_start(q[par][:].rearrange("l (m d) -> l m d", m=NQ), scratch["q"][:, at(b, L), :].rearrange("m l d -> l m d")).then_inc(q_in[par], 16)
                    if not is_first(b):
                        sp.wait_ge(ktr, b * NKT)
                    sp.dma_start(ktok[0:L, NCT, :, :], scratch["k"][at(b, L), :].rearrange("l (h d) -> l h d", h=NKV)).then_inc(kself_in, 16)
                    if not is_first(b):
                        sp.wait_ge(vslo, b)
                    sp.dma_start(vraw[:], scratch["v"][at(b, L), :]).then_inc(vself_in, 16)

                def store(b, g):
                    sp.wait_ge(oev, b * NKV + g + 1)
                    sp.dma_start(scratch["o"][at(b, 1), :, g * GW:(g + 1) * GW].rearrange("a p n -> (a p) n"),
                                 oT[g % 2][:]).then_inc(o_out[g % 2], 16)

                load_self(0, 0)
                for m in range(NQ):
                    sp.dma_start(c["rq"][:, m * B * REP:(m + 1) * B * REP].rearrange("l (b h) -> l b h", b=B),
                                 scratch["rq"][m].rearrange("(b l) h -> l b h", b=B)).then_inc(rq_in, 16)
                next_ctx(1)
                load_self(1, 1)

                def batch(b, par):
                    for g in range(NKV):
                        if exists(*back(b, g, 3)):
                            store(*back(b, g, 3))
                        if not (isinstance(b, int) and b >= B - 2):
                            if g == 0:
                                next_ctx(b + 2)
                            if g == 2:
                                load_self(b + 2, par)

                batch(0, 0)
                with sp.Fori(0, (B - 4) // 2) as i:
                    batch(i * 2 + 1, 1)
                    batch(i * 2 + 2, 0)
                for b in range(B - 3, B):
                    batch(b, b % 2)
                sp.dma_start(wo["raw"][:], io["wo"][:, 0:NH // NWO, :]).then_inc(wo["in"], 16)
                for n in (3, 2, 1):
                    store(*back(B, 0, n))

            @block.gpsimd
            def _(pool):
                def start():
                    for i in range(2 * REP):
                        nc.gpsimd.memset(Pm[i][:, NKEY:], 0.0).then_inc(pads, 1)
                    for i in range(2):
                        for m in kT[i]:
                            nc.gpsimd.memset(f32(m[:, :, NKEY:]), 0.0).then_inc(pads, 1)
                    pool.wait_ge(pads, 2 * REP + 8)

                def piece(b, par, kind, t):
                    if kind == "c":
                        pool.wait_ge(ctx_in, b * 16 + 16)
                        if not is_first(b):
                            pool.wait_ge(vproj, (b - 1) * NCT + t + 1)
                        src = craw[:, :, t * CR:(t + 1) * CR]
                        pool.sem_inc(waited, 1)
                        nc.gpsimd.tensor_copy(ct[t][0][:], src).then_inc(cthi, 1)
                        pool.wait_ge(cthi, b * NCT + t + 1)
                        nc.gpsimd.tensor_tensor(ct[t][1][:], src, f32(ct[t][0][:]), ALU.subtract).then_inc(ctlo, 1)
                    if kind == "k":
                        pool.wait_ge(csum, b * NCT + t + 1)
                        if not (is_first(b) and t == 0):
                            pool.wait_ge(cpow, b * NCT + t)
                        pool.sem_inc(waited, 1)
                        nc.gpsimd.tensor_scalar(csr[:], css[:, t, :], 1.0 / HD, EPS_RMS, ALU.mult, ALU.add).then_inc(cadd, 1)
                        pool.wait_ge(cadd, b * NCT + t + 1)
                        nc.gpsimd.tensor_tensor(crk[:, t, :], csr[:], c["neghalf"][0:CR, 0:NKV], ALU.pow).then_inc(cpow, 1)
                    if kind == "v" and t == 0:
                        pool.wait_ge(vself_in, b * 16 + 16)
                        if not is_first(b, 2):
                            pool.wait_ge(pv, (b - 1) * NKV)
                        pool.sem_inc(waited, 1)
                        nc.gpsimd.tensor_copy(V[par][0][0:L, NCT, :], vraw[:]).then_inc(vshi, 1)
                        pool.wait_ge(vshi, b + 1)
                        nc.gpsimd.tensor_tensor(V[par][1][0:L, NCT, :], vraw[:], f32(V[par][0][0:L, NCT, :]), ALU.subtract).then_inc(vslo, 1)

                def norm(b, g, pair):
                    pool.wait_ge(inverted, b * (NH // 2) + g * (REP // 2) + pair + 1)
                    pool.sem_inc(waited, 1)
                    for h in (2 * pair, 2 * pair + 1):
                        p = Pm[(g % 2) * REP + h]
                        col = g * REP + h
                        nc.gpsimd.tensor_scalar(p[:, 0:NKEY], p[:, 0:NKEY], ri[:, col:col + 1], 1.0, ALU.mult, ALU.mult).then_inc(normed, 1)

                def step(b, par, k, g, h):
                    if h == 0 and exists(*back(b, g, 1)):
                        norm(*back(b, g, 1), 1)
                    if h == 2:
                        norm(b, g, 0)

                schedule(pool, start, lambda: None, step, piece, lambda: norm(B - 1, NKV - 1, 1))

            @block.scalar
            def _(act):
                def start():
                    act.wait_ge(mask_in, 16)
                    nc.scalar.activation(mask[:], maskraw[:], ACT.Copy).then_inc(mask_set, 1)

                def piece(b, par, kind, t):
                    if kind == "k":
                        act.wait_ge(kproj, b * NCT + t + 1)
                        if not (is_first(b) and t == 0):
                            act.wait_ge(csum, b * NCT + t)
                        nc.scalar.activation(sq[:], bank_of(b, (kind, t))[0:CR, :].rearrange("r (h d) -> r h d", h=NKV), ACT.Square).then_inc(csqd, 1)
                    elif kind == "v":
                        act.wait_ge(vproj, b * NCT + t + 1)
                        if not is_first(b, 2):
                            act.wait_ge(pv, (b - 1) * NKV)
                        nc.scalar.activation(V[par][0][:, t, :], bank_of(b, (kind, t))[0:CR, :], ACT.Copy).then_inc(vhi, 1)
                    elif kind == "t":
                        n = L if t == NCT else CR
                        act.wait_ge(ktr, b * NKT + T_ORDER.index(t) + 1)
                        if not is_first(b, 2):
                            act.wait_ge(scored, (b - 1) * NH)
                        nc.scalar.activation(kT[par][0][:, :, t * CR:t * CR + n],
                                             bank_of(b, (kind, t))[:, 0:NKV * CR].rearrange("p (h r) -> p h r", h=NKV)[:, :, 0:n],
                                             ACT.Copy, scale=1.0 if t == NCT else c["wkn"][:, 0:1]).then_inc(kthi, 1)

                def q_hi(b, g):
                    act.wait_ge(qtr, b * NKV + g + 1)
                    if not (is_first(b) and g < 2):
                        act.wait_ge(scored, (b * NKV + g - 1) * REP)
                    nc.scalar.activation(qT[g % 2][0][:], qbank[:, 0:GW], ACT.Copy).then_inc(qthi, 1)

                def p_hi(b, g, h):
                    act.wait_ge(ptr, b * NH + g * REP + h + 1)
                    if h == 0 and not (is_first(b) and g < 2):
                        act.wait_ge(pv, b * NKV + g - 1)
                    nc.scalar.activation(pT[g % 2][0][:, :, h * L:(h + 1) * L],
                                         pbank[h % 2][0:CR, 0:NKT * L].rearrange("r (t l) -> r t l", t=NKT), ACT.Copy).then_inc(pthi, 1)

                def o_read(b, g):
                    act.wait_ge(pv, b * NKV + g + 1)
                    if not (is_first(b) and g < 2):
                        act.wait_ge(o_out[g % 2], (b * (NKV // 2) + g // 2) * 16)
                    nc.scalar.activation(oT[g % 2][:], obank[:, 0:GW], ACT.Copy).then_inc(oev, 1)

                def step(b, par, k, g, h):
                    if h == REP - 1 and exists(*back(b, g, 2)):
                        o_read(*back(b, g, 2))
                    if exists(*back(b, g, 1)):
                        p_hi(*back(b, g, 1), h)
                    if h == 2 and not (is_last(b) and g == NKV - 1):
                        q_hi(*back(b, g, -1))
                    n = b * NH + g * REP + h
                    col = g * REP + h
                    act.wait_ge(biased, n + 1)
                    if not (is_first(b) and g < 2):
                        act.wait_ge(ptr, n + 1 - 2 * REP)
                    if not is_first(b):
                        act.wait_ge(normed, n + 1 - NH)
                    nc.scalar.activation(Pm[(g % 2) * REP + h][:, 0:NKEY], sbank[h % 2][0:L, 0:NKEY], ACT.Exp, bias=nb[:, col:col + 1],
                                         scale=c["rq"][:, bass.ds(g * B * REP + b * REP + h, 1)],
                                         accum_out=rs[:, col:col + 1]).then_inc(exped, 1)

                def tail():
                    for h in range(REP):
                        p_hi(B - 1, NKV - 1, h)
                    o_read(B - 1, NKV - 2)
                    o_read(B - 1, NKV - 1)

                def first_q():
                    q_hi(0, 0)
                    act.wait_ge(rq_in, 16 * NQ)

                schedule(act, start, first_q, step, piece, tail)

            @block.vector
            def _(dve):
                def k_norm(b, t):
                    dve.wait_ge(cpow, b * NCT + t + 1)
                    if not is_first(b):
                        dve.wait_ge(ktr, b * NKT)
                    nc.vector.tensor_tensor(ktok[:, t, :, :], bank_of(b, ("k", t))[0:CR, :].rearrange("r (h d) -> r h d", h=NKV),
                                            crk[:, t, :].unsqueeze(2).broadcast_to([CR, NKV, HD]), ALU.mult).then_inc(kscaled, 1)

                def piece(b, par, kind, t):
                    if kind == "c":
                        return
                    before = users_of(b).index((kind, t)) - 1
                    if before >= 0 and users_of(b)[before][0] == "k":
                        k_norm(b, users_of(b)[before][1])
                    bank = bank_of(b, (kind, t))
                    if kind == "k":
                        dve.wait_ge(csqd, b * NCT + t + 1)
                        if not is_first(b):
                            dve.wait_ge(cadd, (b - 1) * NCT + t + 1)
                        nc.vector.tensor_reduce(css[:, t, :], sq[:], AX.X, ALU.add).then_inc(csum, 1)
                    elif kind == "v":
                        dve.wait_ge(vhi, b * NCT + t + 1)
                        nc.vector.tensor_tensor(V[par][1][:, t, :], bank[0:CR, :], f32(V[par][0][:, t, :]), ALU.subtract).then_inc(vlo, 1)
                    else:
                        n = L if t == NCT else CR
                        hi, lo = (m[:, :, t * CR:t * CR + n] for m in kT[par])
                        dve.wait_ge(kthi, b * NKT + T_ORDER.index(t) + 1)
                        nc.vector.scalar_tensor_tensor(out=lo, in0=bank[:, 0:NKV * CR].rearrange("p (h r) -> p h r", h=NKV)[:, :, 0:n],
                                                       scalar=1.0 if t == NCT else c["wkn"][:, 0:1], in1=f32(hi),
                                                       op0=ALU.mult, op1=ALU.subtract).then_inc(ktlo, 1)

                def q_lo(b, g):
                    dve.wait_ge(qthi, b * NKV + g + 1)
                    nc.vector.tensor_tensor(qT[g % 2][1][:], qbank[:, 0:GW], f32(qT[g % 2][0][:]), ALU.subtract).then_inc(qtlo, 1)

                def p_lo(b, g, h):
                    dve.wait_ge(pthi, b * NH + g * REP + h + 1)
                    nc.vector.tensor_tensor(pT[g % 2][1][:, :, h * L:(h + 1) * L],
                                            pbank[h % 2][0:CR, 0:NKT * L].rearrange("r (t l) -> r t l", t=NKT),
                                            f32(pT[g % 2][0][:, :, h * L:(h + 1) * L]), ALU.subtract).then_inc(ptlo, 1)

                def invert(b, g, pair):
                    n = b * NH + g * REP + 2 * pair
                    col = g * REP + 2 * pair
                    dve.wait_ge(exped, n + 2)
                    if not is_first(b):
                        dve.wait_ge(normed, n + 2 - NH)
                    nc.vector.reciprocal(ri[:, col:col + 2], rs[:, col:col + 2]).then_inc(inverted, 1)

                def step(b, par, k, g, h):
                    n = b * NH + g * REP + h
                    col = g * REP + h
                    dve.wait_ge(scored, n + 1)
                    nc.vector.tensor_reduce(mx[:, col:col + 1], sbank[h % 2][0:L, 0:NKEY], AX.X, ALU.max).then_inc(maxed, 1)
                    if h == 0 and exists(*back(b, g, 1)):
                        invert(*back(b, g, 1), 1)
                    if h == 2:
                        invert(b, g, 0)
                    dve.wait_ge(maxed, n + 1)
                    if not is_first(b):
                        dve.wait_ge(exped, n + 1 - NH)
                    nc.vector.tensor_scalar(nb[:, col:col + 1], mx[:, col:col + 1], c["rq"][:, bass.ds(g * B * REP + b * REP + h, 1)], -1.0, ALU.mult, ALU.mult).then_inc(biased, 1)
                    if exists(*back(b, g, 1)):
                        p_lo(*back(b, g, 1), h)
                    if h == 2 and not (is_last(b) and g == NKV - 1):
                        q_lo(*back(b, g, -1))

                def start():
                    for m in (*V[0], *V[1]):
                        nc.vector.memset(f32(m[96:CR, NCT, :]), 0.0).then_inc(pads, 1)

                def tail():
                    invert(B - 1, NKV - 1, 1)
                    for h in range(REP):
                        p_lo(B - 1, NKV - 1, h)

                def first_q():
                    q_lo(0, 0)
                    dve.wait_ge(rq_in, 16 * NQ)

                schedule(dve, start, first_q, step, piece, tail)

            @block.tensor
            def _(pe):
                def q_t(b, par, k, g):
                    pe.wait_ge(q_in[par], k * 16 + 16)
                    if not (is_first(b) and g == 0):
                        pe.wait_ge(qtlo, b * NKV + g)
                    for r in range(REP):
                        hh = g * REP + r
                        mm = nc.tensor.transpose(qbank[:, r * L:(r + 1) * L], q[par][:, hh * HD:(hh + 1) * HD], c["ident"][0:L, 0:L])
                    mm.then_inc(qtr, 1)

                def bank_read(b, kind, t):
                    if kind == "k":
                        pe.wait_ge(kscaled, b * NCT + t + 1)
                    elif kind == "v":
                        pe.wait_ge(vlo, b * NCT + t + 1)
                    else:
                        pe.wait_ge(ktlo, b * NKT + T_ORDER.index(t) + 1)

                def piece(b, par, kind, t):
                    if kind == "c":
                        return
                    use = users_of(b).index((kind, t))
                    bank = bank_of(b, (kind, t))
                    if use >= 2:
                        bank_read(b, *users_of(b)[use - 2])
                    elif not is_first(b):
                        bank_read(b - 1, *users[use - 2])
                    if kind in "kv":
                        pe.wait_ge(ctlo, b * NCT + t + 1)
                        i = 0 if kind == "k" else 1
                        for kt in range(KT):
                            mm = mm3(nc, bank[0:CR, :], ct[t][0][:, kt, :], ct[t][1][:, kt, :],
                                     wch[:, kt, i, :], wcl[:, kt, i, :], kt == 0, kt == KT - 1)
                        mm.then_inc(kproj if kind == "k" else vproj, 1)
                    else:
                        n = L if t == NCT else CR
                        if t == NCT:
                            pe.wait_ge(kself_in, b * 16 + 16)
                        else:
                            pe.wait_ge(kscaled, b * NCT + t + 1)
                        for h in range(NKV):
                            mm = nc.tensor.transpose(bank[:, h * CR:h * CR + n], ktok[0:n, t, h, :], c["ident"][0:n, 0:n])
                        mm.then_inc(ktr, 1)

                def p_t(b, g, h):
                    n = b * NH + g * REP + h
                    p = Pm[(g % 2) * REP + h]
                    pe.wait_ge(normed, n + 1)
                    if not (is_first(b) and g == 0 and h < 2):
                        pe.wait_ge(ptlo, n - 1)
                    for t in range(NKT):
                        mm = nc.tensor.transpose(pbank[h % 2][0:CR, t * L:(t + 1) * L], p[:, t * CR:(t + 1) * CR], c["ident"][0:L, 0:L])
                    mm.then_inc(ptr, 1)

                def pv_part(b, par, g, t):
                    n = b * NKV + g
                    if t == 0:
                        pe.wait_ge(ptlo, (n + 1) * REP)
                        if not (is_first(b) and g == 0):
                            pe.wait_ge(oev, n)
                    mm = mm3(nc, obank[:, 0:GW], V[par][0][:, t, g * HD:(g + 1) * HD], V[par][1][:, t, g * HD:(g + 1) * HD],
                             pT[g % 2][0][:, t, :], pT[g % 2][1][:, t, :], t == 0, t == NKT - 1)
                    if t == NKT - 1:
                        mm.then_inc(pv, 1)

                def step(b, par, k, g, h):
                    n = b * NH + g * REP + h
                    if h == 0:
                        pe.wait_ge(qtlo, b * NKV + g + 1)
                        if g == 0:
                            pe.wait_ge(ktlo, b * NKT + NKT)
                            pe.wait_ge(vlo, b * NCT + NCT)
                            pe.wait_ge(vslo, b + 1)
                    if not (is_first(b) and g == 0 and h < 2):
                        pe.wait_ge(exped, n - 1)
                    cols = slice(h * L, (h + 1) * L)
                    bank = sbank[h % 2]
                    mm3(nc, bank[0:L, 0:NSC], qT[g % 2][0][:, cols], qT[g % 2][1][:, cols],
                        kT[par][0][:, g, :], kT[par][1][:, g, :], True, False)
                    nc.tensor.matmul(bank[0:L, MO:NSC], c["identr"][0:L, 0:L], mask[:], start=False, stop=True).then_inc(scored, 1)
                    if h == 0 and exists(*back(b, g, 1)):
                        p_t(*back(b, g, 1), h)
                    if exists(*back(b, g, 2)):
                        vb, vg = back(b, g, 2)
                        pv_part(vb, par if g >= 2 else 1 - par, vg, h)
                    if h and exists(*back(b, g, 1)):
                        p_t(*back(b, g, 1), h)
                    if h == 1 and g < NKV - 1:
                        q_t(b, par, k, g + 1)
                    elif h == 1 and not is_last(b):
                        q_t(b + 1, 1 - par, k + par, 0)

                def first_q():
                    pe.wait_ge(mask_set, 1)
                    pe.wait_ge(pads, 2 * REP + 8)
                    q_t(0, 0, 0, 0)

                def tail():
                    for h in range(REP):
                        pv_part(B - 1, 1, NKV - 2, h)
                        p_t(B - 1, NKV - 1, h)
                    for t in range(NKT):
                        pv_part(B - 1, 1, NKV - 1, t)
                    keep_busy(nc, c, mbank[0], 10)

                schedule(pe, lambda: None, first_q, step, piece, tail)


def load_up(sp, io, up, j):
    w = TB if j < NFT else TW
    sp.dma_start(up["raw"][j % RING][:, 0:w], io["sw13"][:, j * TB:j * TB + w]).then_inc(up["in"][j % RING], 16)


def load_down(sp, io, down):
    sp.dma_start(down["raw"][:, 0:NFT, :], io["sw2"]).then_inc(down["in"], 16)
    sp.dma_start(down["raw"][0:TAIL, NFT, :], io["sw2t"]).then_inc(down["in"], 16)


def out_projection(nc, io, scratch, banks, c, x1, x2h, x2l, wo, up, down, routed):
    with ExitStack() as ctx:
        def sb(name, shape, dt=F32):
            return ctx.enter_context(nc.sbuf_tensor(name, shape, dt))

        def sem(name):
            return ctx.enter_context(nc.semaphore(name))

        waited = sem("waited")

        NW = NWO
        HW = NH // NW
        woh, wol = sb("wo_hi", [128, NH, DM], F32R), sb("wo_lo", [128, NH, DM], F32R)
        spare = routed["w0"]
        W1, W2 = HW * DM, HW * DM + NH * L
        assert W2 + DM <= EW
        wraw = [wo["raw"][:], spare[:, 0:W1].rearrange("p (h d) -> p h d", h=HW)]
        oraw = [spare[:, W1:W2], sb("o_raw1", [128, NH * L])[:]]
        oh = [sb(f"o_hi{i}", [128, NH * L], F32R) for i in range(2)]
        ol = [sb(f"o_lo{i}", [128, NH * L], F32R) for i in range(2)]
        x = [spare[0:L, W2:W2 + DM], sb("x_in1", [L, DM])[:]]
        st, mv, ve, rstd = sb("st2", [L, 6]), sb("mv2", [L, 2]), sb("ve2", [L, 1]), sb("rstd2", [L, 1])
        xn = [sb(f"xn2_{i}", [L, DM]) for i in range(2)]
        rows_out = routed["x2_out"]

        w_in = [wo["in"], sem("wo_in1")]
        first_in = [sem(f"first_o_in{n}") for n in range(NW)]
        fhi, flo = sem("first_o_his"), sem("first_o_los")
        o_in, x_in = ([sem(f"{n}{i}") for i in range(2)] for n in ("o_in", "x_ins"))
        whi, wlo, ohi, olo = sem("wo_his"), sem("wo_los"), sem("o_his"), sem("o_los")
        proj, x1_set, ln_st, ln_mv, ln_ve, ln_r, ln_x = (sem(n) for n in (
            "o_proj", "x1_set", "ln2_st", "ln2_mv", "ln2_ve", "ln2_r", "ln2_x"))
        t_done, th, tl = sem("x2_psum"), sem("x2_his"), sem("x2_los")
        ybank, tbank = banks[0:2], banks[2]

        def over_steps(eng, step):
            with eng.Fori(1, B // 2 - 1) as i:
                step(i * 2, 0, i)
                step(i * 2 + 1, 1, i)
            for n in range(B - 2, B + 2):
                step(n, n % 2, n // 2)

        def has(n, back):
            return not isinstance(n, int) or 0 <= n - back < B

        with nc.Block() as block:
            @block.sync
            def _(sp):
                def load_x(b, par):
                    if not is_first(b, 2):
                        sp.wait_ge(x1_set, b - 1)
                    sp.dma_start(x[par], io["x"][at(b, 1), :, :].rearrange("a l d -> (a l) d")).then_inc(x_in[par], 16)

                def load(b, par):
                    if is_first(b, 4):
                        sp.wait_ge(flo, 2 * NW)
                    else:
                        sp.wait_ge(olo, b - 3)
                    sp.dma_start(oraw[par], scratch["o"][at(b, 1), :, :].rearrange("a p n -> (a p) n")).then_inc(o_in[par], 16)
                    load_x(b, par)

                for n in range(NW):
                    if n >= 2:
                        sp.wait_ge(wlo, n - 1)
                    if n:
                        sp.dma_start(wraw[n % 2], io["wo"][:, n * HW:(n + 1) * HW, :]).then_inc(w_in[n % 2], 16)
                    cols = slice(n * HW * L, (n + 1) * HW * L)
                    for b in range(2):
                        sp.dma_start(oraw[b][:, cols], scratch["o"][b][:, cols]).then_inc(first_in[n], 16)
                for b in range(2):
                    load_x(b, b)
                for i in range(2):
                    sp.wait_ge(wo["o_out"][i], 16 * B * NKV // 2)
                for b in range(2, 4):
                    load(b, b % 2)
                with sp.Fori(2, B // 2) as i:
                    load(i * 2, 0)
                    load(i * 2 + 1, 1)
                for j in range(RING):
                    load_up(sp, io, up, j)
                load_down(sp, io, down)

            @block.gpsimd
            def _(pool):
                def batch(b):
                    pool.wait_ge(ln_mv, b + 1)
                    pool.sem_inc(waited, 1)
                    nc.gpsimd.tensor_scalar(ve[:], mv[:, 1:2], 1.0, EPS_LN, ALU.mult, ALU.add).then_inc(ln_ve, 1)
                    pool.wait_ge(ln_ve, b + 1)
                    nc.gpsimd.tensor_tensor(rstd[:], ve[:], c["neghalf"][0:L, 0:1], ALU.pow).then_inc(ln_r, 1)

                with pool.Fori(0, B) as b:
                    batch(b)

            @block.scalar
            def _(act):
                def o_hi(b, par, k):
                    act.wait_ge(o_in[par], k * 16)
                    act.wait_ge(proj, b - 1)
                    nc.scalar.activation(oh[par][:], oraw[par], ACT.Copy).then_inc(ohi, 1)

                for n in range(NW):
                    act.wait_ge(w_in[n % 2], 16 * (n // 2 + 1))
                    nc.scalar.activation(woh[:, n * HW:(n + 1) * HW, :], wraw[n % 2], ACT.Copy).then_inc(whi, 1)
                    cols = slice(n * HW * L, (n + 1) * HW * L)
                    act.wait_ge(first_in[n], 32)
                    for b in range(2):
                        nc.scalar.activation(oh[b][:, cols], oraw[b][:, cols], ACT.Copy).then_inc(fhi, 1)
                o_hi(2, 0, 1)

                def step(n, par, k):
                    if has(n, -1):
                        o_hi(n + 1, 1 - par, k + par)
                    act.wait_ge(t_done, n - 1)
                    nc.scalar.activation(x2h[:, :, at(n - 2, L)], tbank[:, 0:KT * L].rearrange("p (k l) -> p k l", k=KT), ACT.Copy).then_inc(th, 1)
                    act.wait_ge(ln_x, n - 1)
                    act.dma_start(scratch["x2"][at(n - 2, L), :], xn[par][:]).then_inc(rows_out[par], 16)

                over_steps(act, step)

            @block.vector
            def _(dve):
                def o_lo(b, par):
                    dve.wait_ge(ohi, b - 1)
                    dve.wait_ge(proj, b - 1)
                    nc.vector.tensor_tensor(ol[par][:], oraw[par], f32(oh[par][:]), ALU.subtract).then_inc(olo, 1)

                for n in range(NW):
                    dve.wait_ge(whi, n + 1)
                    nc.vector.tensor_tensor(wol[:, n * HW:(n + 1) * HW, :], wraw[n % 2], f32(woh[:, n * HW:(n + 1) * HW, :]), ALU.subtract).then_inc(wlo, 1)
                    cols = slice(n * HW * L, (n + 1) * HW * L)
                    for b in range(2):
                        dve.wait_ge(fhi, n * 2 + b + 1)
                        nc.vector.tensor_tensor(ol[b][:, cols], oraw[b][:, cols], f32(oh[b][:, cols]), ALU.subtract).then_inc(flo, 1)

                def normalise(b, par, k):
                    x1b = x1[:, at(b, 1), :].rearrange("l a d -> l (a d)")
                    dve.wait_ge(proj, b + 1)
                    dve.wait_ge(x_in[par], k * 16 + 16)
                    nc.vector.scalar_tensor_tensor(out=x1b, in0=ybank[par][0:L, :], scalar=c["tanhg"][0:L, 0:1],
                                                   in1=x[par], op0=ALU.mult, op1=ALU.add).then_inc(x1_set, 1)
                    dve.wait_ge(x1_set, b + 1)
                    dve.sem_inc(waited, 1)
                    nc.vector.bn_stats(st[:], x1b).then_inc(ln_st, 1)
                    dve.wait_ge(ln_st, b + 1)
                    dve.sem_inc(waited, 1)
                    nc.vector.bn_aggr(mv[:], st[:]).then_inc(ln_mv, 1)
                    dve.wait_ge(ln_r, b + 1)
                    dve.wait_ge(ln_mv, b + 1)
                    if not is_first(b):
                        dve.wait_ge(t_done, b)
                    if not is_first(b, 2):
                        dve.wait_ge(rows_out[par], 16 * k)
                    nc.vector.tensor_scalar(xn[par][:], x1b, mv[:, 0:1], rstd[:], ALU.subtract, ALU.mult).then_inc(ln_x, 1)

                def step(n, par, k):
                    if has(n, -1):
                        o_lo(n + 1, 1 - par)
                    if has(n, 1):
                        normalise(n - 1, 1 - par, k - 1 + par)
                    dve.wait_ge(th, n - 1)
                    nc.vector.tensor_tensor(x2l[:, :, at(n - 2, L)], tbank[:, 0:KT * L].rearrange("p (k l) -> p k l", k=KT),
                                            f32(x2h[:, :, at(n - 2, L)]), ALU.subtract).then_inc(tl, 1)

                normalise(0, 0, 0)
                o_lo(2, 0)
                over_steps(dve, step)

            @block.tensor
            def _(pe):
                def heads(b, par, first, last):
                    for h in range(first, last):
                        cols = slice(h * L, (h + 1) * L)
                        mm = mm3(nc, ybank[par][0:L, :], oh[par][:, cols], ol[par][:, cols], woh[:, h, :], wol[:, h, :], h == 0, h == NH - 1)
                    if last == NH:
                        mm.then_inc(proj, 1)

                def x2t(b, par):
                    pe.wait_ge(ln_x, b + 1)
                    if not is_first(b):
                        pe.wait_ge(tl, b)
                    for kt in range(KT):
                        mm = nc.tensor.transpose(tbank[:, kt * L:(kt + 1) * L], xn[par][:, kt * 128:(kt + 1) * 128], c["ident"][0:L, 0:L])
                    mm.then_inc(t_done, 1)

                keep_busy(nc, c, banks[7], 14)
                for n in range(NW):
                    pe.wait_ge(wlo, n + 1)
                    for b in range(2):
                        pe.wait_ge(flo, n * 2 + b + 1)
                        heads(b, b, n * HW, (n + 1) * HW)

                def step(n, par, k):
                    if has(n, 0):
                        pe.wait_ge(olo, n - 1)
                        pe.wait_ge(x1_set, n - 1)
                        heads(n, par, 0, NH)
                    if not has(n, 1):
                        keep_busy(nc, c, banks[7], 10)
                    x2t(n - 2, par)

                over_steps(pe, step)
                keep_busy(nc, c, banks[7], 5)


def shared_pair(nc, io, scratch, banks, c, x1, x2h, x2l, spare, up, down, routed):
    with ExitStack() as ctx:
        def sb(name, shape, dt=F32):
            return ctx.enter_context(nc.sbuf_tensor(name, shape, dt))

        def sem(name):
            return ctx.enter_context(nc.semaphore(name))

        waited = sem("waited")

        assert NJ % RING == 0
        praw, up_in, draw, down_in = up["raw"], up["in"], down["raw"], down["in"]
        uph = [sb(f"up_hi{i}", [128, KT, 256], F32R) for i in range(2)]
        upl = [sb(f"up_lo{i}", [128, KT, 256], F32R) for i in range(2)]
        dh, dl = sb("down_hi", [128, NJ, DM], F32R), sb("down_lo", [128, NJ, DM], F32R)
        uh, ul = sb("u_hi", [128, NJ, NT], F32R), sb("u_lo", [128, NJ, NT], F32R)
        sil = [spare[:, i, 0:HALF] for i in range(2)]
        uf = [spare[:, 2 + i, 0:HALF] for i in range(2)]
        gwraw = sb("gate_raw", [128, KT, E])
        gwh, gwl = sb("gate_hi", [128, KT, 128], F32R), sb("gate_lo", [128, KT, 128], F32R)
        bias = sb("router_bias", [L, B, E])
        lt = sb("logits_t", [E, NT])
        sc, se, eq, pk = (sb(n, [L, B, E]) for n in ("scores", "select", "equal", "picked"))
        one1, rev, two1 = sb("first_pick", [L, B, E]), sb("reverse_index", [L, B, E]), sb("second_pick", [L, B, E])
        both = sb("chosen", [L, B, E])
        rd, ws = sb("reduced", [L, B]), sb("weight_sum", [L, B])
        gf, sl = sb("gates_f32", [L, B, E]), sb("slot_f32", [L, B, E])
        token, before, ones = sb("token", [L, B]), sb("before", [L, L]), sb("ones", [L, 128])
        cum, num, nblk = sb("pairs_before", [128, B, E]), sb("pairs", [128, E]), sb("blocks", [128, E])
        ends, base = sb("block_ends", [128, E]), sb("first_slot", [128, E])
        blk, row, ex = sb("block_index", [128, NBLK]), sb("row_index", [128, 1]), sb("block_expert", [128, NBLK])
        pay, pos = sb("payload", [L, TOPK, B, 2]), sb("positions", [L, TOPK, B])
        zeros = sb("empty_slots", [128, NTILE * 2])
        NSMALL = 6 + B

        sm_in = sem("small_in")
        uphi, uplo, dhi, dlo = sem("up_his"), sem("up_los"), sem("down_his"), sem("down_los")
        zeroed, gwhi, gwlo = sem("zeroed"), sem("gate_w_hi"), sem("gate_w_lo")
        lgt, ltc, ltr, chain = sem("logits"), sem("logits_copied"), sem("logits_back"), sem("router_step")
        sigm, picked, counted, placed = sem("sigmoid"), sem("experts_picked"), sem("pairs_counted"), sem("slots_placed")
        emptied, scattered, table_in = sem("table_emptied"), sem("table_scattered"), sem("table_in")
        wset, xset = sem("weight_index_set"), sem("token_index_set")
        h_done, sil_s, u_set = sem("h_done"), sem("silu_s"), sem("u_set")
        uhi, ulo, d_done, y_set = sem("u_his"), sem("u_los"), sem("down_done"), sem("y_set")
        h1b, h3b, yb, lb, xb = banks[0:2], banks[2:4], banks[5:7], (banks[7], banks[4]), banks[7]

        def raw(j):
            return praw[j % RING][:, 0:TB if j < NFT else TW].rearrange("p (k n) -> p k n", k=KT)

        def rows(j):
            return 128 if j < NFT else TAIL

        with nc.Block() as block:
            @block.sync
            def _(sp):
                sp.dma_start(gwraw[:], io["gate_wt"]).then_inc(sm_in, 16)
                for tile, name in ((rev, "c_rev"), (token, "c_token"), (before, "c_before"), (blk, "c_block"), (row, "c_row")):
                    sp.dma_start(tile[:], io[name]).then_inc(sm_in, 16)
                for b in range(B):
                    sp.dma_start(bias[:, b, :], io["router_bias"].partition_broadcast(L)).then_inc(sm_in, 16)
                sp.wait_ge(zeroed, 3)
                sp.dma_start(scratch["slots"].rearrange("(p t) c -> p (t c)", p=128), zeros[:]).then_inc(emptied, 16)
                for j in range(RING, NJ):
                    sp.wait_ge(uplo, j + 1 - RING)
                    load_up(sp, io, up, j)
                sp.wait_ge(scattered, 16 * TOPK * B)
                sp.dma_start(routed["table"][:], scratch["slots"].rearrange("(t p) c -> p t c", p=128)).then_inc(table_in, 16)

            @block.gpsimd
            def _(pool):
                nc.gpsimd.memset(f32(gwh[:]), 0.0).then_inc(zeroed, 1)
                nc.gpsimd.memset(f32(gwl[:]), 0.0).then_inc(zeroed, 1)
                nc.gpsimd.memset(zeros[:], 0.0).then_inc(zeroed, 1)
                nc.gpsimd.memset(cum[:, 0, :], 0.0).then_inc(zeroed, 1)
                nc.gpsimd.memset(ones[:], 1.0).then_inc(zeroed, 1)
                pool.wait_ge(zeroed, 5)
                pool.wait_ge(sm_in, NSMALL * 16)
                pool.sem_inc(waited, 1)
                nc.gpsimd.tensor_scalar(gwh[:, :, 0:E], gwraw[:], 1.0, 1.0, ALU.mult, ALU.mult).then_inc(gwhi, 1)
                pool.wait_ge(gwhi, 1)
                nc.gpsimd.tensor_tensor(gwl[:, :, 0:E], gwraw[:], f32(gwh[:, :, 0:E]), ALU.subtract).then_inc(gwlo, 1)
                pool.wait_ge(down_in, 32)
                for part in (slice(0, NFT), slice(NFT, NJ)):
                    r = 128 if part.start == 0 else TAIL
                    nc.gpsimd.tensor_scalar(dh[0:r, part, :], draw[0:r, part, :], 1.0, 1.0, ALU.mult, ALU.mult).then_inc(dhi, 1)
                pool.wait_ge(dhi, 2)
                for part in (slice(0, NFT), slice(NFT, NJ)):
                    r = 128 if part.start == 0 else TAIL
                    op = nc.gpsimd.tensor_tensor(dl[0:r, part, :], draw[0:r, part, :], f32(dh[0:r, part, :]), ALU.subtract)
                op.then_inc(dlo, 1)
                EARLY = 0

                def scatter(first, last):
                    for n in range(first, last):
                        i, b = n // B, n % B
                        nc.gpsimd.indirect_dma_start(scratch["slots"], bass.IndirectOffsetOnAxis(ap=routed["slot"][:, i, b:b + 1], axis=0),
                                                     pay[:, i, b, :], None).then_inc(scattered, 16)

                for j in range(NJ):
                    if j == NJ - 2:
                        pool.wait_ge(wset, 1)
                        nc.gpsimd.indirect_dma_start(routed["w0"][:], None, io["wex"],
                                                     bass.IndirectOffsetOnAxis(ap=routed["widx"][0][:], axis=0)).then_inc(routed["w_in"][0], 16)
                    if j == NJ - 1:
                        pool.wait_ge(placed, 1)
                        pool.wait_ge(emptied, 16)
                        scatter(0, EARLY)
                    for s in range(2):
                        n = j * 2 + s
                        r = rows(j)
                        cols = slice(s * HALF, (s + 1) * HALF)
                        pool.wait_ge(u_set, n + 1)
                        nc.gpsimd.tensor_scalar(uh[0:r, j, cols], uf[s][0:r, :], 1.0, 1.0, ALU.mult, ALU.mult).then_inc(uhi, 1)
                        pool.wait_ge(uhi, n + 1)
                        nc.gpsimd.tensor_tensor(ul[0:r, j, cols], uf[s][0:r, :], f32(uh[0:r, j, cols]), ALU.subtract).then_inc(ulo, 1)
                scatter(EARLY, TOPK * B)
                for i in range(2):
                    pool.wait_ge(routed["x2_out"][i], 16 * B // 2)
                for i in range(2):
                    pool.wait_ge(xset, i + 1)
                    nc.gpsimd.indirect_dma_start(routed["xg"][i][:], None, scratch["x2"],
                                                 bass.IndirectOffsetOnAxis(ap=routed["xidx"][i][:], axis=0)).then_inc(routed["x_in"][i], 16)

            @block.scalar
            def _(act):
                def split(j):
                    w = 256 if j < NFT else 2 * TAIL
                    act.wait_ge(up_in[j % RING], (j // RING + 1) * 16)
                    if j >= 2:
                        act.wait_ge(h_done, (j - 1) * 2)
                    nc.scalar.activation(uph[j % 2][:, :, 0:w], raw(j), ACT.Copy).then_inc(uphi, 1)

                split(0)
                for j in range(NJ):
                    if j + 1 < NJ:
                        split(j + 1)
                    if j == 1:
                        act.wait_ge(lgt, 2)
                        for s in range(2):
                            nc.scalar.activation(lt[:, s * HALF:(s + 1) * HALF], lb[s][0:E, 0:HALF], ACT.Copy).then_inc(ltc, 1)
                    if j == 2:
                        act.wait_ge(ltr, 1)
                        nc.scalar.activation(sc[:], xb[0:L, 0:B * E].rearrange("l (b e) -> l b e", b=B), ACT.Sigmoid).then_inc(sigm, 1)
                    for s in range(2):
                        n = j * 2 + s
                        act.wait_ge(h_done, n + 1)
                        if j:
                            act.wait_ge(u_set, n - 1)
                        if j < NFT:
                            nc.scalar.activation(sil[s], h1b[s][:, 0:HALF], ACT.Silu).then_inc(sil_s, 1)
                        else:
                            nc.scalar.activation(sil[s][128 - TAIL:, :], h1b[s][0:TAIL, 0:HALF], ACT.Silu).then_inc(sil_s, 1)

            @block.vector
            def _(dve):
                V = nc.vector
                count = [0]

                def then(op):
                    op.then_inc(chain, 1)
                    count[0] += 1
                    dve.wait_ge(chain, count[0])

                def over_e(r):
                    return r[:].unsqueeze(2).broadcast_to([L, B, E])

                def split(j):
                    w = 256 if j < NFT else 2 * TAIL
                    dve.wait_ge(uphi, j + 1)
                    V.tensor_tensor(upl[j % 2][:, :, 0:w], raw(j), f32(uph[j % 2][:, :, 0:w]), ALU.subtract).then_inc(uplo, 1)

                def pick(dst):
                    then(V.tensor_reduce(rd[:], se[:], AX.X, ALU.max))
                    then(V.tensor_tensor(eq[:], se[:], over_e(rd), ALU.is_equal))
                    then(V.tensor_tensor(pk[:], eq[:], rev[:], ALU.mult))
                    then(V.tensor_reduce(rd[:], pk[:], AX.X, ALU.max))
                    then(V.tensor_tensor(dst[:], pk[:], over_e(rd), ALU.is_equal))

                def pick_first():
                    dve.wait_ge(sigm, 1)
                    dve.wait_ge(sm_in, NSMALL * 16)
                    then(V.tensor_tensor(se[:], sc[:], bias[:], ALU.add))
                    pick(one1)
                    then(V.scalar_tensor_tensor(out=se[:], in0=one1[:], scalar=-1e30, in1=se[:], op0=ALU.mult, op1=ALU.add))

                def pick_second():
                    pick(two1)
                    then(V.tensor_tensor(both[:], two1[:], one1[:], ALU.add))
                    dve.sem_inc(picked, 1)

                def gates():
                    then(V.tensor_tensor(gf[:], both[:], sc[:], ALU.mult))
                    then(V.tensor_reduce(ws[:], gf[:], AX.X, ALU.add))
                    then(V.tensor_scalar(ws[:], ws[:], 1e-12, None, ALU.max))
                    then(V.reciprocal(ws[:], ws[:]))
                    then(V.tensor_tensor(gf[:], gf[:], over_e(ws), ALU.mult))

                def count_pairs():
                    total = xb[:, B * E:2 * B * E].rearrange("p (b e) -> p b e", b=B)
                    dve.wait_ge(counted, 1)
                    dve.wait_ge(zeroed, 5)
                    for b in range(B):
                        then(V.tensor_tensor(cum[:, b + 1, :] if b + 1 < B else num[:], cum[:, b, :], total[:, b, :], ALU.add))
                    then(V.tensor_scalar(nblk[:], num[:], 0.0, None, ALU.is_gt))
                    for full in range(SLOTS, NT, SLOTS):
                        then(V.scalar_tensor_tensor(out=nblk[:], in0=num[:], scalar=float(full), in1=nblk[:], op0=ALU.is_gt, op1=ALU.add))

                def place_experts():
                    then(V.tensor_copy(ends[:], nblk[:]))
                    for e in range(1, E):
                        then(V.tensor_tensor(ends[:, e:e + 1], ends[:, e - 1:e], nblk[:, e:e + 1], ALU.add))
                    then(V.tensor_tensor(base[:], ends[:], nblk[:], ALU.subtract))
                    then(V.tensor_scalar(base[:], base[:], float(SLOTS), None, ALU.mult))
                    then(V.tensor_scalar(ex[:], blk[:], ends[:, 0:1], None, ALU.is_ge))
                    for e in range(1, E - 1):
                        then(V.scalar_tensor_tensor(out=ex[:], in0=blk[:], scalar=ends[:, e:e + 1], in1=ex[:], op0=ALU.is_ge, op1=ALU.add))
                    then(V.tensor_scalar(routed["wrow"][:], ex[:], 128.0, row[:, 0:1], ALU.mult, ALU.add))
                    V.tensor_copy(routed["widx"][0][:], routed["wrow"][:, 0:1]).then_inc(wset, 1)

                def place_pairs():
                    then(V.tensor_tensor(cum[0:L], cum[0:L], base[0:L, :].unsqueeze(1).broadcast_to([L, B, E]), ALU.add))
                    then(V.tensor_tensor(sl[:], cum[0:L], xb[0:L, 0:B * E].rearrange("l (b e) -> l b e", b=B), ALU.add))
                    for i, one in enumerate((one1, two1)):
                        then(V.tensor_tensor(pk[:], one[:], sl[:], ALU.mult))
                        then(V.tensor_reduce(pos[:, i, :], pk[:], AX.X, ALU.add))
                        then(V.tensor_tensor(eq[:], one[:], gf[:], ALU.mult))
                        then(V.tensor_reduce(pay[:, i, :, 1], eq[:], AX.X, ALU.add))
                        then(V.tensor_copy(pay[:, i, :, 0], token[:]))
                    then(V.tensor_copy(routed["slot"][:], pos[:]))
                    dve.sem_inc(placed, 1)

                split(0)
                for j in range(NJ):
                    if j + 1 < NJ:
                        split(j + 1)
                    if j == 2:
                        pick_first()
                        pick_second()
                    if j == 3:
                        gates()
                        count_pairs()
                        place_experts()
                    if j == 4:
                        place_pairs()
                    for s in range(2):
                        n = j * 2 + s
                        a = 0 if j < NFT else 128 - TAIL
                        src = (h3b[s] if j < NFT else h1b[s])[a:, 0:HALF]
                        dve.wait_ge(sil_s, n + 1)
                        if j:
                            dve.wait_ge(ulo, n - 1)
                        V.tensor_tensor(uf[s][0:rows(j), :], src, sil[s][a:, :], ALU.mult).then_inc(u_set, 1)
                for b in range(B):
                    dve.wait_ge(d_done, b + 1)
                    V.scalar_tensor_tensor(out=x1[:, b, :], in0=yb[b % 2][0:L, :], scalar=c["tanhg"][0:L, 1:2],
                                           in1=x1[:, b, :], op0=ALU.mult, op1=ALU.add).then_inc(y_set, 1)
                    if b == B - 3:
                        dve.wait_ge(table_in, 16)
                        for i in range(2):
                            V.tensor_copy(routed["xidx"][i][:], routed["table"][:, i, 0:1]).then_inc(xset, 1)

            @block.tensor
            def _(pe):
                def logits():
                    pe.wait_ge(gwlo, 1)
                    for s in range(2):
                        cols = slice(s * HALF, (s + 1) * HALF)
                        for kt in range(KT):
                            mm = mm3(nc, lb[s][:, 0:HALF], gwh[:, kt, :], gwl[:, kt, :], x2h[:, kt, cols], x2l[:, kt, cols],
                                     kt == 0, kt == KT - 1)
                        mm.then_inc(lgt, 1)

                def turn_logits():
                    pe.wait_ge(ltc, 2)
                    for b in range(B):
                        mm = nc.tensor.transpose(xb[0:L, b * E:(b + 1) * E], lt[:, b * L:(b + 1) * L], c["ident"][0:E, 0:E])
                    mm.then_inc(ltr, 1)

                def count_pairs():
                    pe.wait_ge(picked, 1)
                    pe.wait_ge(zeroed, 5)
                    chosen = both[:].rearrange("l b e -> l (b e)")
                    nc.tensor.matmul(xb[0:L, 0:B * E], before[:], chosen, start=True, stop=True)
                    nc.tensor.matmul(xb[:, B * E:2 * B * E], ones[:], chosen, start=True, stop=True).then_inc(counted, 1)

                keep_busy(nc, c, yb[0], 5)
                for j in range(NJ):
                    pe.wait_ge(uplo, j + 1)
                    wh, wl = uph[j % 2], upl[j % 2]
                    for s in range(2):
                        n = j * 2 + s
                        cols = slice(s * HALF, (s + 1) * HALF)
                        if j:
                            pe.wait_ge(u_set, n - 1)
                        for i, bank in enumerate((h1b[s], h3b[s]) if j < NFT else (h1b[s],)):
                            ws = slice(i * 128, (i + 1) * 128)
                            for kt in range(KT):
                                mm = mm3(nc, bank[:, 0:HALF], wh[:, kt, ws], wl[:, kt, ws],
                                         x2h[:, kt, cols], x2l[:, kt, cols], kt == 0, kt == KT - 1)
                        mm.then_inc(h_done, 1)
                    if j == 0:
                        logits()
                    if j == 1:
                        turn_logits()
                    if j == 2:
                        count_pairs()
                pe.wait_ge(dlo, 1)
                for b in range(B):
                    half, first = b // (B // 2), b % (B // 2) == 0
                    if first:
                        pe.wait_ge(ulo, 2 * NJ - 2 + half)
                    if b >= 2:
                        pe.wait_ge(y_set, b - 1)
                    for j in range(NJ):
                        if first and j == NJ - 1:
                            pe.wait_ge(ulo, 2 * NJ - 1 + half)
                        r, cols = rows(j), slice(b * L, (b + 1) * L)
                        mm = mm3(nc, yb[b % 2][0:L, :], uh[0:r, j, cols], ul[0:r, j, cols], dh[0:r, j, :], dl[0:r, j, :],
                                 j == 0, j == NJ - 1)
                    mm.then_inc(d_done, 1)


def over_blocks(eng, body):
    body(0, 0, 0)
    with eng.Fori(0, (NBLK - 4) // 2) as i:
        body(i * 2 + 1, 1, i)
        body(i * 2 + 2, 0, i + 1)
    for i in range(NBLK - 3, NBLK):
        body(i, i % 2, i // 2)


def experts(nc, io, scratch, out, banks, c, x1, routed):
    with ExitStack() as ctx:
        def sb(name, shape, dt=F32):
            return ctx.enter_context(nc.sbuf_tensor(name, shape, dt))

        def sem(name):
            return ctx.enter_context(nc.semaphore(name))

        waited = sem("waited")

        assert NBLK % 2 == 0 and TILES == 2
        CUTS = [kt * EW1 for kt in range(KT + 1)] + [KT * EW1 + DM * EJ // 2, EW]
        NP = len(CUTS) - 1
        raw = [routed["w0"], sb("expert_raw1", [128, EW])]
        wh = [sb(f"expert_hi{i}", [128, EW], F32R) for i in range(2)]
        wl = [sb(f"expert_lo{i}", [128, EW], F32R) for i in range(2)]
        xg, table = routed["xg"], routed["table"]
        xh, xl = ([sb(f"xg_t_{m}{i}", [128, KT * 128], F32R) for i in range(2)] for m in ("hi", "lo"))
        sil, u = sb("silu", [128, INTER]), sb("hidden", [128, EJ * 128])
        uh, ul = sb("hidden_t_hi", [128, EJ * 128], F32R), sb("hidden_t_lo", [128, EJ * 128], F32R)
        ys = [sb(f"y_rows{i}", [128, DM]) for i in range(2)]
        NY = 3
        yg = [[sb(f"y_back{i}_{n}", [L, DM]) for n in range(NY)] for i in range(TOPK)]
        ysum = [sb(f"y_sum{i}", [L, DM]) for i in range(2)]
        ob = [sb(f"out{i}", [L, DM]) for i in range(2)]

        w_in, x_in = routed["w_in"], routed["x_in"]
        widx_set, xidx_set, whi, wlo = sem("weight_idx"), sem("token_idx"), sem("expert_his"), sem("expert_los")
        xt, xhi, xlo = sem("x_turned"), sem("xg_his"), sem("xg_los")
        h1_done, h3_done, silu_s, padded, u_set = sem("h1_done"), sem("h3_done"), sem("silued"), sem("padded"), sem("hidden_set")
        ut, uhi, ulo, y_done, y_read = sem("hidden_turned"), sem("hidden_his"), sem("hidden_los"), sem("y_done"), sem("y_read")
        y_out = [sem(f"y_stored{i}") for i in range(2)]
        back, summed, oset, oout = ([sem(f"y_back_in{n}") for n in range(NY)], sem("y_summed"), sem("out_set"),
                                    [sem(f"out_stored{i}") for i in range(2)])
        h1b, h3b, yb, xtb, utb = banks[0:2], banks[2:4], banks[4:6], banks[6], banks[7]

        def gather(dst, src, index):
            return nc.gpsimd.indirect_dma_start(dst, None, src, bass.IndirectOffsetOnAxis(ap=index, axis=0))

        with nc.Block() as block:
            @block.sync
            def _(sp):
                def store(i, par, k):
                    for s in range(TILES):
                        t = i * TILES + s
                        sp.wait_ge(y_read, t + 1)
                        sp.dma_start(scratch["y"][at(t, 128), :], ys[s][:]).then_inc(y_out[s], 16)

                over_blocks(sp, store)
                for b in range(B):
                    sp.wait_ge(oset, b + 1)
                    sp.dma_start(out[b], ob[b % 2][:]).then_inc(oout[b % 2], 16)
                for i in range(2):
                    sp.wait_ge(oout[i], 16 * B // 2)

            @block.gpsimd
            def _(pool):
                def weights(i, par):
                    pool.wait_ge(widx_set, i)
                    if not (isinstance(i, int) and i < 2):
                        pool.wait_ge(wlo, NP * (i - 1))
                    pool.sem_inc(waited, 1)
                    gather(raw[par][:], io["wex"], routed["widx"][par][:]).then_inc(w_in[par], 16)

                def body(i, par, k):
                    if isinstance(i, int) and i == NBLK - 1:
                        return
                    for s in range(TILES):
                        if s == 1 and not (isinstance(i, int) and i >= NBLK - 2):
                            weights(i + 2, par)
                        t = (i + 1) * TILES + s
                        pool.wait_ge(xidx_set, t - 1)
                        pool.wait_ge(xt, t - 1)
                        pool.sem_inc(waited, 1)
                        gather(xg[s][:], scratch["x2"], routed["xidx"][s][:]).then_inc(x_in[s], 16)

                nc.gpsimd.memset(u[:, INTER:], 0.0).then_inc(padded, 1)
                weights(1, 1)
                over_blocks(pool, body)
                for i in range(2):
                    pool.wait_ge(y_out[i], 16 * NBLK)
                for b in range(B):
                    if b >= NY:
                        pool.wait_ge(summed, b - NY + 1)
                    for i in range(TOPK):
                        gather(yg[i][b % NY][:], scratch["y"], routed["slot"][:, i, b:b + 1]).then_inc(back[b % NY], 16)

            @block.scalar
            def _(act):
                def split(i, par, k, pieces):
                    for p in pieces:
                        if p == 0:
                            act.wait_ge(w_in[par], k * 16 + 16)
                        if not (isinstance(i, int) and i < 2):
                            if p < KT:
                                act.wait_ge(h3_done, TILES * (i - 1))
                            else:
                                act.wait_ge(y_done, TILES * (i - 1))
                        cols = slice(CUTS[p], CUTS[p + 1])
                        nc.scalar.activation(wh[par][:, cols], raw[par][:, cols], ACT.Copy).then_inc(whi, 1)

                def x_hi(t, s):
                    act.wait_ge(xt, t + 1)
                    if not (isinstance(t, int) and t < 2):
                        act.wait_ge(h3_done, t - 1)
                    nc.scalar.activation(xh[s][:], xtb[:], ACT.Copy).then_inc(xhi, 1)

                def u_hi(t):
                    act.wait_ge(ut, t + 1)
                    if not (isinstance(t, int) and t == 0):
                        act.wait_ge(y_done, t)
                    nc.scalar.activation(uh[:], utb[:, 0:EJ * 128], ACT.Copy).then_inc(uhi, 1)

                def y_copy(t, s, k):
                    act.wait_ge(y_done, t + 1)
                    if not (isinstance(t, int) and t < 2):
                        act.wait_ge(y_out[s], k * 16)
                    nc.scalar.activation(ys[s][:], yb[s][:], ACT.Copy).then_inc(y_read, 1)

                def body(i, par, k):
                    start, last = isinstance(i, int) and i == 0, isinstance(i, int) and i == NBLK - 1
                    for s in range(TILES):
                        t = i * TILES + s
                        mine = [] if last else range(NP) if start and s else [] if start else range(s * NP // 2, (s + 1) * NP // 2)
                        act.wait_ge(h1_done, t + 1)
                        if not (start and s == 0):
                            act.wait_ge(u_set, t)
                        nc.scalar.activation(sil[:], h1b[s][:, 0:INTER], ACT.Silu).then_inc(silu_s, 1)
                        if not (start and s == 0):
                            u_hi(t - 1)
                        split(i + 1, 1 - par, k + par, mine[:1])
                        if not (last and s):
                            x_hi(t + 1, 1 - s)
                        split(i + 1, 1 - par, k + par, mine[1:])
                        if not (start and s == 0):
                            y_copy(t - 1, 1 - s, i - 1 + s)

                x_hi(0, 0)
                split(0, 0, 0, range(NP))
                over_blocks(act, body)
                u_hi(NTILE - 1)
                y_copy(NTILE - 1, 1, NBLK - 1)

            @block.vector
            def _(dve):
                V = nc.vector

                def split(i, par, pieces):
                    for p in pieces:
                        dve.wait_ge(whi, i * NP + p + 1)
                        cols = slice(CUTS[p], CUTS[p + 1])
                        V.tensor_tensor(wl[par][:, cols], raw[par][:, cols], f32(wh[par][:, cols]), ALU.subtract).then_inc(wlo, 1)

                def x_lo(t, s):
                    dve.wait_ge(xhi, t + 1)
                    V.tensor_tensor(xl[s][:], xtb[:], f32(xh[s][:]), ALU.subtract).then_inc(xlo, 1)

                def u_lo(t):
                    dve.wait_ge(uhi, t + 1)
                    V.tensor_tensor(ul[:], utb[:, 0:EJ * 128], f32(uh[:]), ALU.subtract).then_inc(ulo, 1)

                def body(i, par, k):
                    start, last = isinstance(i, int) and i == 0, isinstance(i, int) and i == NBLK - 1
                    for s in range(TILES):
                        t = i * TILES + s
                        mine = [] if last else range(NP) if start and s else [] if start else range(s * NP // 2, (s + 1) * NP // 2)
                        if not last:
                            dve.wait_ge(x_in[s], i * 16 + 16)
                            V.tensor_copy(routed["xidx"][s][:], table[:, bass.ds(t + 2, 1), 0]).then_inc(xidx_set, 1)
                        if s == 0 and not (isinstance(i, int) and i >= NBLK - 2):
                            dve.wait_ge(w_in[par], k * 16 + 16)
                            V.tensor_copy(routed["widx"][par][:], routed["wrow"][:, bass.ds(i + 2, 1)]).then_inc(widx_set, 1)
                        if not (start and s == 0):
                            u_lo(t - 1)
                        split(i + 1, 1 - par, mine[:1])
                        dve.wait_ge(silu_s, t + 1)
                        dve.wait_ge(h3_done, t + 1)
                        if not (start and s == 0):
                            dve.wait_ge(ut, t)
                        V.scalar_tensor_tensor(out=u[:, 0:INTER], in0=h3b[s][:, 0:INTER], scalar=table[:, bass.ds(t, 1), 1],
                                               in1=sil[:], op0=ALU.mult, op1=ALU.mult).then_inc(u_set, 1)
                        if not (last and s):
                            x_lo(t + 1, 1 - s)
                        split(i + 1, 1 - par, mine[1:])

                V.tensor_copy(routed["widx"][1][:], routed["wrow"][:, 1:2]).then_inc(widx_set, 1)
                x_lo(0, 0)
                split(0, 0, range(NP))
                over_blocks(dve, body)
                u_lo(NTILE - 1)
                for b in range(B):
                    dve.wait_ge(back[b % NY], 16 * TOPK * (b // NY + 1))
                    if b >= 2:
                        dve.wait_ge(oset, b - 1)
                    V.tensor_tensor(ysum[b % 2][:], yg[0][b % NY][:], yg[1][b % NY][:], ALU.add).then_inc(summed, 1)
                    dve.wait_ge(summed, b + 1)
                    if b >= 2:
                        dve.wait_ge(oout[b % 2], 16 * (b // 2))
                    V.scalar_tensor_tensor(out=ob[b % 2][:], in0=ysum[b % 2][:], scalar=c["tanhg"][0:L, 1:2],
                                           in1=x1[:, b, :], op0=ALU.mult, op1=ALU.add).then_inc(oset, 1)

            @block.tensor
            def _(pe):
                def x_turn(t, s, k):
                    pe.wait_ge(x_in[s], k * 16 + 16)
                    if not (isinstance(t, int) and t == 0):
                        pe.wait_ge(xlo, t)
                    for kt in range(KT):
                        cols = slice(kt * 128, (kt + 1) * 128)
                        mm = nc.tensor.transpose(xtb[:, cols], xg[s][:, cols], c["ident"][:])
                    mm.then_inc(xt, 1)

                def hidden(bank, i, par, s, part):
                    for kt in range(KT):
                        if s == 0 and part == 0:
                            pe.wait_ge(wlo, i * NP + kt + 1)
                        x = slice(kt * 128, (kt + 1) * 128)
                        w = slice(kt * EW1 + part * INTER, kt * EW1 + (part + 1) * INTER)
                        mm = mm3(nc, bank[:, 0:INTER], xh[s][:, x], xl[s][:, x], wh[par][:, w], wl[par][:, w], kt == 0, kt == KT - 1)
                    return mm

                def u_turn(t):
                    pe.wait_ge(u_set, t + 1)
                    if not (isinstance(t, int) and t == 0):
                        pe.wait_ge(ulo, t)
                    for j in range(EJ):
                        cols = slice(j * 128, (j + 1) * 128)
                        mm = nc.tensor.transpose(utb[:, cols], u[:, cols], c["ident"][:])
                    mm.then_inc(ut, 1)

                def outputs(t, i, par, s):
                    pe.wait_ge(ulo, t + 1)
                    if s == 0:
                        pe.wait_ge(wlo, (i + 1) * NP)
                    if not (isinstance(t, int) and t < 2):
                        pe.wait_ge(y_read, t - 1)
                    for j in range(EJ):
                        x = slice(j * 128, (j + 1) * 128)
                        w = slice(KT * EW1 + j * DM, KT * EW1 + (j + 1) * DM)
                        mm = mm3(nc, yb[s][:], uh[:, x], ul[:, x], wh[par][:, w], wl[par][:, w], j == 0, j == EJ - 1)
                    mm.then_inc(y_done, 1)

                def body(i, par, k):
                    start, last = isinstance(i, int) and i == 0, isinstance(i, int) and i == NBLK - 1
                    for s in range(TILES):
                        t = i * TILES + s
                        pe.wait_ge(xlo, t + 1)
                        if not start:
                            pe.wait_ge(silu_s, t - 1)
                            pe.wait_ge(u_set, t - 1)
                        hidden(h1b[s], i, par, s, 0).then_inc(h1_done, 1)
                        if not (start and s == 0):
                            u_turn(t - 1)
                        hidden(h3b[s], i, par, s, 1).then_inc(h3_done, 1)
                        if not (last and s):
                            x_turn(t + 1, 1 - s, i + s)
                        if s:
                            outputs(t - 1, i, par, 0)
                        elif not start:
                            outputs(t - 1, i - 1, 1 - par, 1)

                pe.wait_ge(padded, 1)
                x_turn(0, 0, 0)
                keep_busy(nc, c, utb, 12)
                over_blocks(pe, body)
                u_turn(NTILE - 1)
                outputs(NTILE - 1, NBLK - 1, 1, 1)


def kernel(**inputs):
    import numpy as _np
    import concourse.bacc as _bacc
    from concourse import mybir as _mybir
    from concourse.bass_utils import run_bass_kernel_spmd as _run

    a = {n: _np.asarray(v) for n, v in inputs.items()}
    p = "L0_xattn_"
    f = "L0_ffn_"

    def rows_first(w):
        return w.reshape(w.shape[0] // 128, 128, w.shape[1]).transpose(1, 0, 2)

    w1 = a[f + "sw1"].T.reshape(KT, 128, GH).transpose(1, 0, 2)
    w3 = a[f + "sw3"].T.reshape(KT, 128, GH).transpose(1, 0, 2)
    tiles = []
    for j in range(NJ):
        cols = slice(j * 128, min((j + 1) * 128, GH))
        tiles.append(_np.concatenate([w1[..., cols], w3[..., cols]], -1).reshape(128, -1))
    w2 = a[f + "sw2"].T
    up = _np.concatenate([a[f + "W1"], a[f + "W3"]], -1).reshape(E, KT, 128, EW1).transpose(0, 2, 1, 3).reshape(E * 128, -1)
    down = _np.zeros((E, EJ * 128, DM), a[f + "W2"].dtype)
    down[:, :INTER] = a[f + "W2"]
    down = down.reshape(E, EJ, 128, DM).transpose(0, 2, 1, 3).reshape(E * 128, -1)
    arrays = {
        "x": a["x"],
        "ctxt": a["ctx_2048"].transpose(0, 2, 1).reshape(B, KT, 128, T).transpose(0, 2, 1, 3),
        "g_xattn": a["g_xattn"], "g_ffn": a["g_ffn"],
        "wqkv": rows_first(_np.concatenate([a[p + n] for n in ("wk", "wq", "wv", "wk_ctx", "wv_ctx")], 1))
                .reshape(128, KT, NQ + 4, 512).transpose(2, 0, 1, 3),
        "wo": rows_first(a[p + "wo"]),
        "qn": a[p + "q_norm_w"], "kn": a[p + "k_norm_w"],
        "gate_wt": rows_first(a[f + "gate_w"].T),
        "router_bias": a[f + "router_bias"],
        "sw13": _np.concatenate(tiles, -1),
        "sw2": w2[:NFT * 128].reshape(NFT, 128, DM).transpose(1, 0, 2),
        "sw2t": w2[NFT * 128:],
        "wex": _np.concatenate([up, down], -1),
        **constants(),
    }
    nc = _bacc.Bacc("TRN2", target_bir_lowering=False, num_devices=1)
    launch, io = {}, {}
    for name, v in arrays.items():
        launch[f"in_{name}"] = _np.ascontiguousarray(v)
        io[name] = nc.dram_tensor(f"in_{name}", v.shape, _mybir.dt.float32, kind="ExternalInput").ap()
    out = nc.dram_tensor("out", (B, L, DM), _mybir.dt.float32, kind="ExternalOutput").ap()
    build(nc, io, out)
    r = _run(nc, [launch], core_ids=[0])
    return r.results[0]["out"]
```
